# Optimizing a Trainium2 kernel written in Bass

```python
import numpy as np
import jax
import jax.numpy as jnp

def _softmax(x, axis=-1):
    return jax.nn.softmax(x, axis=axis)

def _gelu(x):
    return jax.nn.gelu(x, approximate=True)

def _silu(x):
    return jax.nn.silu(x)

def _sigmoid(x):
    return jax.nn.sigmoid(x)

def _layernorm(x, axis=-1, eps=1e-05):
    m = jnp.mean(x, axis=axis, keepdims=True)
    v = jnp.var(x, axis=axis, keepdims=True)
    return (x - m) / jnp.sqrt(v + eps)

def _scatter_add(tgt, idx, src, axis=0):
    return tgt.at[idx].add(src)

def _segment_sum(src, seg, n):
    return jax.ops.segment_sum(src, seg, n)
kernel_name = 'mk_adj_ffn_d2_adj_r2_3fa361'

def setup_inputs(seed: int=0):
    np.random.seed(seed)
    _w = jnp.asarray

    def _rec_inputs():
        import jax
        import jax.numpy as jnp
        _gk = jax.random.key(seed)
        x = -0.0005207 + 1.001 * jax.random.normal(jax.random.fold_in(_gk, 1), (4096, 128), jnp.float32)
        _a = jax.random.bernoulli(jax.random.fold_in(_gk, 2), 0.00195312, (4096, 4096))
        adj = _a.astype(jnp.int32)
        return (x, adj)
    x, adj = _rec_inputs()

    def _L0_gnn_setup():
        import jax, jax.numpy as jnp
        import numpy as np
        N, D, H = (4096, 128, 128)
        NEG_BIG = -1000000000.0
        LEAKY_SLOPE = 0.01
        key = jax.random.key(seed)
        ks = jax.random.split(key, 6)
        inlayer = jax.random.normal(ks[0], (N, D), jnp.float32)
        inlayer2 = jax.random.normal(ks[1], (N, D), jnp.float32)
        adj_mat = jax.random.randint(ks[2], (N, N), 0, 2, jnp.int32)
        W = jax.random.uniform(ks[3], (H, D), jnp.float32, -1.0, 1.0) * np.float32(np.sqrt(6.0 / (D + H)))
        b = jnp.zeros((H,), jnp.float32)
        w1 = jax.random.uniform(ks[4], (H,), jnp.float32, -1.0, 1.0) * np.float32(np.sqrt(6.0 / (H + 1)))
        b1 = jnp.zeros((1,), jnp.float32)
        w2 = jax.random.uniform(ks[5], (H,), jnp.float32, -1.0, 1.0) * np.float32(np.sqrt(6.0 / (H + 1)))
        b2 = jnp.zeros((1,), jnp.float32)
        return {'inlayer': inlayer, 'inlayer2': inlayer2, 'adj_mat': adj_mat, 'W': W, 'b': b, 'w1': w1, 'b1': b1, 'w2': w2, 'b2': b2}
    _L0_gnn_all = _L0_gnn_setup()
    _L0_gnn_in = {k: v for k, v in _L0_gnn_all.items() if k in ('inlayer2', 'W', 'b', 'w1', 'b1', 'w2', 'b2')}
    del _L0_gnn_all

    def _L0_ffn_setup():
        import jax, jax.numpy as jnp
        import numpy as np
        B, A = (2048, 8)
        IN, OUT = (128, 128)
        SH1, SH2 = (128, 128)
        EH1, EH2 = (128, 64)
        E, TOPK = (4, 2)

        def _shared_mlp(x, W1, b1, W2, b2, W3, b3):
            h = jax.nn.relu(x @ W1 + b1)
            h = jax.nn.relu(h @ W2 + b2)
            return h @ W3 + b3

        def _experts_mlp(x, eW1, eb1, eW2, eb2, eW3, eb3):
            h = jax.nn.relu(jnp.einsum('baf,efh->ebah', x, eW1) + eb1[:, None, None, :])
            h = jax.nn.relu(jnp.einsum('ebah,ehg->ebag', h, eW2) + eb2[:, None, None, :])
            o = jnp.einsum('ebag,ego->ebao', h, eW3) + eb3[:, None, None, :]
            return jnp.moveaxis(o, 0, -1)
        key = jax.random.key(seed)
        ks = jax.random.split(key, 16)
        s = 0.05
        return {'x': jax.random.normal(ks[0], (B, A, IN), jnp.float32), 'sW1': jax.random.normal(ks[1], (IN, SH1), jnp.float32) * s, 'sb1': jnp.zeros((SH1,), jnp.float32), 'sW2': jax.random.normal(ks[2], (SH1, SH2), jnp.float32) * s, 'sb2': jnp.zeros((SH2,), jnp.float32), 'sW3': jax.random.normal(ks[3], (SH2, OUT), jnp.float32) * s, 'sb3': jnp.zeros((OUT,), jnp.float32), 'eW1': jax.random.normal(ks[4], (E, IN, EH1), jnp.float32) * s, 'eb1': jnp.zeros((E, EH1), jnp.float32), 'eW2': jax.random.normal(ks[5], (E, EH1, EH2), jnp.float32) * s, 'eb2': jnp.zeros((E, EH2), jnp.float32), 'eW3': jax.random.normal(ks[6], (E, EH2, OUT), jnp.float32) * s, 'eb3': jnp.zeros((E, OUT), jnp.float32), 'gW': jax.random.normal(ks[7], (IN, E), jnp.float32) * s, 'gb': jnp.zeros((E,), jnp.float32)}
    _L0_ffn_all = _L0_ffn_setup()
    _L0_ffn_in = {k: v for k, v in _L0_ffn_all.items() if k in ('sW1', 'sb1', 'sW2', 'sb2', 'sW3', 'sb3', 'eW1', 'eb1', 'eW2', 'eb2', 'eW3', 'eb3', 'gW', 'gb')}
    del _L0_ffn_all

    def _L1_gnn_setup():
        import jax, jax.numpy as jnp
        import numpy as np
        SIZE_U = 2048
        SIZE_V = 2048
        N = SIZE_U + SIZE_V
        D_IN = 128
        QK_DIM = 128
        V_DIM = 128
        HEADS = 2
        DH = QK_DIM // HEADS
        DV = V_DIM // HEADS
        SCALE = DH ** (-0.5)
        NEG_INF = -9000000000000000.0
        key = jax.random.key(seed)
        ks = jax.random.split(key, 8)
        s = 1.0 / np.sqrt(D_IN)
        x = jax.random.normal(ks[0], (N, D_IN), jnp.float32)
        adj = jax.random.randint(ks[1], (N, N), 0, 2, jnp.int32)
        Wq = jax.random.normal(ks[2], (D_IN, QK_DIM), jnp.float32) * s
        Wk = jax.random.normal(ks[3], (D_IN, QK_DIM), jnp.float32) * s
        Wv = jax.random.normal(ks[4], (D_IN, V_DIM), jnp.float32) * s
        weightr = jax.random.normal(ks[5], (V_DIM, V_DIM), jnp.float32) * s
        weightd = jax.random.normal(ks[6], (V_DIM, V_DIM), jnp.float32) * s
        bias = jnp.zeros((V_DIM,), jnp.float32)
        return {'x': x, 'adj': adj, 'Wq': Wq, 'Wk': Wk, 'Wv': Wv, 'weightr': weightr, 'weightd': weightd, 'bias': bias}
    _L1_gnn_all = _L1_gnn_setup()
    _L1_gnn_in = {k: v for k, v in _L1_gnn_all.items() if k in ('Wq', 'Wk', 'Wv', 'weightr', 'weightd', 'bias')}
    del _L1_gnn_all

    def _L1_ffn_setup():
        import jax, jax.numpy as jnp
        import numpy as np
        B, S, H, NH, NE = (4, 512, 128, 4, 4)
        D = H // NH
        EPS = 1e-08

        def layernorm(x, g, b):
            m = jnp.mean(x, axis=-1, keepdims=True)
            v = jnp.mean((x - m) ** 2, axis=-1, keepdims=True)
            return (x - m) / jnp.sqrt(v + EPS) * g + b
        key = jax.random.key(seed)
        ks = jax.random.split(key, 18)
        sc = 0.05
        return {'x': jax.random.normal(ks[0], (B, S, H), jnp.float32), 'hl_w': jax.random.normal(ks[1], (NH, D, H), jnp.float32) * sc, 'hl_b': jax.random.normal(ks[2], (NH, D), jnp.float32) * sc, 'wq': jax.random.normal(ks[3], (NH, NE, D, D), jnp.float32) * sc, 'wk': jax.random.normal(ks[4], (NH, D, D), jnp.float32) * sc, 'wv': jax.random.normal(ks[5], (NH, D, D), jnp.float32) * sc, 'gate_w': jax.random.normal(ks[6], (NH, NE, NE * D), jnp.float32) * sc, 'gate_b': jax.random.normal(ks[7], (NH, NE), jnp.float32) * sc, 'ln_g': jnp.ones((D,), jnp.float32), 'ln_b': jnp.zeros((D,), jnp.float32), 'fc1_w': jax.random.normal(ks[8], (D, D), jnp.float32) * sc, 'fc1_b': jax.random.normal(ks[9], (D,), jnp.float32) * sc, 'fc2_w': jax.random.normal(ks[10], (D, D), jnp.float32) * sc, 'fc2_b': jax.random.normal(ks[11], (D,), jnp.float32) * sc, 'fnorm_g': jnp.ones((D,), jnp.float32), 'fnorm_b': jnp.zeros((D,), jnp.float32), 'fgate_w': jax.random.normal(ks[12], (NH, H), jnp.float32) * sc}
    _L1_ffn_all = _L1_ffn_setup()
    _L1_ffn_in = {k: v for k, v in _L1_ffn_all.items() if k in ('hl_w', 'hl_b', 'wq', 'wk', 'wv', 'gate_w', 'gate_b', 'ln_g', 'ln_b', 'fc1_w', 'fc1_b', 'fc2_w', 'fc2_b', 'fnorm_g', 'fnorm_b', 'fgate_w')}
    del _L1_ffn_all
    return {'x': x, 'adj': adj, 'L0_gnn_inlayer2': _L0_gnn_in['inlayer2'], 'L0_gnn_W': _L0_gnn_in['W'], 'L0_gnn_b': _L0_gnn_in['b'], 'L0_gnn_w1': _L0_gnn_in['w1'], 'L0_gnn_b1': _L0_gnn_in['b1'], 'L0_gnn_w2': _L0_gnn_in['w2'], 'L0_gnn_b2': _L0_gnn_in['b2'], 'L0_ffn_sW1': _L0_ffn_in['sW1'], 'L0_ffn_sb1': _L0_ffn_in['sb1'], 'L0_ffn_sW2': _L0_ffn_in['sW2'], 'L0_ffn_sb2': _L0_ffn_in['sb2'], 'L0_ffn_sW3': _L0_ffn_in['sW3'], 'L0_ffn_sb3': _L0_ffn_in['sb3'], 'L0_ffn_eW1': _L0_ffn_in['eW1'], 'L0_ffn_eb1': _L0_ffn_in['eb1'], 'L0_ffn_eW2': _L0_ffn_in['eW2'], 'L0_ffn_eb2': _L0_ffn_in['eb2'], 'L0_ffn_eW3': _L0_ffn_in['eW3'], 'L0_ffn_eb3': _L0_ffn_in['eb3'], 'L0_ffn_gW': _L0_ffn_in['gW'], 'L0_ffn_gb': _L0_ffn_in['gb'], 'L1_gnn_Wq': _L1_gnn_in['Wq'], 'L1_gnn_Wk': _L1_gnn_in['Wk'], 'L1_gnn_Wv': _L1_gnn_in['Wv'], 'L1_gnn_weightr': _L1_gnn_in['weightr'], 'L1_gnn_weightd': _L1_gnn_in['weightd'], 'L1_gnn_bias': _L1_gnn_in['bias'], 'L1_ffn_hl_w': _L1_ffn_in['hl_w'], 'L1_ffn_hl_b': _L1_ffn_in['hl_b'], 'L1_ffn_wq': _L1_ffn_in['wq'], 'L1_ffn_wk': _L1_ffn_in['wk'], 'L1_ffn_wv': _L1_ffn_in['wv'], 'L1_ffn_gate_w': _L1_ffn_in['gate_w'], 'L1_ffn_gate_b': _L1_ffn_in['gate_b'], 'L1_ffn_ln_g': _L1_ffn_in['ln_g'], 'L1_ffn_ln_b': _L1_ffn_in['ln_b'], 'L1_ffn_fc1_w': _L1_ffn_in['fc1_w'], 'L1_ffn_fc1_b': _L1_ffn_in['fc1_b'], 'L1_ffn_fc2_w': _L1_ffn_in['fc2_w'], 'L1_ffn_fc2_b': _L1_ffn_in['fc2_b'], 'L1_ffn_fnorm_g': _L1_ffn_in['fnorm_g'], 'L1_ffn_fnorm_b': _L1_ffn_in['fnorm_b'], 'L1_ffn_fgate_w': _L1_ffn_in['fgate_w']}

def reference(x, adj, L0_gnn_inlayer2, L0_gnn_W, L0_gnn_b, L0_gnn_w1, L0_gnn_b1, L0_gnn_w2, L0_gnn_b2, L0_ffn_sW1, L0_ffn_sb1, L0_ffn_sW2, L0_ffn_sb2, L0_ffn_sW3, L0_ffn_sb3, L0_ffn_eW1, L0_ffn_eb1, L0_ffn_eW2, L0_ffn_eb2, L0_ffn_eW3, L0_ffn_eb3, L0_ffn_gW, L0_ffn_gb, L1_gnn_Wq, L1_gnn_Wk, L1_gnn_Wv, L1_gnn_weightr, L1_gnn_weightd, L1_gnn_bias, L1_ffn_hl_w, L1_ffn_hl_b, L1_ffn_wq, L1_ffn_wk, L1_ffn_wv, L1_ffn_gate_w, L1_ffn_gate_b, L1_ffn_ln_g, L1_ffn_ln_b, L1_ffn_fc1_w, L1_ffn_fc1_b, L1_ffn_fc2_w, L1_ffn_fc2_b, L1_ffn_fnorm_g, L1_ffn_fnorm_b, L1_ffn_fgate_w):
    import jax
    import jax.numpy as jnp

    def _L0_gnn_ref(inlayer, inlayer2, adj_mat, W, b, w1, b1, w2, b2):
        import jax, jax.numpy as jnp
        import numpy as np
        N, D, H = (4096, 128, 128)
        NEG_BIG = -1000000000.0
        LEAKY_SLOPE = 0.01
        h = inlayer2 @ W.T + b
        f1 = h @ w1 + b1
        f2 = h @ w2 + b2
        logits = f1[:, None] + f2[None, :]
        bias_mat = NEG_BIG * (1.0 - (adj_mat > 0).astype(jnp.float32))
        coefs = jax.nn.softmax(jax.nn.leaky_relu(logits, LEAKY_SLOPE) + bias_mat, axis=-1)
        vals = coefs @ inlayer
        return vals

    def _L0_ffn_ref(x, sW1, sb1, sW2, sb2, sW3, sb3, eW1, eb1, eW2, eb2, eW3, eb3, gW, gb):
        import jax, jax.numpy as jnp
        import numpy as np
        B, A = (2048, 8)
        IN, OUT = (128, 128)
        SH1, SH2 = (128, 128)
        EH1, EH2 = (128, 64)
        E, TOPK = (4, 2)

        def _shared_mlp(x, W1, b1, W2, b2, W3, b3):
            h = jax.nn.relu(x @ W1 + b1)
            h = jax.nn.relu(h @ W2 + b2)
            return h @ W3 + b3

        def _experts_mlp(x, eW1, eb1, eW2, eb2, eW3, eb3):
            h = jax.nn.relu(jnp.einsum('baf,efh->ebah', x, eW1) + eb1[:, None, None, :])
            h = jax.nn.relu(jnp.einsum('ebah,ehg->ebag', h, eW2) + eb2[:, None, None, :])
            o = jnp.einsum('ebag,ego->ebao', h, eW3) + eb3[:, None, None, :]
            return jnp.moveaxis(o, 0, -1)
        all_out = _experts_mlp(x, eW1, eb1, eW2, eb2, eW3, eb3)
        shared = _shared_mlp(x, sW1, sb1, sW2, sb2, sW3, sb3)
        gates = jax.nn.softmax(x @ gW + gb, axis=-1)
        topv, topi = jax.lax.top_k(gates, TOPK)
        topw = jax.nn.softmax(topv, axis=-1)
        sel = jnp.take_along_axis(all_out, topi[:, :, None, :], axis=-1)
        gated = jnp.sum(sel * topw[:, :, None, :], axis=-1)
        return shared + gated

    def _L1_gnn_ref(x, adj, Wq, Wk, Wv, weightr, weightd, bias):
        import jax, jax.numpy as jnp
        import numpy as np
        SIZE_U = 2048
        SIZE_V = 2048
        N = SIZE_U + SIZE_V
        D_IN = 128
        QK_DIM = 128
        V_DIM = 128
        HEADS = 2
        DH = QK_DIM // HEADS
        DV = V_DIM // HEADS
        SCALE = DH ** (-0.5)
        NEG_INF = -9000000000000000.0
        q = (x @ Wq).reshape(N, HEADS, DH)
        k = (x @ Wk).reshape(N, HEADS, DH)
        v = (x @ Wv).reshape(N, HEADS, DV)
        scores = jnp.einsum('nhd,mhd->hnm', q * SCALE, k)
        scores = jnp.where(adj[None, :, :] > 0, scores, NEG_INF)
        attn = jax.nn.softmax(scores, axis=-1)
        sat = jnp.einsum('hnm,mhd->nhd', attn, v).reshape(N, V_DIM)
        out = jnp.concatenate([sat[:SIZE_U] @ weightr, sat[SIZE_U:] @ weightd], axis=0)
        out = out + bias
        return jax.nn.leaky_relu(out, negative_slope=0.01)

    def _L1_ffn_ref(x, hl_w, hl_b, wq, wk, wv, gate_w, gate_b, ln_g, ln_b, fc1_w, fc1_b, fc2_w, fc2_b, fnorm_g, fnorm_b, fgate_w):
        import jax, jax.numpy as jnp
        import numpy as np
        B, S, H, NH, NE = (4, 512, 128, 4, 4)
        D = H // NH
        EPS = 1e-08

        def layernorm(x, g, b):
            m = jnp.mean(x, axis=-1, keepdims=True)
            v = jnp.mean((x - m) ** 2, axis=-1, keepdims=True)
            return (x - m) / jnp.sqrt(v + EPS) * g + b
        b, s, h = x.shape
        nh, d, _ = wk.shape
        ne = wq.shape[1]
        sx = jnp.einsum('bsh,ndh->bnsd', x, hl_w) + hl_b[None, :, None, :]
        pad = sx == 0
        q = jnp.einsum('bnsd,neod->bneso', sx, wq)
        k = jnp.einsum('bnsd,nod->bnso', sx, wk)
        v = jnp.einsum('bnsd,nod->bnso', sx, wv)
        causal = jnp.where(jnp.tril(jnp.ones((s, s), bool)), 0.0, -jnp.inf).astype(x.dtype)
        scores = jnp.einsum('bnesd,bntd->bnest', q, k) * d ** 0.5 + causal
        att = jax.nn.softmax(scores, axis=-1)
        qkv = jnp.einsum('bnest,bntd->bnesd', att, v)
        qkv = jnp.where(pad[:, :, None], 0.0, qkv)
        out = jnp.transpose(qkv, (0, 1, 3, 2, 4)).reshape(b, nh, s, ne * d)
        gs = jax.nn.softmax(jnp.einsum('bnsf,nef->bnse', out, gate_w) + gate_b[None, :, None, :], axis=-1)
        mixed = jnp.einsum('bnsed,bnse->bnsd', out.reshape(b, nh, s, ne, d), gs)
        resid = sx[jnp.arange(nh), jnp.arange(nh)]
        hn = layernorm(mixed + resid, ln_g, ln_b)
        f_n = jnp.transpose(hn, (0, 2, 1, 3)).reshape(b, s, h)
        fx = f_n.reshape(b, s, nh, d)
        pm = fx == 0
        hx = jnp.where(pm, 0.0, fx @ fc1_w.T + fc1_b)
        hx = jax.nn.relu(hx)
        hx = jnp.where(pm, 0.0, hx @ fc2_w.T + fc2_b)
        hx = layernorm(hx + fx, fnorm_g, fnorm_b)
        fout = hx.reshape(b, s, h)
        fg = jax.nn.softmax(fout @ fgate_w.T, axis=-1)
        return (fout.reshape(b, s, nh, d) * fg[..., None]).reshape(b, s, h)
    x = x + _L0_gnn_ref(_layernorm(x, axis=-1), L0_gnn_inlayer2, adj, L0_gnn_W, L0_gnn_b, L0_gnn_w1, L0_gnn_b1, L0_gnn_w2, L0_gnn_b2)
    x = x + _L0_ffn_ref(_layernorm(x, axis=-1)[None], L0_ffn_sW1, L0_ffn_sb1, L0_ffn_sW2, L0_ffn_sb2, L0_ffn_sW3, L0_ffn_sb3, L0_ffn_eW1, L0_ffn_eb1, L0_ffn_eW2, L0_ffn_eb2, L0_ffn_eW3, L0_ffn_eb3, L0_ffn_gW, L0_ffn_gb)[0]
    x = x + _L1_gnn_ref(_layernorm(x, axis=-1), adj, L1_gnn_Wq, L1_gnn_Wk, L1_gnn_Wv, L1_gnn_weightr, L1_gnn_weightd, L1_gnn_bias)
    x = x + _L1_ffn_ref(_layernorm(x, axis=-1)[None], L1_ffn_hl_w, L1_ffn_hl_b, L1_ffn_wq, L1_ffn_wk, L1_ffn_wv, L1_ffn_gate_w, L1_ffn_gate_b, L1_ffn_ln_g, L1_ffn_ln_b, L1_ffn_fc1_w, L1_ffn_fc1_b, L1_ffn_fc2_w, L1_ffn_fc2_b, L1_ffn_fnorm_g, L1_ffn_fnorm_b, L1_ffn_fgate_w)[0]
    return x

_drawn_inputs = setup_inputs


def setup_inputs(seed=0):
    import zlib

    import numpy as np

    out = dict(_drawn_inputs(seed))
    spreads = {'L0_gnn_b': (0.0, 0.1),
     'L0_ffn_sb1': (0.0, 0.597),
     'L0_ffn_sb2': (0.0, 0.1),
     'L0_ffn_sb3': (0.0, 0.1),
     'L0_ffn_eb1': (0.0, 0.8),
     'L0_ffn_eb2': (0.0, 0.518),
     'L0_ffn_eb3': (0.0, 0.1),
     'L0_ffn_gb': (0.0, 0.399),
     'L1_gnn_bias': (0.0, 0.1),
     'L1_ffn_ln_g': (1.0, 0.2),
     'L1_ffn_ln_b': (0.0, 0.321),
     'L1_ffn_fnorm_g': (1.0, 0.2),
     'L1_ffn_fnorm_b': (0.0, 0.312)}
    factors = {'L1_ffn_wq': 7.818,
     'L1_ffn_wk': 7.629,
     'L1_ffn_wv': 4.299,
     'L1_ffn_gate_w': 8.0,
     'L1_ffn_gate_b': 8.0,
     'L1_ffn_fc1_w': 5.184,
     'L1_ffn_fc1_b': 8.0,
     'L1_ffn_fc2_w': 4.702,
     'L1_ffn_fc2_b': 4.626}
    for name, (base, spread) in spreads.items():
        noise = np.random.default_rng([zlib.crc32(name.encode()), seed]).standard_normal(out[name].shape)
        drawn = base * np.exp(spread * noise) if base else spread * noise
        out[name] = jnp.asarray(drawn.astype(out[name].dtype))
    for name, factor in factors.items():
        out[name] = (out[name] * factor).astype(out[name].dtype)
    return out
```

```python
from contextlib import ExitStack

import concourse.bass as bass
from concourse import mybir

ALU = mybir.AluOpType
ACT = mybir.ActivationFunctionType
AX = mybir.AxisListType
F32 = mybir.dt.float32
BF16 = mybir.dt.bfloat16
F16 = mybir.dt.float16
I32 = mybir.dt.int32

P = 128
N = 4096
D = 128
NT = N // P
CT = 4
CW = CT * P
NC = N // CW
HALF = N // 2
SLOPE = 0.01
BIG = 2.0 ** 60
FLOOR = -(2.0 ** 40)
M16_MAX = 60000.0
G_HEADS, G_DH = 2, 64
F_HEADS, F_EXP, F_DH = 4, 4, 32
S_HIDDEN, E_HIDDEN, N_EXP = 128, 64, 4


class Count:

    def __init__(self, sem, per=0, credit=0):
        self.sem, self.per, self.credit = sem, per, credit

    def after(self, turn, k):
        return turn * self.per + (self.credit + k)


class Chain:

    def __init__(self, eng, sem, turn=0, per=0):
        self.eng, self.sem, self.base, self.k, self.per = eng, sem, turn * per, 0, per

    def link(self, ins):
        self.k += 1
        ins.then_inc(self.sem, 1)
        self.eng.wait_ge(self.sem, self.base + self.k)


class Core:

    def __init__(self, nc, ctx):
        self.nc, self.ctx = nc, ctx
        self.X = self.sb(ctx, "X", [P, NT, D], F32)
        self.ident = self.sb(ctx, "ident", [P, P], F32)
        self.identb = self.sb(ctx, "identb", [P, P], BF16)
        self.negbig = self.sb(ctx, "negbig", [P, P], BF16)
        self.ones = self.sb(ctx, "ones", [P, P], F32)

    def sb(self, ctx, name, shape, dt):
        return ctx.enter_context(self.nc.sbuf_tensor(name, shape, dt))

    def ps(self, ctx, name, shape, dt=F32):
        return ctx.enter_context(self.nc.psum_tensor(name, shape, dt))

    def sem(self, name):
        return self.ctx.enter_context(self.nc.semaphore(name))


def stage_constants(k, x):
    nc = k.nc
    x_in, zeroed, made = k.sem("x_in"), k.sem("const_zeroed"), k.sem("const_made")
    with nc.Block() as block:
        @block.sync
        def _(sp):
            sp.dma_start(k.X[:], x.rearrange("(t p) f -> p t f", p=P)).then_inc(x_in, 16)
            sp.wait_ge(x_in, 16)

        @block.gpsimd
        def _(pool):
            pool.memset(k.ones[:], 1.0).then_inc(made, 1)
            for m in (k.ident, k.identb, k.negbig):
                pool.memset(m[:], 0.0).then_inc(zeroed, 1)
            pool.wait_ge(zeroed, 3)
            for m, fill in ((k.ident, 1.0), (k.identb, 1.0), (k.negbig, -BIG)):
                pool.affine_select(out=m[:], in_=m[:], compare_op=ALU.not_equal, fill=fill, base=0,
                                   pattern=[[-1, P]], channel_multiplier=1).then_inc(made, 1)


def emit_layernorm(dve, chain, src, dst, sq, st, width, eps, std_in, std_out):
    shape = list(src.shape)
    s = [st[:, i] for i in range(5)]

    def wide(a):
        return a.unsqueeze(len(shape) - 1).broadcast_to(shape)

    chain.link(dve.tensor_reduce(s[0], src, AX.X, ALU.add))
    chain.link(dve.tensor_scalar(s[0], s[0], 1.0 / width, None, ALU.mult))
    chain.link(dve.tensor_tensor(dst, src, wide(s[0]), ALU.subtract))
    chain.link(dve.tensor_tensor(sq, dst, dst, ALU.mult))
    chain.link(dve.tensor_reduce(s[1], sq, AX.X, ALU.add))
    dve.tensor_scalar(s[1], s[1], 1.0 / width, eps, ALU.mult, ALU.add).then_inc(std_in, 1)
    dve.wait_ge(std_out, 1)
    chain.link(dve.reciprocal(s[3], s[2]))
    chain.link(dve.tensor_tensor(s[4], s[3], s[3], ALU.mult))
    chain.link(dve.tensor_tensor(s[4], s[4], s[1], ALU.mult))
    chain.link(dve.tensor_scalar(s[4], s[4], -0.5, 1.5, ALU.mult, ALU.add))
    chain.link(dve.tensor_tensor(s[3], s[3], s[4], ALU.mult))
    chain.link(dve.tensor_tensor(dst, dst, wide(s[3]), ALU.mult))


def stage_layernorm(k, tag, Y, YT=None):
    nc = k.nc
    with ExitStack() as ctx:
        sq = k.sb(ctx, f"{tag}_sq", [P, NT, D], F32)
        st = k.sb(ctx, f"{tag}_st", [P, 5, NT], F32)
        pt = k.ps(ctx, f"{tag}_pt", [P, 2, CW])
        steps, std_in, std_out = k.sem(f"{tag}_steps"), k.sem(f"{tag}_var"), k.sem(f"{tag}_std")
        y_done, turned, moved = k.sem(f"{tag}_y_done"), k.sem(f"{tag}_turned"), k.sem(f"{tag}_moved")
        with nc.Block() as block:
            @block.vector
            def _(dve):
                emit_layernorm(dve, Chain(dve, steps), k.X[:], Y, sq[:], st, D, 1e-5, std_in, std_out)
                dve.sem_inc(y_done, 1)

            @block.scalar
            def _(act):
                act.wait_ge(std_in, 1)
                nc.scalar.activation(st[:, 2], st[:, 1], ACT.Sqrt).then_inc(std_out, 1)
                if YT is not None:
                    for c in range(NC):
                        act.wait_ge(turned, c + 1)
                        nc.scalar.activation(YT[:, c * CW:(c + 1) * CW], pt[:, c % 2], ACT.Copy).then_inc(moved, 1)

            if YT is not None:
                @block.tensor
                def _(pe):
                    pe.wait_ge(y_done, 1)
                    for c in range(NC):
                        if c >= 2:
                            pe.wait_ge(moved, c - 1)
                        for t in range(CT):
                            mm = nc.tensor.matmul(pt[:, c % 2, t * P:(t + 1) * P], Y[:, c * CT + t, :],
                                                  k.ident[:], start=(t == 0), stop=True, skip_group_check=True)
                        mm.then_inc(turned, 1)


def stage_gat_vectors(k, g, a):
    nc = k.nc
    with ExitStack() as ctx:
        in2 = k.sb(ctx, "in2", [P, NT, D], F32)
        sq = k.sb(ctx, "in2_sq", [P, NT, D], F32)
        W = k.sb(ctx, "gat_W", [P, D], F32)
        cols = k.sb(ctx, "gat_cols", [P, 5], F32)
        Ab = k.sb(ctx, "gat_Ab", [P, 2, D], F32)
        kap = k.sb(ctx, "gat_kap", [P, 2], F32)
        pA = k.ps(ctx, "gat_pA", [P, 2, D])
        pk = k.ps(ctx, "gat_pk", [P, 2])
        pF = k.ps(ctx, "gat_pF", [P, 2, CW])
        pS = k.ps(ctx, "gat_pS", [P, D + 1])
        loaded, steps, prod = k.sem("gatv_loaded"), k.sem("gatv_steps"), k.sem("gatv_A_done")
        f_done, rows, moved, summed = k.sem("gatv_f"), k.sem("gatv_rows"), k.sem("gatv_moved"), k.sem("gatv_sum")
        sv_done, filled = k.sem("gatv_sv"), k.sem("gatv_filled")
        with nc.Block() as block:
            @block.sync
            def _(sp):
                sp.dma_start(W[:], a["W"]).then_inc(loaded, 16)
                for i, v in enumerate((a["w1"], a["w2"], a["b"])):
                    sp.dma_start(cols[:, i:i + 1], v.rearrange("(p o) -> p o", o=1)).then_inc(loaded, 16)
                for i, v in enumerate((a["b1"], a["b2"])):
                    sp.dma_start(cols[:, 3 + i:4 + i], v.rearrange("(o p) -> o p", o=1).broadcast_to([P, 1])).then_inc(loaded, 16)
                sp.dma_start(in2[:], a["inlayer2"].rearrange("(t p) f -> p t f", p=P)).then_inc(loaded, 16)

            @block.gpsimd
            def _(pool):
                pool.memset(g.row0[:], 0.0).then_inc(filled, 1)
                pool.wait_ge(filled, 1)
                pool.memset(g.row0[0:1, :], 1.0).then_inc(filled, 1)
                pool.memset(g.V[:, :, D:D + 1], 1.0).then_inc(filled, 1)

            @block.tensor
            def _(pe):
                pe.wait_ge(loaded, 16 * 7)
                for i in range(2):
                    w = cols[:, i:i + 1].broadcast_to([P, P])
                    nc.tensor.matmul(pA[:, i], w, W[:], start=(i == 0), stop=True, skip_group_check=True)
                for i in range(2):
                    w = cols[:, i:i + 1].broadcast_to([P, P])
                    mm = nc.tensor.matmul(pk[:, i:i + 1], w, cols[:, 2:3], start=(i == 0), stop=True, skip_group_check=True)
                mm.then_inc(prod, 1)
                pe.wait_ge(filled, 3)
                for t in range(NT):
                    mm = nc.tensor.matmul(pS[:], k.ones[:], g.V[:, t, :], start=(t == 0), stop=(t == NT - 1))
                mm.then_inc(summed, 1)
                for i in range(2):
                    pe.wait_ge(f_done, i + 1)
                    for c in range(NC):
                        n = i * NC + c
                        if n >= 2:
                            pe.wait_ge(moved, n - 1)
                        for t in range(CT):
                            f = g.fcol[:, i, c * CT + t:c * CT + t + 1].broadcast_to([P, P])
                            mm = nc.tensor.matmul(pF[:, n % 2, t * P:(t + 1) * P], f, k.ident[:],
                                                  start=(t == 0), stop=True, skip_group_check=True)
                        mm.then_inc(rows, 1)

            @block.scalar
            def _(act):
                for i, dst in enumerate((g.f1row, g.f2row)):
                    for c in range(NC):
                        n = i * NC + c
                        act.wait_ge(rows, n + 1)
                        nc.scalar.activation(dst[:, c * CW:(c + 1) * CW], pF[:, n % 2], ACT.Copy).then_inc(moved, 1)

            @block.vector
            def _(dve):
                ch = Chain(dve, steps)
                dve.wait_ge(prod, 1)
                ch.link(dve.tensor_copy(Ab[:], pA[:]))
                ch.link(dve.tensor_tensor(kap[:], pk[:], cols[:, 3:5], ALU.add))
                dve.wait_ge(loaded, 16 * 7)
                for i in range(2):
                    w = Ab[:, i:i + 1, :].broadcast_to([P, NT, D])
                    ch.link(dve.tensor_tensor(sq[:], in2[:], w, ALU.mult))
                    ch.link(dve.tensor_reduce(g.fcol[:, i], sq[:], AX.X, ALU.add))
                    dve.tensor_scalar(g.fcol[:, i], g.fcol[:, i], kap[:, i:i + 1], None, ALU.add).then_inc(f_done, 1)
                dve.wait_ge(f_done, 2)
                ch.link(dve.tensor_scalar(g.f2s[:, 0], g.fcol[:, 1], SLOPE, None, ALU.mult))
                ch.link(dve.tensor_scalar(g.f2s[:, 1], g.fcol[:, 1], 1 - SLOPE, None, ALU.mult))
                dve.wait_ge(summed, 1)
                dve.tensor_copy(g.sumV[:], pS[:]).then_inc(sv_done, 1)


def stage_gat(k, g, adj):
    nc = k.nc
    QW = N // 4
    QN = 4 * CT
    AS = 4
    TS = 2
    LS = 4
    PSL = 4
    LAG = 2
    with ExitStack() as ctx:
        A = k.sb(ctx, "gat_adj", [P, AS, QW], I32)
        NM = k.sb(ctx, "gat_nm", [P, 2, CT, N], BF16)
        L = k.sb(ctx, "gat_logits", [P, LS, CW], F32)
        Pr = k.sb(ctx, "gat_probs", [P, PSL, CW], F32)
        f1c = k.sb(ctx, "gat_f1c", [P, CW], F32)
        mx = k.sb(ctx, "gat_mx", [P, CT, 4], F32)
        m4 = k.sb(ctx, "gat_m4", [P, 4, CT], F32)
        ecol = k.sb(ctx, "gat_ecol", [P, CT], F32)
        erow = k.sb(ctx, "gat_erow", [1, CW], F32)
        Mrow = k.sb(ctx, "gat_Mrow", [P, CW], BF16)
        rd = k.sb(ctx, "gat_rd", [P, CT], F32)
        pm = k.ps(ctx, "gat_pm", [P, 2, QW])
        pt = k.ps(ctx, "gat_pt", [P, TS, CW])
        po = k.ps(ctx, "gat_po", [P, CT, 2 * P])

        adj_in = [k.sem(f"gat_adj_in{s}") for s in range(AS)]
        converted = Count(k.sem("gat_converted"), QN, AS)
        biased = Count(k.sem("gat_biased"), QN + 2)
        reduced = Count(k.sem("gat_reduced"), QN + 2, 2)
        mcol = Count(k.sem("gat_mcol"), 1)
        steps = k.sem("gat_steps")
        f1_here = Count(k.sem("gat_f1_here"), 1)
        masked = Count(k.sem("gat_masked"), NT)
        logits = Count(k.sem("gat_logits_done"), NT)
        summed = Count(k.sem("gat_added"), NT, TS)
        probs = Count(k.sem("gat_probs_done"), NT, LS)
        used = Count(k.sem("gat_probs_used"), NT, PSL)
        out_done = Count(k.sem("gat_out"), 1)
        out_moved = Count(k.sem("gat_out_moved"), CT, CT)

        with nc.Block() as block:
            @block.sync
            def _(sp):
                with sp.Fori(0, NC) as c:
                    for q in range(QN):
                        t, w, s = q // 4, q % 4, q % AS
                        sp.wait_ge(converted.sem, converted.after(c, q + 1 - AS))
                        sp.dma_start(A[:, s], adj[bass.ds((c * CT + t) * P, P), w * QW:(w + 1) * QW]).then_inc(adj_in[s], 16)

            @block.vector
            def _(dve):
                dve.sem_inc(converted.sem, AS)
                dve.sem_inc(reduced.sem, 2)
                dve.sem_inc(summed.sem, TS)
                dve.sem_inc(out_moved.sem, CT)

                def convert(c, q):
                    t, w, s = q // 4, q % 4, q % AS
                    dve.wait_ge(adj_in[s], 16 * (c * (QN // AS) + q // AS + 1))
                    dve.tensor_scalar(NM[:, bass.ds(c % 2, 1), t, w * QW:(w + 1) * QW], A[:, s:s + 1], 0.0, None,
                                      ALU.is_le).then_inc(converted.sem, 1)

                def chunk(c, convert_next):
                    ch = Chain(dve, steps, c, 9)
                    for q in range(QN):
                        dve.wait_ge(biased.sem, biased.after(c, q + 1))
                        dve.tensor_reduce(mx[:, q // 4, q % 4:q % 4 + 1], pm[:, q % 2], AX.X, ALU.max).then_inc(reduced.sem, 1)
                    dve.wait_ge(reduced.sem, reduced.after(c, QN))
                    dve.tensor_copy(f1c[:].unsqueeze(1), g.f1row[:, bass.ds(c * CW, CW)].unsqueeze(1)).then_inc(f1_here.sem, 1)
                    F, z, M, Mn = (m4[:, i] for i in range(4))
                    ch.link(dve.tensor_reduce(F, mx[:], AX.X, ALU.max))
                    ch.link(dve.tensor_scalar(ecol[:], F, -BIG / 2, None, ALU.is_lt))
                    ch.link(dve.tensor_scalar(F, F, FLOOR, None, ALU.max))
                    ch.link(dve.tensor_tensor(z, F, g.fcol[:, 0, bass.ds(c * CT, CT)], ALU.add))
                    ch.link(dve.tensor_scalar(M, z, SLOPE, None, ALU.mult))
                    ch.link(dve.tensor_tensor(M, M, z, ALU.max))
                    dve.scalar_tensor_tensor(out=Mn, in0=g.fcol[:, 0, bass.ds(c * CT, CT)], scalar=SLOPE, in1=M,
                                             op0=ALU.mult, op1=ALU.subtract).then_inc(mcol.sem, 1)
                    dve.wait_ge(biased.sem, biased.after(c, QN + 1))
                    dve.tensor_copy(Mrow[:], pm[:, 0, 0:CW]).then_inc(reduced.sem, 1)
                    dve.wait_ge(biased.sem, biased.after(c, QN + 2))
                    ch.link(dve.tensor_copy(erow[:], pm[0:1, 1, 0:CW]))
                    ch.link(dve.tensor_copy(g.Erow[0:1, bass.ds(c * CW, CW)], erow[:]))
                    dve.sem_inc(reduced.sem, 1)
                    for j in range(NT):
                        s = j % TS
                        dve.wait_ge(masked.sem, masked.after(c, j + 1))
                        dve.wait_ge(logits.sem, logits.after(c, j + 1))
                        dve.tensor_tensor(L[:, j % LS], pt[:, s], L[:, j % LS], ALU.add).then_inc(summed.sem, 1)
                        if convert_next and j % 2 == 1:
                            convert(c + 1, j // 2)
                    dve.wait_ge(out_done.sem, out_done.after(c, 1))
                    dve.reciprocal(rd[:], po[:, :, D]).then_inc(steps, 1)
                    return ch

                def finish(c):
                    dve.wait_ge(steps, (c + 1) * 9)
                    for t in range(CT):
                        xt = k.X[:, bass.ds(c * CT + t, 1), :]
                        dve.scalar_tensor_tensor(out=xt, in0=po[:, t:t + 1, 0:D], scalar=rd[:, t:t + 1], in1=xt,
                                                 op0=ALU.mult, op1=ALU.add).then_inc(out_moved.sem, 1)

                for q in range(QN):
                    convert(0, q)
                with dve.Fori(0, NC - 1) as c:
                    chunk(c, True)
                    finish(c)
                chunk(NC - 1, False)
                finish(NC - 1)

            @block.scalar
            def _(act):
                act.sem_inc(probs.sem, LS)
                with act.Fori(0, NC) as c:
                    def logit(j):
                        act.wait_ge(probs.sem, probs.after(c, j + 1 - LS))
                        if j == 0:
                            act.wait_ge(f1_here.sem, f1_here.after(c, 1))
                        nc.scalar.activation(L[:, j % LS], f1c[:], ACT.Relu, bias=g.f2s[:, 1, j:j + 1],
                                             scale=1 - SLOPE).then_inc(logits.sem, 1)

                    logit(0)
                    for j in range(NT):
                        if j + 1 < NT:
                            logit(j + 1)
                        act.wait_ge(summed.sem, summed.after(c, j + 1))
                        act.wait_ge(used.sem, used.after(c, j + 1 - PSL))
                        nc.scalar.activation(Pr[:, j % PSL], L[:, j % LS], ACT.Exp,
                                             bias=g.f2s[:, 0, j:j + 1]).then_inc(probs.sem, 1)

            @block.tensor
            def _(pe):
                pe.sem_inc(used.sem, PSL)
                with pe.Fori(0, NC) as c:
                    par = c % 2
                    for q in range(QN):
                        t, w = q // 4, q % 4
                        pe.wait_ge(converted.sem, converted.after(c, q + 1))
                        pe.wait_ge(reduced.sem, reduced.after(c, q + 1 - 2))
                        for h in range(2):
                            o = w * QW + h * CW
                            dst = pm[:, q % 2, h * CW:(h + 1) * CW]
                            nc.tensor.matmul(dst, k.negbig[:], NM[:, bass.ds(par, 1), t, o:o + CW], start=True, stop=False)
                            mm = nc.tensor.matmul(dst, g.row0[:], g.f2row[:, o:o + CW], start=False, stop=True)
                        mm.then_inc(biased.sem, 1)
                    pe.wait_ge(mcol.sem, mcol.after(c, 1))
                    pe.wait_ge(reduced.sem, reduced.after(c, QN))
                    for t in range(CT):
                        mm = nc.tensor.matmul(pm[:, 0, t * P:(t + 1) * P], m4[:, 3, t:t + 1].broadcast_to([P, P]),
                                              k.ident[:], start=(t == 0), stop=True, skip_group_check=True)
                    mm.then_inc(biased.sem, 1)
                    for t in range(CT):
                        mm = nc.tensor.matmul(pm[0:1, 1, t * P:(t + 1) * P], ecol[:, t:t + 1],
                                              k.ident[:], start=(t == 0), stop=True, skip_group_check=True)
                    mm.then_inc(biased.sem, 1)
                    pe.wait_ge(reduced.sem, reduced.after(c, QN + 2))
                    for j in range(NT + LAG):
                        if j < NT:
                            pe.wait_ge(summed.sem, summed.after(c, j + 1 - TS))
                            nc.tensor.matmul(pt[:, j % TS], g.row0[:], Mrow[:], start=True, stop=False, skip_group_check=True)
                            for t in range(CT):
                                mm = nc.tensor.matmul(pt[:, j % TS, t * P:(t + 1) * P],
                                                      NM[:, bass.ds(par, 1), t, j * P:(j + 1) * P], k.negbig[:],
                                                      start=False, stop=(t == CT - 1), skip_group_check=True)
                            mm.then_inc(masked.sem, 1)
                        i = j - LAG
                        if i < 0:
                            continue
                        pe.wait_ge(probs.sem, probs.after(c, i + 1))
                        if i == 0:
                            pe.wait_ge(out_moved.sem, out_moved.after(c, 0))
                        for t in range(CT):
                            mm = nc.tensor.matmul(po[:, t, 0:D + 1], Pr[:, i % PSL, t * P:(t + 1) * P], g.V[:, i, :],
                                                  start=(i == 0 and t % 2 == 0), stop=False, skip_group_check=True)
                        mm.then_inc(used.sem, 1)
                    for t in range(CT):
                        mm = nc.tensor.matmul(po[:, t, 0:D + 1], erow[0:1, t * P:(t + 1) * P], g.sumV[0:1, :],
                                              start=False, stop=True, skip_group_check=True)
                    mm.then_inc(out_done.sem, 1)


class Gat:
    def __init__(self, k, ctx):
        self.V = k.sb(ctx, "gat_V", [P, NT, D + 1], F32)
        self.fcol = k.sb(ctx, "gat_fcol", [P, 2, NT], F32)
        self.f1row = k.sb(ctx, "gat_f1row", [P, N], F32)
        self.f2row = k.sb(ctx, "gat_f2row", [P, N], BF16)
        self.row0 = k.sb(ctx, "gat_row0", [P, P], BF16)
        self.sumV = k.sb(ctx, "gat_sumV", [P, D + 1], F32)
        self.f2s = k.sb(ctx, "gat_f2s", [P, 2, NT], F32)
        self.Erow = k.Erow


def build(nc, a, out):
    with ExitStack() as top:
        k = Core(nc, top)
        k.Erow = k.sb(top, "Erow", [1, N], BF16)
        stage_constants(k, a["x"])
        with ExitStack() as ctx:
            g = Gat(k, ctx)
            stage_layernorm(k, "ln0", g.V[:, :, 0:D])
            stage_gat_vectors(k, g, a)
            stage_gat(k, g, a["adj"])
        with ExitStack() as ctx:
            Y = k.sb(ctx, "moe_Y", [P, NT, D], F32)
            YT = k.sb(ctx, "moe_YT", [P, N], F32)
            stage_layernorm(k, "ln1", Y[:], YT)
            stage_moe(k, a, Y, YT)
        stage_graph_attention(k, a)
        with ExitStack() as ctx:
            SX = k.sb(ctx, "sa_SX", [P, NT, D], F32)
            MIX = k.sb(ctx, "sa_MIX", [P, NT, D], F32)
            stage_self_attention(k, a, (SX, MIX))
            stage_feed_forward(k, a, SX, MIX)
        stored = k.sem("stored")
        with nc.Block() as block:
            @block.sync
            def _(sp):
                sp.dma_start(out.rearrange("(t p) f -> p t f", p=P), k.X[:]).then_inc(stored, 16)
                sp.wait_ge(stored, 16)


def emit_softmax4(dve, chain, lg, tmp, exp_in, exp_out, turn=0):
    def wide(a):
        return a.unsqueeze(2).broadcast_to([P, NT, 4])

    chain.link(dve.tensor_reduce(tmp, lg, AX.X, ALU.max))
    dve.tensor_tensor(lg, lg, wide(tmp), ALU.subtract).then_inc(exp_in, 1)
    dve.wait_ge(exp_out, turn + 1)
    chain.link(dve.tensor_reduce(tmp, lg, AX.X, ALU.add))
    chain.link(dve.reciprocal(tmp, tmp))
    chain.link(dve.tensor_tensor(lg, lg, wide(tmp), ALU.mult))


def stage_moe(k, a, Y, YT):
    nc = k.nc
    U = 1 + N_EXP
    with ExitStack() as ctx:
        W1 = k.sb(ctx, "moe_W1", [P, U, P], F32)
        W2 = k.sb(ctx, "moe_W2", [P, U, P], F32)
        W3 = k.sb(ctx, "moe_W3", [P, U, P], F32)
        b1 = k.sb(ctx, "moe_b1", [P, U], F32)
        b2 = k.sb(ctx, "moe_b2", [P, U], F32)
        b3 = k.sb(ctx, "moe_b3", [P, D], F32)
        gW = k.sb(ctx, "moe_gW", [P, N_EXP], F32)
        gb = k.sb(ctx, "moe_gb", [P, N_EXP], F32)
        G = k.sb(ctx, "moe_G", [P, NT, N_EXP], F32)
        sel = k.sb(ctx, "moe_sel", [P, 2, NT, N_EXP], F32)
        coef = k.sb(ctx, "moe_coef", [P, NT, N_EXP], F32)
        sm = k.sb(ctx, "moe_small", [P, 6, NT], F32)
        H1 = k.sb(ctx, "moe_H1", [P, 2, CW], F32)
        H2s = k.sb(ctx, "moe_H2s", [P, CW], F32)
        H2 = k.sb(ctx, "moe_H2", [P, 2, CW], F32)
        cc = k.sb(ctx, "moe_cc", [P, CT, N_EXP], F32)
        p1 = k.ps(ctx, "moe_p1", [P, 2, CW])
        p2 = k.ps(ctx, "moe_p2", [P, 2, CW])
        p3 = k.ps(ctx, "moe_p3", [P, 2, CT, P])
        pg = k.ps(ctx, "moe_pg", [P, NT, N_EXP])
        loaded, steps, gated = k.sem("moe_loaded"), k.sem("moe_steps"), k.sem("moe_gated")
        exp_in, exp_out = k.sem("moe_exp_in"), k.sem("moe_exp_out")
        w_in, w_out, coef_ok = k.sem("moe_w_in"), k.sem("moe_w_out"), k.sem("moe_coef_done")
        ones_ok = k.sem("moe_ones")
        h1 = Count(k.sem("moe_h1"), U, 2)
        r1 = Count(k.sem("moe_r1"), U, 2)
        h2 = Count(k.sem("moe_h2"), U, 2)
        r2 = Count(k.sem("moe_r2"), U, 2)
        h3 = Count(k.sem("moe_h3"), U, 2)
        added = Count(k.sem("moe_added"), U, 2)
        steps2 = k.sem("moe_steps2")
        n_loads = 7 * 1 + 7

        def last_user(u):
            return {0: 0, 1: -1}.get(u, u - 1)

        def hidden2(u):
            return H2s[:] if u == 0 else H2[:, u % 2]

        def rows(u):
            return S_HIDDEN if u == 0 else E_HIDDEN + 1

        with nc.Block() as block:
            @block.sync
            def _(sp):
                sp.dma_start(W1[:, 0], a["sW1"]).then_inc(loaded, 16)
                sp.dma_start(W1[:, 1:U], a["eW1"].rearrange("e i o -> i e o")).then_inc(loaded, 16)
                sp.dma_start(W2[:, 0], a["sW2"]).then_inc(loaded, 16)
                sp.dma_start(W2[:, 1:U, 0:E_HIDDEN], a["eW2"].rearrange("e i o -> i e o")).then_inc(loaded, 16)
                sp.dma_start(W3[:, 0], a["sW3"]).then_inc(loaded, 16)
                sp.dma_start(W3[0:E_HIDDEN, 1:U], a["eW3"].rearrange("e i o -> i e o")).then_inc(loaded, 16)
                sp.dma_start(W3[E_HIDDEN:E_HIDDEN + 1, 1:U], a["eb3"].rearrange("(a e) o -> a e o", a=1)).then_inc(loaded, 16)
                sp.dma_start(b1[:, 0:1], a["sb1"].rearrange("(p o) -> p o", o=1)).then_inc(loaded, 16)
                sp.dma_start(b1[:, 1:U], a["eb1T"]).then_inc(loaded, 16)
                sp.dma_start(b2[:, 0:1], a["sb2"].rearrange("(p o) -> p o", o=1)).then_inc(loaded, 16)
                sp.dma_start(b2[0:E_HIDDEN, 1:U], a["eb2T"]).then_inc(loaded, 16)
                sp.dma_start(b3[:], a["sb3"].rearrange("(o n) -> o n", o=1).broadcast_to([P, D])).then_inc(loaded, 16)
                sp.dma_start(gW[:], a["gW"]).then_inc(loaded, 16)
                sp.dma_start(gb[:], a["gb"].rearrange("(o n) -> o n", o=1).broadcast_to([P, N_EXP])).then_inc(loaded, 16)

            @block.gpsimd
            def _(pool):
                pool.memset(H2[:], 1.0).then_inc(ones_ok, 1)

            @block.tensor
            def _(pe):
                pe.wait_ge(loaded, 16 * n_loads)
                for t in range(NT):
                    mm = nc.tensor.matmul(pg[:, t], YT[:, t * P:(t + 1) * P], gW[:], start=(t == 0), stop=True,
                                          skip_group_check=True)
                mm.then_inc(gated, 1)
                pe.sem_inc(h1.sem, 2)
                pe.sem_inc(h2.sem, 2)
                pe.sem_inc(h3.sem, 2)
                pe.wait_ge(ones_ok, 1)

                with pe.Fori(0, NC) as c:
                    def first(u):
                        pe.wait_ge(r1.sem, r1.after(c, last_user(u)))
                        nc.tensor.matmul(p1[:, u % 2].unsqueeze(1), W1[:, u], YT[:, bass.ds(c * CW, CW)].unsqueeze(1),
                                         start=True, stop=True).then_inc(h1.sem, 1)

                    def second(u):
                        m = S_HIDDEN if u == 0 else E_HIDDEN
                        pe.wait_ge(r1.sem, r1.after(c, u + 1))
                        pe.wait_ge(r2.sem, r2.after(c, last_user(u)))
                        nc.tensor.matmul(p2[0:m, u % 2], W2[:, u, 0:m], H1[:, u % 2], start=True, stop=True).then_inc(h2.sem, 1)

                    def third(u):
                        pe.wait_ge(r2.sem, r2.after(c, u + 1))
                        pe.wait_ge(added.sem, added.after(c, last_user(u)))
                        for t in range(CT):
                            mm = nc.tensor.matmul(p3[:, u % 2, t], hidden2(u)[0:rows(u), t * P:(t + 1) * P],
                                                  W3[0:rows(u), u], start=(t == 0), stop=True, skip_group_check=True)
                        mm.then_inc(h3.sem, 1)

                    first(0)
                    for u in range(U):
                        if u + 1 < U:
                            first(u + 1)
                        second(u)
                        if u >= 1:
                            third(u - 1)
                    third(U - 1)

            @block.scalar
            def _(act):
                act.wait_ge(exp_in, 1)
                nc.scalar.activation(G[:], G[:], ACT.Exp).then_inc(exp_out, 1)
                act.wait_ge(w_in, 1)
                nc.scalar.activation(sm[:, 3], sm[:, 3], ACT.Exp).then_inc(w_out, 1)
                act.sem_inc(r1.sem, 2)
                act.sem_inc(r2.sem, 2)
                act.wait_ge(ones_ok, 1)
                act.wait_ge(loaded, 16 * n_loads)
                with act.Fori(0, NC) as c:
                    def relu1(u):
                        act.wait_ge(h1.sem, h1.after(c, u + 1))
                        act.wait_ge(h2.sem, h2.after(c, last_user(u)))
                        nc.scalar.activation(H1[:, u % 2], p1[:, u % 2], ACT.Relu, bias=b1[:, u:u + 1]).then_inc(r1.sem, 1)

                    def relu2(u):
                        m = S_HIDDEN if u == 0 else E_HIDDEN
                        act.wait_ge(h2.sem, h2.after(c, u + 1))
                        act.wait_ge(h3.sem, h3.after(c, last_user(u)))
                        nc.scalar.activation(hidden2(u)[0:m], p2[0:m, u % 2], ACT.Relu, bias=b2[0:m, u:u + 1]).then_inc(r2.sem, 1)

                    relu1(0)
                    for u in range(U):
                        if u + 1 < U:
                            relu1(u + 1)
                        relu2(u)

            @block.vector
            def _(dve):
                ch = Chain(dve, steps)
                dve.wait_ge(gated, 1)
                ch.link(dve.tensor_tensor(G[:], pg[:], gb[:].unsqueeze(1).broadcast_to([P, NT, N_EXP]), ALU.add))
                emit_softmax4(dve, ch, G[:], sm[:, 0], exp_in, exp_out)
                free, m1, m2 = sm[:, 5], sm[:, 1], sm[:, 2]
                for r, m in enumerate((m1, m2)):
                    ch.link(dve.tensor_reduce(m, G[:], AX.X, ALU.max))
                    ch.link(dve.memset(free, 1.0))
                    for e in range(N_EXP):
                        s = sel[:, r, :, e]
                        ch.link(dve.tensor_tensor(s, G[:, :, e], m, ALU.is_equal))
                        ch.link(dve.tensor_tensor(s, s, free, ALU.mult))
                        ch.link(dve.tensor_tensor(free, free, s, ALU.subtract))
                    if r == 0:
                        ch.link(dve.scalar_tensor_tensor(out=G[:], in0=sel[:, 0], scalar=-2.0, in1=G[:],
                                                         op0=ALU.mult, op1=ALU.add))
                dve.tensor_tensor(sm[:, 3], m2, m1, ALU.subtract).then_inc(w_in, 1)
                dve.wait_ge(w_out, 1)
                ch.link(dve.tensor_scalar(sm[:, 4], sm[:, 3], 1.0, None, ALU.add))
                ch.link(dve.reciprocal(sm[:, 4], sm[:, 4]))
                ch.link(dve.tensor_tensor(sm[:, 3], sm[:, 3], sm[:, 4], ALU.mult))
                for r, w in ((0, sm[:, 4]), (1, sm[:, 3])):
                    ch.link(dve.tensor_tensor(sel[:, r], sel[:, r], w.unsqueeze(2).broadcast_to([P, NT, N_EXP]), ALU.mult))
                ch.link(dve.tensor_tensor(coef[:], sel[:, 0], sel[:, 1], ALU.add))
                ch.link(dve.tensor_tensor(k.X[:], k.X[:], b3[:].unsqueeze(1).broadcast_to([P, NT, D]), ALU.add))
                dve.sem_inc(added.sem, 2)
                with dve.Fori(0, NC) as c:
                    ch = Chain(dve, steps2, c, 1 + CT * U)
                    ch.link(dve.tensor_scalar(cc[:], coef[:, bass.ds(c * CT, CT), :], 1.0, None, ALU.mult))
                    for u in range(U):
                        dve.wait_ge(h3.sem, h3.after(c, u + 1))
                        for t in range(CT):
                            x = k.X[:, bass.ds(c * CT + t, 1), :]
                            o = p3[:, u % 2, t:t + 1]
                            if u == 0:
                                ins = dve.tensor_tensor(x, o, x, ALU.add)
                            else:
                                ins = dve.scalar_tensor_tensor(out=x, in0=o, scalar=cc[:, t, u - 1:u], in1=x,
                                                               op0=ALU.mult, op1=ALU.add)
                            ch.k += 1
                            ins.then_inc(steps2, 1)
                        dve.wait_ge(steps2, ch.base + ch.k)
                        dve.sem_inc(added.sem, 1)


def emit_convert(dve, c, q, A, NM, adj_in, converted, QW, QN, AS):
    t, w, s = q // 4, q % 4, q % AS
    dve.wait_ge(adj_in[s], 16 * (c * (QN // AS) + q // AS + 1))
    dve.tensor_scalar(NM[:, bass.ds(c % 2, 1), t, w * QW:(w + 1) * QW], A[:, s:s + 1], 0.0, None,
                      ALU.is_le).then_inc(converted.sem, 1)


def stage_graph_attention(k, a):
    nc = k.nc
    H, DH = G_HEADS, G_DH
    QW = N // 4
    QN = 4 * CT
    AS = 4
    PSL = 4
    LAG = 2
    U = H * NT
    with ExitStack() as outer:
        qA = k.sb(outer, "ga_qA", [P, H, N], F16)
        kA = k.sb(outer, "ga_kA", [P, H, N], F16)
        qB = k.sb(outer, "ga_qB", [96, H, N], F16)
        kB = k.sb(outer, "ga_kB", [96, H, N], F16)
        V = k.sb(outer, "ga_V", [P, NT, H, DH + 1], F32)
        sumV = k.sb(outer, "ga_sumV", [1, H * (DH + 1)], F32)
        We = k.sb(outer, "ga_We", [DH + 1, 2, H, D + 1], F32)
        bias = k.sb(outer, "ga_bias", [P, D], F32)
        with ExitStack() as ctx:
            YT = k.sb(ctx, "ga_YT", [P, N], F32)
            with ExitStack() as inner:
                Y = k.sb(inner, "ga_Y", [P, NT, D], F32)
                stage_layernorm(k, "ln2", Y[:], YT)
            Wq = k.sb(ctx, "ga_Wq", [P, H, P], F32)
            Wk = k.sb(ctx, "ga_Wk", [P, H, P], F32)
            Wv = k.sb(ctx, "ga_Wv", [P, D], F32)
            pp = k.ps(ctx, "ga_pp", [P, 2, CW])
            pv = k.ps(ctx, "ga_pv", [P, 2, CT, H, DH])
            ps = k.ps(ctx, "ga_ps", [1, H * (DH + 1)])
            loaded, late, filled = k.sem("ga_loaded"), k.sem("ga_late"), k.sem("ga_filled")
            projected, his, los = k.sem("ga_projected"), k.sem("ga_hi"), k.sem("ga_lo")
            vals, vmoved, vsum, vsum_ok = k.sem("ga_values"), k.sem("ga_vmoved"), k.sem("ga_vsum"), k.sem("ga_vsum_ok")
            units = [(h, s, c) for h in range(H) for s in range(2) for c in range(NC)]
            with nc.Block() as block:
                @block.sync
                def _(sp):
                    for h in range(H):
                        for r in range(2):
                            for W, name in ((Wq, "Wq"), (Wk, "Wk")):
                                sp.dma_start(W[:, h, r * DH:(r + 1) * DH], a[name][:, h * DH:(h + 1) * DH]).then_inc(loaded, 16)
                    sp.dma_start(Wv[:], a["Wv"]).then_inc(loaded, 16)
                    for s, name in enumerate(("weightr", "weightd")):
                        sp.dma_start(We[0:DH, s, :, 0:D], a[name].rearrange("(h i) o -> i h o", h=H)).then_inc(late, 16)
                    sp.dma_start(bias[:], a["bias"].rearrange("(o n) -> o n", o=1).broadcast_to([P, D])).then_inc(late, 16)
                    sp.wait_ge(late, 48)

                @block.gpsimd
                def _(pool):
                    for n, (tile, value) in enumerate((
                            (qB[DH:96], 0.0), (kB[DH:96], 0.0), (kB[DH:DH + 1], 1.0), (V[:, :, :, DH:DH + 1], 1.0),
                            (We[0:DH, :, :, D:D + 1], 0.0), (We[DH:DH + 1, :, :, 0:D], 0.0), (We[DH:DH + 1, :, :, D:D + 1], 1.0))):
                        pool.memset(tile, value).then_inc(filled, 1)
                        pool.wait_ge(filled, n + 1)

                @block.tensor
                def _(pe):
                    pe.wait_ge(loaded, 16 * 9)
                    for n, (h, s, c) in enumerate(units):
                        if n >= 2:
                            pe.wait_ge(los, n - 1)
                        nc.tensor.matmul(pp[:, n % 2], (Wk if s else Wq)[:, h], YT[:, c * CW:(c + 1) * CW],
                                         start=True, stop=True).then_inc(projected, 1)
                    for c in range(NC):
                        if c >= 2:
                            pe.wait_ge(vmoved, c - 1)
                        for t in range(CT):
                            mm = nc.tensor.matmul(pv[:, c % 2, t], YT[:, (c * CT + t) * P:(c * CT + t + 1) * P], Wv[:],
                                                  start=(t == 0), stop=True, skip_group_check=True)
                        mm.then_inc(vals, 1)
                    pe.wait_ge(vmoved, NC)
                    pe.wait_ge(filled, 4)
                    for t in range(NT):
                        mm = nc.tensor.matmul(ps[:], k.ones[:, 0:1], V[:, t], start=(t == 0), stop=(t == NT - 1))
                    mm.then_inc(vsum, 1)

                @block.scalar
                def _(act):
                    for n, (h, s, c) in enumerate(units):
                        cols = slice(c * CW, (c + 1) * CW)
                        act.wait_ge(projected, n + 1)
                        if s == 0:
                            nc.scalar.activation(qA[:, h, cols], pp[:, n % 2], ACT.Copy, scale=DH ** -0.5).then_inc(his, 2)
                        else:
                            nc.scalar.activation(kA[:, h, cols], pp[:, n % 2], ACT.Copy).then_inc(his, 1)
                            nc.scalar.activation(kB[0:DH, h, cols], pp[0:DH, n % 2], ACT.Copy).then_inc(his, 1)

                @block.vector
                def _(dve):
                    for n, (h, s, c) in enumerate(units):
                        cols = slice(c * CW, (c + 1) * CW)
                        dve.wait_ge(his, 2 * (n + 1))
                        if s == 0:
                            dve.scalar_tensor_tensor(out=qB[0:DH, h, cols], in0=pp[0:DH, n % 2], scalar=DH ** -0.5,
                                                     in1=qA[0:DH, h, cols], op0=ALU.mult, op1=ALU.subtract).then_inc(los, 1)
                        else:
                            dve.tensor_tensor(kA[DH:P, h, cols], pp[DH:P, n % 2], kA[DH:P, h, cols],
                                              ALU.subtract).then_inc(los, 1)
                    for c in range(NC):
                        dve.wait_ge(vals, c + 1)
                        dve.tensor_copy(V[:, c * CT:(c + 1) * CT, :, 0:DH], pv[:, c % 2]).then_inc(vmoved, 1)
                    dve.wait_ge(vsum, 1)
                    dve.tensor_copy(sumV[:], ps[:]).then_inc(vsum_ok, 1)

        with ExitStack() as ctx:
            A = k.sb(ctx, "ga_adj", [P, AS, QW], I32)
            NM = k.sb(ctx, "ga_nm", [P, 2, CT, N], BF16)
            Pr = k.sb(ctx, "ga_probs", [P, PSL, CW], F32)
            mx = k.sb(ctx, "ga_mx", [P, H, CT, 4], F32)
            mc = k.sb(ctx, "ga_mc", [P, H, CT], F32)
            pm = k.ps(ctx, "ga_pm", [P, 2, QW])
            pt = k.ps(ctx, "ga_pt", [P, 2, CW])
            po = k.ps(ctx, "ga_po", [DH + 1, H, CW])
            uT = k.sb(ctx, "ga_uT", [DH + 1, H, CW], F32)
            er = k.sb(ctx, "ga_er", [1, CW], F32)
            rd = k.sb(ctx, "ga_rd", [P, H, CT], F32)
            Z = k.sb(ctx, "ga_Z", [P, CT, D], F32)
            Z2 = k.sb(ctx, "ga_Z2", [P, CT, D], F32)
            steps = k.sem("ga_steps")
            adj_in = [k.sem(f"ga_adj_in{s}") for s in range(AS)]
            R = H * QN
            converted = Count(k.sem("ga_converted"), QN, AS)
            scored = Count(k.sem("ga_scored"), R + 2 * H)
            reduced = Count(k.sem("ga_reduced"), R + 2 * H, 2)
            mcol = Count(k.sem("ga_mcol"), 3)
            er_here = Count(k.sem("ga_er_here"), 1)
            trans = Count(k.sem("ga_trans"), U)
            probs = Count(k.sem("ga_probs_done"), U, 2)
            used = Count(k.sem("ga_probs_used"), U, PSL)
            out_done = Count(k.sem("ga_out"), H)
            out_moved = Count(k.sem("ga_out_moved"), H, H)
            with nc.Block() as block:
                @block.sync
                def _(sp):
                    with sp.Fori(0, NC) as c:
                        for q in range(QN):
                            t, w, s = q // 4, q % 4, q % AS
                            sp.wait_ge(converted.sem, converted.after(c, q + 1 - AS))
                            sp.dma_start(A[:, s], a["adj"][bass.ds((c * CT + t) * P, P), w * QW:(w + 1) * QW]).then_inc(adj_in[s], 16)

                @block.vector
                def _(dve):
                    dve.sem_inc(converted.sem, AS)
                    dve.sem_inc(reduced.sem, 2)
                    dve.sem_inc(out_moved.sem, H)

                    def chunk(c, convert_next):
                        for r in range(R):
                            h, q = r // QN, r % QN
                            dve.wait_ge(scored.sem, scored.after(c, r + 1))
                            dve.tensor_reduce(mx[:, h, q // 4, q % 4:q % 4 + 1], pm[:, r % 2], AX.X, ALU.max).then_inc(reduced.sem, 1)
                        dve.wait_ge(reduced.sem, reduced.after(c, R))
                        dve.tensor_scalar(er[:], k.Erow[:, bass.ds(c * CW, CW)], 1.0, None, ALU.mult).then_inc(er_here.sem, 1)
                        dve.tensor_reduce(mc[:], mx[:], AX.X, ALU.max).then_inc(mcol.sem, 1)
                        dve.wait_ge(mcol.sem, mcol.after(c, 1))
                        dve.tensor_scalar(mc[:], mc[:], -M16_MAX, M16_MAX, ALU.max, ALU.min).then_inc(mcol.sem, 1)
                        for h in range(H):
                            dve.wait_ge(scored.sem, scored.after(c, R + h + 1))
                            dve.tensor_scalar(qB[DH:DH + 1, h:h + 1, bass.ds(c * CW, CW)], pm[0:1, h:h + 1, 0:CW], -1.0, None,
                                              ALU.mult).then_inc(reduced.sem, 1)
                        if convert_next:
                            for q in range(QN):
                                emit_convert(dve, c + 1, q, A, NM, adj_in, converted, QW, QN, AS)
                        for h in range(H):
                            dve.wait_ge(out_done.sem, out_done.after(c, h + 1))
                            dve.tensor_copy(uT[:, h], po[:, h]).then_inc(out_moved.sem, 1)
                        ch = Chain(dve, steps, c, 5 + 2 * CT)
                        for h in range(H):
                            o = pm[:, h].rearrange("p (t n) -> p t n", t=CT)
                            dve.wait_ge(scored.sem, scored.after(c, R + H + h + 1))
                            ch.link(dve.reciprocal(rd[:, h], o[:, :, D]))
                            for t in range(CT):
                                if h == 0:
                                    ins = dve.tensor_scalar(Z[:, t], o[:, t, 0:D], rd[:, h, t:t + 1], None, ALU.mult)
                                else:
                                    ins = dve.scalar_tensor_tensor(out=Z[:, t], in0=o[:, t, 0:D], scalar=rd[:, h, t:t + 1],
                                                                   in1=Z[:, t], op0=ALU.mult, op1=ALU.add)
                                ch.k += 1
                                ins.then_inc(steps, 1)
                            dve.wait_ge(steps, ch.base + ch.k)
                            dve.sem_inc(reduced.sem, 1)
                        ch.link(dve.tensor_tensor(Z[:], Z[:], bias[:].unsqueeze(1).broadcast_to([P, CT, D]), ALU.add))
                        ch.link(dve.tensor_scalar(Z2[:], Z[:], SLOPE, None, ALU.mult))
                        ch.link(dve.tensor_tensor(Z[:], Z[:], Z2[:], ALU.max))
                        x = k.X[:, bass.ds(c * CT, CT), :]
                        dve.tensor_tensor(x, x, Z[:], ALU.add).then_inc(mcol.sem, 1)
                        dve.wait_ge(mcol.sem, mcol.after(c, 3))

                    for q in range(QN):
                        emit_convert(dve, 0, q, A, NM, adj_in, converted, QW, QN, AS)
                    with dve.Fori(0, NC - 1) as c:
                        chunk(c, True)
                    chunk(NC - 1, False)

                @block.scalar
                def _(act):
                    act.sem_inc(probs.sem, 2)
                    with act.Fori(0, NC) as c:
                        for u in range(U):
                            act.wait_ge(trans.sem, trans.after(c, u + 1))
                            act.wait_ge(used.sem, used.after(c, u + 1 - PSL))
                            nc.scalar.activation(Pr[:, u % PSL], pt[:, u % 2], ACT.Exp).then_inc(probs.sem, 1)

                @block.tensor
                def _(pe):
                    pe.sem_inc(used.sem, PSL)
                    with pe.Fori(0, NC) as c:
                        pe.get_value_cache().nocache = True
                        par = pe.snap(c % 2)
                        for r in range(R):
                            h, q = r // QN, r % QN
                            t, w = q // 4, q % 4
                            if h == 0:
                                pe.wait_ge(converted.sem, converted.after(c, q + 1))
                            pe.wait_ge(reduced.sem, reduced.after(c, r + 1 - 2))
                            for i in range(2):
                                o = w * QW + i * CW
                                dst = pm[:, r % 2, i * CW:(i + 1) * CW]
                                nc.tensor.matmul(dst, k.negbig[:], NM[:, bass.ds(par, 1), t, o:o + CW], start=True, stop=False)
                                mm = nc.tensor.matmul(dst, qA[:, h:h + 1, bass.ds(c * CW + t * P, P)], kA[:, h, o:o + CW],
                                                      start=False, stop=True)
                            mm.then_inc(scored.sem, 1)
                        pe.wait_ge(mcol.sem, mcol.after(c, 2))
                        pe.wait_ge(reduced.sem, reduced.after(c, R))
                        for h in range(H):
                            for t in range(CT):
                                mm = nc.tensor.matmul(pm[0:1, h, t * P:(t + 1) * P], mc[:, h, t:t + 1], k.ident[:],
                                                      start=(t == 0), stop=True, skip_group_check=True)
                            mm.then_inc(scored.sem, 1)
                        for u in range(U + LAG):
                            if u < U:
                                h, j = u // NT, u % NT
                                pe.wait_ge(probs.sem, probs.after(c, u + 1 - 2))
                                if j == 0:
                                    pe.wait_ge(reduced.sem, reduced.after(c, R + h + 1))
                                dst = pt[:, u % 2]
                                rhs = lambda q: q[:, h:h + 1, bass.ds(c * CW, CW)]
                                nc.tensor.matmul(dst.unsqueeze(1), kA[:, h, j * P:(j + 1) * P], rhs(qA), start=True, stop=False,
                                                 skip_group_check=True)
                                nc.tensor.matmul(dst.unsqueeze(1), kB[:, h, j * P:(j + 1) * P], rhs(qB), start=False, stop=False,
                                                 skip_group_check=True)
                                for t in range(CT):
                                    mm = nc.tensor.matmul(pt[:, u % 2, t * P:(t + 1) * P],
                                                          NM[:, bass.ds(par, 1), t, j * P:(j + 1) * P], k.negbig[:],
                                                          start=False, stop=(t == CT - 1), skip_group_check=True)
                                mm.then_inc(trans.sem, 1)
                            v = u - LAG
                            if v < 0:
                                continue
                            h, j = v // NT, v % NT
                            pe.wait_ge(probs.sem, probs.after(c, v + 1))
                            if j == 0:
                                pe.wait_ge(out_moved.sem, out_moved.after(c, h + 1 - H))
                            nc.tensor.matmul(po[:, h], V[:, j, h], Pr[:, v % PSL], start=(j == 0), stop=False,
                                             skip_group_check=True).then_inc(used.sem, 1)
                            if j == NT - 1:
                                pe.wait_ge(er_here.sem, er_here.after(c, 1))
                                nc.tensor.matmul(po[:, h], sumV[0:1, h * (DH + 1):(h + 1) * (DH + 1)], er[:], start=False,
                                                 stop=True, skip_group_check=True).then_inc(out_done.sem, 1)
                        for h in range(H):
                            pe.wait_ge(out_moved.sem, out_moved.after(c, h + 1))
                            pe.wait_ge(reduced.sem, reduced.after(c, R + H))
                            for t in range(CT):
                                mm = nc.tensor.matmul(pm[:, h:h + 1, t * 2 * P:t * 2 * P + D + 1], uT[:, h, t * P:(t + 1) * P],
                                                      We[:, bass.ds(c * CW // HALF, 1), h], start=(t % 2 == 0), stop=True,
                                                      skip_group_check=True)
                            mm.then_inc(scored.sem, 1)



def stage_self_attention(k, a, ctx_out):
    nc = k.nc
    H, E, DH = F_HEADS, F_EXP, F_DH
    HI2, LO, MR = DH, 2 * DH, 3 * DH
    KR = MR + 1
    SCALE = float(DH) ** 0.5
    VW = DH + 1
    QW = 2 * CW
    PSL = 4
    LAG = 2
    SX, MIX = ctx_out
    with ExitStack() as outer:
        sxT = k.sb(outer, "sa_sxT", [P, N], F32)
        V = k.sb(outer, "sa_V", [P, NT, H, VW], F32)
        causA = k.sb(outer, "sa_causA", [P, P], BF16)
        causT = k.sb(outer, "sa_causT", [P, 2 * P], BF16)
        two = k.sb(outer, "sa_two", [KR, P], F32)
        GW = k.sb(outer, "sa_GW", [P, H, E, E * DH], F32)
        gb = k.sb(outer, "sa_gb", [P, H, E], F32)
        notpad = k.sb(outer, "sa_notpad", [P, NT, D], BF16)
        with ExitStack() as ctx:
            HL = k.sb(ctx, "sa_HL", [P, P], F32)
            hb = k.sb(ctx, "sa_hb", [P, 1], F32)
            Wv = k.sb(ctx, "sa_Wv", [P, P], F32)
            YT = k.sb(ctx, "sa_YT", [P, N], F32)
            with ExitStack() as inner:
                Y = k.sb(inner, "sa_Y", [P, NT, D], F32)
                stage_layernorm(k, "ln3", Y[:], YT)
            pp = k.ps(ctx, "sa_pp", [P, 2, CW])
            px = k.ps(ctx, "sa_px", [P, 2, CT, P])
            pv = k.ps(ctx, "sa_pv", [P, 2, CT, P])
            loaded, filled, late = k.sem("sap_loaded"), k.sem("sap_filled"), k.sem("sap_late")
            proj, biased = k.sem("sap_proj"), k.sem("sap_biased")
            turned, xmoved, vals, vmoved = k.sem("sap_turned"), k.sem("sap_xmoved"), k.sem("sap_vals"), k.sem("sap_vmoved")
            with nc.Block() as block:
                @block.sync
                def _(sp):
                    sp.dma_start(HL[:], a["hlT"]).then_inc(loaded, 16)
                    sp.dma_start(hb[:], a["hlb"]).then_inc(loaded, 16)
                    sp.dma_start(Wv[:], a["wvB"]).then_inc(loaded, 16)
                    sp.dma_start(GW[:], a["gate_w"].rearrange("h e f -> (h e f)").rearrange("(o n) -> o n", o=1)
                                 .broadcast_to([P, H * E * E * DH]).rearrange("p (h e f) -> p h e f", h=H, e=E)).then_inc(late, 16)
                    sp.dma_start(gb[:], a["gate_b"].rearrange("h e -> (h e)").rearrange("(o n) -> o n", o=1)
                                 .broadcast_to([P, H * E]).rearrange("p (h e) -> p h e", h=H)).then_inc(late, 16)
                    sp.wait_ge(late, 32)

                @block.gpsimd
                def _(pool):
                    steps = ((causA, 0.0), (causT, 0.0), (two, 0.0))
                    for m, v in steps:
                        pool.memset(m[:], v).then_inc(filled, 1)
                    pool.memset(V[:, :, :, DH:VW], 1.0).then_inc(filled, 1)
                    pool.wait_ge(filled, 4)
                    pool.affine_select(out=causA[:], in_=causA[:], compare_op=ALU.is_ge, fill=-BIG, base=0,
                                       pattern=[[-1, P]], channel_multiplier=1).then_inc(filled, 1)
                    pool.affine_select(out=causT[:], in_=causT[:], compare_op=ALU.is_ge, fill=-BIG, base=-P,
                                       pattern=[[1, 2 * P]], channel_multiplier=-1).then_inc(filled, 1)
                    pool.affine_select(out=two[:], in_=two[:], compare_op=ALU.not_equal, fill=1.0, base=0,
                                       pattern=[[-1, P]], channel_multiplier=1).then_inc(filled, 1)
                    pool.wait_ge(filled, 7)
                    pool.affine_select(out=two[:], in_=two[:], compare_op=ALU.not_equal, fill=1.0, base=-64,
                                       pattern=[[-1, P]], channel_multiplier=1).then_inc(filled, 1)

                @block.tensor
                def _(pe):
                    pe.wait_ge(loaded, 48)
                    for c in range(NC):
                        if c >= 2:
                            pe.wait_ge(biased, c - 1)
                        nc.tensor.matmul(pp[:, c % 2], HL[:], YT[:, c * CW:(c + 1) * CW], start=True, stop=True).then_inc(proj, 1)
                    for c in range(NC):
                        pe.wait_ge(biased, c + 1)
                        for s, (dst, w, done, freed) in enumerate(((px, k.ident, turned, xmoved), (pv, Wv, vals, vmoved))):
                            if c >= 2:
                                pe.wait_ge(freed, c - 1)
                            for t in range(CT):
                                mm = nc.tensor.matmul(dst[:, c % 2, t], sxT[:, (c * CT + t) * P:(c * CT + t + 1) * P], w[:],
                                                      start=(t == 0), stop=True, skip_group_check=True)
                            mm.then_inc(done, 1)

                @block.scalar
                def _(act):
                    act.wait_ge(loaded, 48)
                    for c in range(NC):
                        act.wait_ge(proj, c + 1)
                        nc.scalar.activation(sxT[:, c * CW:(c + 1) * CW], pp[:, c % 2], ACT.Identity, bias=hb[:]).then_inc(biased, 1)

                @block.vector
                def _(dve):
                    for c in range(NC):
                        dve.wait_ge(turned, c + 1)
                        dve.tensor_copy(SX[:, c * CT:(c + 1) * CT], px[:, c % 2]).then_inc(xmoved, 1)
                        dve.wait_ge(vals, c + 1)
                        dve.tensor_copy(V[:, c * CT:(c + 1) * CT, :, 0:DH],
                                        pv[:, c % 2].rearrange("p t (h d) -> p t h d", h=H)).then_inc(vmoved, 1)
                    dve.wait_ge(xmoved, NC)
                    dve.tensor_scalar(notpad[:], SX[:], 0.0, None, ALU.not_equal).then_inc(xmoved, 1)

        with ExitStack() as ctx:
            W = k.sb(ctx, "sa_W", [P, 1 + E, MR], F32)
            QS = k.sb(ctx, "sa_QS", [KR, E, N], F16)
            KS = k.sb(ctx, "sa_KS", [KR, N], F16)
            Vc = k.sb(ctx, "sa_Vc", [P, NT, VW], F32)
            ATT = k.sb(ctx, "sa_ATT", [P, E, NT, DH], F32)
            tmp = k.sb(ctx, "sa_tmp", [P, NT, E, DH], F32)
            Pr = k.sb(ctx, "sa_probs", [P, PSL, CW], F32)
            mx = k.sb(ctx, "sa_mx", [P, CT, 4], F32)
            mc = k.sb(ctx, "sa_mc", [P, 2, CT], F32)
            OT = k.sb(ctx, "sa_OT", [KR, CW], F32)
            rd = k.sb(ctx, "sa_rd", [P, CT], F32)
            lg = k.sb(ctx, "sa_lg", [P, NT, E], F32)
            sm = k.sb(ctx, "sa_sm", [P, NT], F32)
            pm = k.ps(ctx, "sa_pm", [P, 2, QW])
            pt = k.ps(ctx, "sa_pt", [P, 2, CW])
            po = k.ps(ctx, "sa_po", [P, CW])
            pz = k.ps(ctx, "sa_pz", [P, CT, P])

            RW = [CT * (c // 2 + 1) for c in range(NC)]
            TU = [CT * (c + 1) for c in range(NC)]
            R0 = [sum(RW[:c]) for c in range(NC + 1)]
            T0 = [sum(TU[:c]) for c in range(NC + 1)]
            KQ = (1 + E) * NC
            w_in = Count(k.sem("sa_w_in"), 16)
            w_free = Count(k.sem("sa_w_free"), 1, 1)
            proj = Count(k.sem("sa_proj"), KQ)
            his = Count(k.sem("sa_hi"), KQ)
            los = Count(k.sem("sa_lo"), KQ, 2)
            v_here = Count(k.sem("sa_v_here"), 1)
            head_done = Count(k.sem("sa_head_done"), 1, 1)
            scored = Count(k.sem("sa_scored"), R0[NC])
            reduced = Count(k.sem("sa_reduced"), R0[NC], 2)
            mcol = Count(k.sem("sa_mcol"), 2 * NC)
            zin = Count(k.sem("sa_zin"), 2 * NC)
            zout = Count(k.sem("sa_zout"), 2 * NC, 1)
            trans = Count(k.sem("sa_trans"), T0[NC])
            probs = Count(k.sem("sa_probs_done"), T0[NC], 2)
            used = Count(k.sem("sa_used"), T0[NC], PSL)
            summed_out = Count(k.sem("sa_summed_out"), 2 * NC, 2)
            rds = k.sem("sa_rds")
            steps = k.sem("sa_steps")
            e_in, e_out, ready = k.sem("sa_exp_in"), k.sem("sa_exp_out"), k.sem("sa_ready")

            with nc.Block() as block:
                @block.sync
                def _(sp):
                    with sp.Fori(0, H) as n:
                        sp.wait_ge(w_free.sem, w_free.after(n, 0))
                        sp.dma_start(W[:].unsqueeze(1), a["wqk"][:, bass.ds(n, 1)]).then_inc(w_in.sem, 16)

                @block.gpsimd
                def _(pool):
                    pool.memset(OT[:], 0.0).then_inc(ready, 1)
                    pool.wait_ge(ready, 1)
                    pool.memset(KS[MR:KR], 1.0).then_inc(ready, 1)
                    pool.wait_ge(ready, 2)
                    with pool.Fori(0, H) as n:
                        pool.wait_ge(head_done.sem, head_done.after(n, 0))
                        pool.tensor_copy(Vc[:].unsqueeze(2), V[:, :, bass.ds(n, 1), :]).then_inc(v_here.sem, 1)

                def projections():
                    return [(s, c) for s in range(1 + E) for c in range(NC)]

                def z_row(c):
                    return 2 * c - 1 if c else 0

                def z_sums(c):
                    return 2 * c + 2 if c < NC - 1 else 2 * NC - 1

                def schedule(c):
                    n_t, n_r = TU[c], RW[c + 1] if c + 1 < NC else 0
                    first = LAG + 1 if c else 0
                    span = max(1, n_t - 1 - first)
                    order, done = [], 0
                    for j in range(n_t):
                        if c and j == first:
                            order.append(("s", c - 1))
                        due = min(n_r, -(-n_r * (j + 1 - first) // span)) if j >= first else 0
                        while done < due:
                            order.append(("r", done))
                            done += 1
                        order.append(("t", j))
                    return order

                def piece(c, r):
                    per = c // 2 + 1
                    t, w = r // per, r % per
                    end = (c * CT + t + 1) * P
                    return t, w, w * QW, min(end, (w + 1) * QW)

                def first_query(c, j):
                    return 0 if (c == 0 and j == 1) else max(0, j - c * CT) * P

                @block.tensor
                def _(pe):
                    pe.sem_inc(used.sem, PSL)
                    pe.sem_inc(w_free.sem, 1)
                    pe.sem_inc(head_done.sem, 1)
                    pe.wait_ge(ready, 2)
                    with pe.Fori(0, H) as n:
                        pe.get_value_cache().nocache = True
                        pe.wait_ge(w_in.sem, w_in.after(n, 16))
                        for i, (s, c) in enumerate(projections()):
                            pe.wait_ge(los.sem, los.after(n, i + 1 - 2))
                            mm = nc.tensor.matmul(pt[0:MR, i % 2], W[:, s], sxT[:, c * CW:(c + 1) * CW], start=True, stop=True)
                            mm.then_inc(proj.sem, 1)
                        pe.wait_ge(proj.sem, proj.after(n, KQ))
                        pe.sem_inc(w_free.sem, 1)
                        with pe.Fori(0, E) as e:
                            pe.get_value_cache().nocache = True
                            g = pe.snap(n * E + e)
                            pe.wait_ge(los.sem, los.after(n, KQ))
                            pe.wait_ge(v_here.sem, v_here.after(n, 1))

                            def maxima(c, r):
                                t, w, a0, a1 = piece(c, r)
                                u = R0[c] + r
                                pe.wait_ge(reduced.sem, reduced.after(g, u + 1 - 2))
                                q = QS[0:MR, bass.ds(e, 1), (c * CT + t) * P:(c * CT + t + 1) * P]
                                last = a1 == (c * CT + t + 1) * P
                                for o in range(a0, a1, CW):
                                    o1 = min(a1, o + CW)
                                    diag = last and o1 == a1
                                    mm = nc.tensor.matmul(pm[:, u % 2, o - a0:o1 - a0], q, KS[0:MR, o:o1], start=True, stop=not diag,
                                                          skip_group_check=True)
                                    if diag:
                                        mm = nc.tensor.matmul(pm[:, u % 2, a1 - P - a0:a1 - a0], k.identb[:], causA[:], start=False,
                                                              stop=True, skip_group_check=True)
                                mm.then_inc(scored.sem, 1)

                            def row(c):
                                pe.wait_ge(mcol.sem, mcol.after(g, 2 * c + 2))
                                pe.wait_ge(zout.sem, zout.after(g, z_row(c)))
                                for t in range(CT):
                                    mm = nc.tensor.matmul(pz[0:1, t], mc[:, c % 2, t:t + 1], k.ident[:], start=(t == 0), stop=True,
                                                          skip_group_check=True)
                                mm.then_inc(zin.sem, 1)

                            def values(c, j):
                                u = T0[c] + j
                                o = first_query(c, j)
                                pe.wait_ge(probs.sem, probs.after(g, u + 1))
                                if j < 2:
                                    pe.wait_ge(summed_out.sem, summed_out.after(g, 2 * c))
                                b = 64 * (j % 2)
                                mm = nc.tensor.matmul(po[b:b + VW, o:CW], Vc[:, j], Pr[:, u % PSL, o:CW], start=(j < 2),
                                                      stop=(j >= TU[c] - 2), skip_group_check=True)
                                mm.then_inc(used.sem, 1)

                            def scores(c, j):
                                u = T0[c] + j
                                o = first_query(c, j)
                                pe.wait_ge(probs.sem, probs.after(g, u + 1 - 2))
                                if j == 0:
                                    pe.wait_ge(zout.sem, zout.after(g, z_row(c) + 1))
                                q = QS[0:KR, bass.ds(e, 1), c * CW + o:(c + 1) * CW]
                                diag = j >= c * CT
                                mm = nc.tensor.matmul(pt[:, u % 2:u % 2 + 1, o:CW], KS[0:KR, j * P:(j + 1) * P], q, start=True,
                                                      stop=not diag, skip_group_check=True)
                                if diag:
                                    d = (j - c * CT) * P
                                    mm = nc.tensor.matmul(pt[:, u % 2, o:d + P], k.identb[:], causT[:, P - (d - o):2 * P],
                                                          start=False, stop=True, skip_group_check=True)
                                mm.then_inc(trans.sem, 1)

                            def by_token(c):
                                pe.wait_ge(summed_out.sem, summed_out.after(g, 2 * c + 2))
                                pe.wait_ge(zout.sem, zout.after(g, z_sums(c)))
                                for t in range(CT):
                                    mm = nc.tensor.matmul(pz[:, t], OT[:, t * P:(t + 1) * P], two[:], start=(t == 0), stop=True,
                                                          skip_group_check=True)
                                mm.then_inc(zin.sem, 1)

                            for r in range(RW[0]):
                                maxima(0, r)
                            row(0)
                            queue = []
                            for c in range(NC):
                                for what, i in schedule(c):
                                    if what == "r":
                                        maxima(c + 1, i)
                                    elif what == "s":
                                        by_token(i)
                                    else:
                                        scores(c, i)
                                        queue.append((c, i))
                                        if len(queue) > LAG:
                                            values(*queue.pop(0))
                                if c + 1 < NC:
                                    row(c + 1)
                            while queue:
                                values(*queue.pop(0))
                            by_token(NC - 1)
                        pe.wait_ge(used.sem, used.after(n * E + (E - 1), T0[NC]))
                        pe.sem_inc(head_done.sem, 1)

                @block.scalar
                def _(act):
                    act.sem_inc(probs.sem, 2)
                    with act.Fori(0, H) as n:
                        act.get_value_cache().nocache = True
                        for i, (s, c) in enumerate(projections()):
                            act.wait_ge(proj.sem, proj.after(n, i + 1))
                            cols = slice(c * CW, (c + 1) * CW)
                            dst = KS[0:MR, cols] if s == 0 else QS[0:MR, s - 1, cols]
                            nc.scalar.activation(dst, pt[0:MR, i % 2], ACT.Copy, scale=1.0 if s == 0 else SCALE).then_inc(his.sem, 1)
                        with act.Fori(0, E) as e:
                            act.get_value_cache().nocache = True
                            g = act.snap(n * E + e)

                            def odd_sums(c):
                                act.wait_ge(used.sem, used.after(g, T0[c + 1]))
                                act.wait_ge(zin.sem, zin.after(g, z_sums(c - 1) + 1 if c else 0))
                                nc.scalar.activation(OT[64:64 + VW], po[64:64 + VW], ACT.Copy).then_inc(summed_out.sem, 1)

                            for c in range(NC):
                                for j in range(TU[c]):
                                    u = T0[c] + j
                                    o = first_query(c, j)
                                    if c and j == LAG:
                                        odd_sums(c - 1)
                                    act.wait_ge(trans.sem, trans.after(g, u + 1))
                                    act.wait_ge(used.sem, used.after(g, u + 1 - PSL))
                                    nc.scalar.activation(Pr[:, u % PSL, o:CW], pt[:, u % 2, o:CW], ACT.Exp).then_inc(probs.sem, 1)
                            odd_sums(NC - 1)
                        act.wait_ge(e_in, n + 1)
                        nc.scalar.activation(lg[:], lg[:], ACT.Exp).then_inc(e_out, 1)

                @block.vector
                def _(dve):
                    dve.sem_inc(los.sem, 2)
                    dve.sem_inc(reduced.sem, 2)
                    dve.sem_inc(zout.sem, 1)
                    dve.sem_inc(summed_out.sem, 2)
                    with dve.Fori(0, H) as n:
                        dve.get_value_cache().nocache = True
                        for i, (s, c) in enumerate(projections()):
                            dve.wait_ge(his.sem, his.after(n, i + 1))
                            cols = slice(c * CW, (c + 1) * CW)
                            if s == 0:
                                dve.tensor_tensor(KS[HI2:LO, cols], pt[HI2:LO, i % 2], KS[HI2:LO, cols],
                                                  ALU.subtract).then_inc(los.sem, 1)
                            else:
                                q = QS[LO:MR, s - 1, cols]
                                dve.scalar_tensor_tensor(out=q, in0=pt[LO:MR, i % 2], scalar=SCALE, in1=q, op0=ALU.mult,
                                                         op1=ALU.subtract).then_inc(los.sem, 1)
                        with dve.Fori(0, E) as e:
                            dve.get_value_cache().nocache = True
                            g = dve.snap(n * E + e)

                            def maxima(c):
                                for r in range(RW[c]):
                                    t, w, a0, a1 = piece(c, r)
                                    u = R0[c] + r
                                    dve.wait_ge(scored.sem, scored.after(g, u + 1))
                                    dve.tensor_reduce(mx[:, t, w:w + 1], pm[:, u % 2, 0:a1 - a0], AX.X, ALU.max).then_inc(reduced.sem, 1)
                                m = mc[:, c % 2]
                                dve.wait_ge(reduced.sem, reduced.after(g, R0[c + 1]))
                                dve.tensor_reduce(m, mx[:, :, 0:c // 2 + 1], AX.X, ALU.max).then_inc(mcol.sem, 1)
                                dve.wait_ge(mcol.sem, mcol.after(g, 2 * c + 1))
                                dve.tensor_scalar(m, m, -M16_MAX, M16_MAX, ALU.max, ALU.min).then_inc(mcol.sem, 1)
                                dve.wait_ge(zin.sem, zin.after(g, z_row(c) + 1))
                                dve.tensor_scalar(QS[MR:KR, bass.ds(e, 1), c * CW:(c + 1) * CW],
                                                  pz[0:1].rearrange("p t n -> p (t n)").unsqueeze(1), -1.0, None,
                                                  ALU.mult).then_inc(zout.sem, 1)

                            def results(c):
                                dve.wait_ge(used.sem, used.after(g, T0[c + 1]))
                                dve.wait_ge(zin.sem, zin.after(g, z_sums(c - 1) + 1 if c else 0))
                                dve.tensor_copy(OT[0:VW], po[0:VW]).then_inc(summed_out.sem, 1)
                                dve.wait_ge(zin.sem, zin.after(g, z_sums(c) + 1))
                                dve.reciprocal(rd[:], pz[:, :, DH]).then_inc(rds, 1)
                                dve.wait_ge(rds, g * NC + (c + 1))
                                dve.tensor_tensor(ATT[:, bass.ds(e, 1), c * CT:(c + 1) * CT, :], pz[:, :, 0:DH].unsqueeze(1),
                                                  rd[:].unsqueeze(2).broadcast_to([P, CT, DH]).unsqueeze(1), ALU.mult).then_inc(zout.sem, 1)

                            maxima(0)
                            for c in range(NC):
                                if c:
                                    results(c - 1)
                                if c + 1 < NC:
                                    maxima(c + 1)
                            results(NC - 1)

                        ch = Chain(dve, steps, n, 17)
                        dve.wait_ge(zout.sem, zout.after(n * E + (E - 1), 2 * NC))
                        np_ = notpad[:, :, bass.ds(n * DH, DH)]
                        ch.link(dve.tensor_tensor(ATT[:], ATT[:], np_.unsqueeze(1).broadcast_to([P, E, NT, DH]), ALU.mult))
                        att_t = ATT[:].rearrange("p e t d -> p t e d")
                        for x in range(E):
                            w = GW[:, bass.ds(n, 1), x, :].rearrange("p a (e d) -> p a e d", e=E).broadcast_to([P, NT, E, DH])
                            ch.link(dve.tensor_tensor(tmp[:], att_t, w, ALU.mult))
                            ch.link(dve.tensor_reduce(lg[:, :, x], tmp[:], AX.XY, ALU.add))
                        ch.link(dve.tensor_tensor(lg[:], lg[:], gb[:, bass.ds(n, 1), :].broadcast_to([P, NT, E]), ALU.add))
                        emit_softmax4(dve, ch, lg[:], sm[:], e_in, e_out, n)
                        ch.link(dve.tensor_tensor(tmp[:], att_t, lg[:].unsqueeze(3).broadcast_to([P, NT, E, DH]), ALU.mult))
                        ch.link(dve.tensor_tensor(tmp[:, :, 0:2], tmp[:, :, 0:2], tmp[:, :, 2:4], ALU.add))
                        ch.link(dve.tensor_tensor(MIX[:, :, bass.ds(n * DH, DH)], tmp[:, :, 0], tmp[:, :, 1], ALU.add))
                        assert ch.k == 17, ch.k


def emit_layernorm_heads(dve, chain, src, dst, sq, st, gb, eps, std_in, std_out, turn):
    s = [st[:, i] for i in range(5)]
    v = lambda x: x.rearrange("p t (h d) -> p (t h) d", h=F_HEADS)
    src, dst, sq = v(src), v(dst), v(sq)
    shape = [P, NT * F_HEADS, F_DH]

    def wide(a):
        return a.unsqueeze(2).broadcast_to(shape)

    chain.link(dve.tensor_reduce(s[0], src, AX.X, ALU.add))
    chain.link(dve.tensor_scalar(s[0], s[0], 1.0 / F_DH, None, ALU.mult))
    chain.link(dve.tensor_tensor(dst, src, wide(s[0]), ALU.subtract))
    chain.link(dve.tensor_tensor(sq, dst, dst, ALU.mult))
    chain.link(dve.tensor_reduce(s[1], sq, AX.X, ALU.add))
    dve.tensor_scalar(s[1], s[1], 1.0 / F_DH, eps, ALU.mult, ALU.add).then_inc(std_in, 1)
    dve.wait_ge(std_out, turn + 1)
    chain.link(dve.reciprocal(s[3], s[2]))
    chain.link(dve.tensor_tensor(s[4], s[3], s[3], ALU.mult))
    chain.link(dve.tensor_tensor(s[4], s[4], s[1], ALU.mult))
    chain.link(dve.tensor_scalar(s[4], s[4], -0.5, 1.5, ALU.mult, ALU.add))
    chain.link(dve.tensor_tensor(s[3], s[3], s[4], ALU.mult))
    chain.link(dve.tensor_tensor(dst, dst, wide(s[3]), ALU.mult))
    chain.link(dve.tensor_tensor(dst, dst, gb[:, 0:1, :].broadcast_to(shape), ALU.mult))
    chain.link(dve.tensor_tensor(dst, dst, gb[:, 1:2, :].broadcast_to(shape), ALU.add))


def stage_feed_forward(k, a, SX, MIX):
    nc = k.nc
    with ExitStack() as ctx:
        FN = k.sb(ctx, "ff_FN", [P, NT, D], F32)
        B = k.sb(ctx, "ff_B", [P, NT, D], F32)
        FT = k.sb(ctx, "ff_FT", [P, N], F32)
        H1 = k.sb(ctx, "ff_H1", [P, N], F32)
        st = k.sb(ctx, "ff_st", [P, 5, NT * F_HEADS], F32)
        ln = k.sb(ctx, "ff_ln", [P, 4, F_DH], F32)
        W1 = k.sb(ctx, "ff_W1", [P, P], F32)
        W2 = k.sb(ctx, "ff_W2", [P, P], F32)
        b1 = k.sb(ctx, "ff_b1", [P, 1], F32)
        b2 = k.sb(ctx, "ff_b2", [P, F_DH], F32)
        fg = k.sb(ctx, "ff_fg", [P, F_HEADS, D], F32)
        lg = k.sb(ctx, "ff_lg", [P, NT, F_HEADS], F32)
        sm = k.sb(ctx, "ff_sm", [P, NT], F32)
        pt = k.ps(ctx, "ff_pt", [P, 2, CW])
        ph = k.ps(ctx, "ff_ph", [P, 2, CW])
        pz = k.ps(ctx, "ff_pz", [P, 2, CT, P])
        loaded, steps, std_in, std_out = k.sem("ff_loaded"), k.sem("ff_steps"), k.sem("ff_std_in"), k.sem("ff_std_out")
        normed, turned, tmoved = k.sem("ff_normed"), k.sem("ff_turned"), k.sem("ff_tmoved")
        hid, relued, masked, outp, omoved = (k.sem("ff_hid"), k.sem("ff_relued"), k.sem("ff_masked"), k.sem("ff_out"),
                                             k.sem("ff_omoved"))
        e_in, e_out = k.sem("ff_exp_in"), k.sem("ff_exp_out")
        with nc.Block() as block:
            @block.sync
            def _(sp):
                for i, name in enumerate(("ln_g", "ln_b", "fnorm_g", "fnorm_b")):
                    sp.dma_start(ln[:, i], a[name].rearrange("(o n) -> o n", o=1).broadcast_to([P, F_DH])).then_inc(loaded, 16)
                sp.dma_start(b2[:], a["fc2_b"].rearrange("(o n) -> o n", o=1).broadcast_to([P, F_DH])).then_inc(loaded, 16)
                sp.dma_start(W1[:], a["fc1B"]).then_inc(loaded, 16)
                sp.dma_start(W2[:], a["fc2B"]).then_inc(loaded, 16)
                sp.dma_start(b1[:], a["fc1b"]).then_inc(loaded, 16)
                sp.dma_start(fg[:], a["fgate_w"].rearrange("h n -> (h n)").rearrange("(o n) -> o n", o=1)
                             .broadcast_to([P, F_HEADS * D]).rearrange("p (h n) -> p h n", h=F_HEADS)).then_inc(loaded, 16)

            @block.tensor
            def _(pe):
                pe.wait_ge(normed, 1)
                pe.wait_ge(loaded, 16 * 9)
                for c in range(NC + 2):
                    if c < NC:
                        if c >= 2:
                            pe.wait_ge(tmoved, c - 1)
                        for t in range(CT):
                            mm = nc.tensor.matmul(pt[:, c % 2, t * P:(t + 1) * P], FN[:, c * CT + t], k.ident[:], start=(t == 0),
                                                  stop=True, skip_group_check=True)
                        mm.then_inc(turned, 1)
                    if 1 <= c <= NC:
                        i = c - 1
                        pe.wait_ge(tmoved, i + 1)
                        if i >= 2:
                            pe.wait_ge(relued, i - 1)
                        nc.tensor.matmul(ph[:, i % 2], W1[:], FT[:, i * CW:(i + 1) * CW], start=True, stop=True).then_inc(hid, 1)
                    if c >= 2:
                        i = c - 2
                        pe.wait_ge(masked, i + 1)
                        if i >= 2:
                            pe.wait_ge(omoved, i - 1)
                        for t in range(CT):
                            j = i * CT + t
                            mm = nc.tensor.matmul(pz[:, i % 2, t], H1[:, j * P:(j + 1) * P], W2[:], start=(t == 0), stop=True,
                                                  skip_group_check=True)
                        mm.then_inc(outp, 1)

            @block.scalar
            def _(act):
                act.wait_ge(std_in, 1)
                nc.scalar.activation(st[:, 2], st[:, 1], ACT.Sqrt).then_inc(std_out, 1)
                act.wait_ge(loaded, 16 * 9)
                for c in range(NC + 1):
                    if c < NC:
                        act.wait_ge(turned, c + 1)
                        nc.scalar.activation(FT[:, c * CW:(c + 1) * CW], pt[:, c % 2], ACT.Copy).then_inc(tmoved, 1)
                    if c >= 1:
                        i = c - 1
                        act.wait_ge(hid, i + 1)
                        nc.scalar.activation(H1[:, i * CW:(i + 1) * CW], ph[:, i % 2], ACT.Relu, bias=b1[:]).then_inc(relued, 1)
                act.wait_ge(std_in, 2)
                nc.scalar.activation(st[:, 2], st[:, 1], ACT.Sqrt).then_inc(std_out, 1)
                act.wait_ge(e_in, 1)
                nc.scalar.activation(lg[:], lg[:], ACT.Exp).then_inc(e_out, 1)

            @block.vector
            def _(dve):
                ch = Chain(dve, steps)
                dve.wait_ge(loaded, 16 * 9)
                ch.link(dve.tensor_tensor(MIX[:], MIX[:], SX[:], ALU.add))
                emit_layernorm_heads(dve, ch, MIX[:], FN[:], B[:], st, ln[:, 0:2], 1e-8, std_in, std_out, 0)
                dve.sem_inc(normed, 1)
                for c in range(NC + 1):
                    if c < NC:
                        cols = slice(c * CW, (c + 1) * CW)
                        dve.wait_ge(relued, c + 1)
                        dve.scalar_tensor_tensor(out=H1[:, cols], in0=FT[:, cols], scalar=0.0, in1=H1[:, cols],
                                                 op0=ALU.not_equal, op1=ALU.mult).then_inc(masked, 1)
                    if c >= 1:
                        i = c - 1
                        dve.wait_ge(outp, i + 1)
                        v = lambda x: x.rearrange("p t (h d) -> p t h d", h=F_HEADS)
                        dve.tensor_tensor(v(B[:, i * CT:(i + 1) * CT]), v(pz[:, i % 2]),
                                          b2[:].unsqueeze(1).unsqueeze(1).broadcast_to([P, CT, F_HEADS, F_DH]),
                                          ALU.add).then_inc(omoved, 1)
                dve.wait_ge(omoved, NC)
                ch.link(dve.scalar_tensor_tensor(out=B[:], in0=FN[:], scalar=0.0, in1=B[:], op0=ALU.not_equal, op1=ALU.mult))
                ch.link(dve.tensor_tensor(B[:], B[:], FN[:], ALU.add))
                emit_layernorm_heads(dve, ch, B[:], FN[:], MIX[:], st, ln[:, 2:4], 1e-8, std_in, std_out, 1)
                for h in range(F_HEADS):
                    ch.link(dve.tensor_tensor(B[:], FN[:], fg[:, h:h + 1].broadcast_to([P, NT, D]), ALU.mult))
                    ch.link(dve.tensor_reduce(lg[:, :, h], B[:], AX.X, ALU.add))
                emit_softmax4(dve, ch, lg[:], sm[:], e_in, e_out)
                v = lambda x: x.rearrange("p t (h d) -> p (t h) d", h=F_HEADS)
                ch.link(dve.tensor_tensor(v(B[:]), v(FN[:]), lg[:].rearrange("p t h -> p (t h)").unsqueeze(2)
                                          .broadcast_to([P, NT * F_HEADS, F_DH]), ALU.mult))
                ch.link(dve.tensor_tensor(k.X[:], k.X[:], B[:], ALU.add))


def lay_out(inputs):
    import numpy as np
    get = {n: np.ascontiguousarray(np.asarray(v)) for n, v in inputs.items()}
    r = {"x": get["x"], "adj": get["adj"]}
    for n in ("inlayer2", "W", "b", "w1", "b1", "w2", "b2"):
        r[n] = get["L0_gnn_" + n]
    for n in ("sW1", "sb1", "sW2", "sb2", "sW3", "sb3", "eW1", "eW2", "eW3", "eb3", "gW", "gb"):
        r[n] = get["L0_ffn_" + n]
    for n in ("eb1", "eb2"):
        r[n + "T"] = np.ascontiguousarray(get["L0_ffn_" + n].T)
    for n in ("Wq", "Wk", "Wv", "weightr", "weightd", "bias"):
        r[n] = get["L1_gnn_" + n]
    f = {n[7:]: v for n, v in get.items() if n.startswith("L1_ffn_")}
    r["hlT"] = np.ascontiguousarray(f["hl_w"].reshape(D, D).T)
    r["hlb"] = f["hl_b"].reshape(D, 1)
    wqk = np.zeros((D, F_HEADS, 1 + F_EXP, 3 * F_DH), np.float32)
    for name in ("wvB", "fc1B", "fc2B"):
        r[name] = np.zeros((D, D), np.float32)
    for h in range(F_HEADS):
        rows = slice(h * F_DH, (h + 1) * F_DH)
        for i in range(3):
            cols = slice(i * F_DH, (i + 1) * F_DH)
            wqk[rows, h, 0, cols] = f["wk"][h].T
            for e in range(F_EXP):
                wqk[rows, h, 1 + e, cols] = f["wq"][h, e].T
        r["wvB"][rows, rows] = f["wv"][h].T
        r["fc1B"][rows, rows] = f["fc1_w"].T
        r["fc2B"][rows, rows] = f["fc2_w"].T
    r["wqk"] = wqk
    r["fc1b"] = np.tile(f["fc1_b"], F_HEADS).reshape(D, 1)
    for n in ("gate_w", "gate_b", "ln_g", "ln_b", "fnorm_g", "fnorm_b", "fc2_b", "fgate_w"):
        r[n] = f[n]
    return r


def kernel(**inputs):
    import concourse.bacc as _bacc
    from concourse import mybir as _mybir
    from concourse.bass_utils import run_bass_kernel_spmd as _run

    nc = _bacc.Bacc("TRN2", target_bir_lowering=False, num_devices=1)
    arrays, args = {}, {}
    for name, arr in lay_out(inputs).items():
        arrays[f"in_{name}"] = arr
        args[name] = nc.dram_tensor(f"in_{name}", arr.shape, _mybir.dt.from_np(arr.dtype), kind="ExternalInput").ap()
    out = nc.dram_tensor("out_x", (N, D), F32, kind="ExternalOutput").ap()
    build(nc, args, out)
    res = _run(nc, [arrays], core_ids=[0])
    return res.results[0]["out_x"]
```

```python
from contextlib import ExitStack

import concourse.bass as bass
from concourse import mybir

ALU = mybir.AluOpType
ACT = mybir.ActivationFunctionType
AX = mybir.AxisListType
F32 = mybir.dt.float32
BF16 = mybir.dt.bfloat16
F16 = mybir.dt.float16
I32 = mybir.dt.int32

P = 128
N = 4096
D = 128
NT = N // P
CT = 4
CW = CT * P
NC = N // CW
HALF = N // 2
SLOPE = 0.01
BIG = 2.0 ** 60
FLOOR = -(2.0 ** 40)
M16_MAX = 60000.0
G_HEADS, G_DH = 2, 64
F_HEADS, F_EXP, F_DH = 4, 4, 32
S_HIDDEN, E_HIDDEN, N_EXP = 128, 64, 4


class Count:

    def __init__(self, sem, per=0, credit=0):
        self.sem, self.per, self.credit = sem, per, credit

    def after(self, turn, k):
        return turn * self.per + (self.credit + k)


class Chain:

    def __init__(self, eng, sem, turn=0, per=0):
        self.eng, self.sem, self.base, self.k, self.per = eng, sem, turn * per, 0, per

    def link(self, ins):
        self.k += 1
        ins.then_inc(self.sem, 1)
        self.eng.wait_ge(self.sem, self.base + self.k)


class Core:

    def __init__(self, nc, ctx):
        self.nc, self.ctx = nc, ctx
        self.X = self.sb(ctx, "X", [P, NT, D], F32)
        self.ident = self.sb(ctx, "ident", [P, P], F32)
        self.identb = self.sb(ctx, "identb", [P, P], BF16)
        self.negbig = self.sb(ctx, "negbig", [P, P], BF16)
        self.ones = self.sb(ctx, "ones", [P, P], F32)

    def sb(self, ctx, name, shape, dt):
        return ctx.enter_context(self.nc.sbuf_tensor(name, shape, dt))

    def ps(self, ctx, name, shape, dt=F32):
        return ctx.enter_context(self.nc.psum_tensor(name, shape, dt))

    def sem(self, name):
        return self.ctx.enter_context(self.nc.semaphore(name))


def stage_constants(k, x):
    nc = k.nc
    x_in, zeroed, made = k.sem("x_in"), k.sem("const_zeroed"), k.sem("const_made")
    with nc.Block() as block:
        @block.sync
        def _(sp):
            sp.dma_start(k.X[:], x.rearrange("(t p) f -> p t f", p=P)).then_inc(x_in, 16)
            sp.wait_ge(x_in, 16)

        @block.gpsimd
        def _(pool):
            pool.memset(k.ones[:], 1.0).then_inc(made, 1)
            for m in (k.ident, k.identb, k.negbig):
                pool.memset(m[:], 0.0).then_inc(zeroed, 1)
            pool.wait_ge(zeroed, 3)
            for m, fill in ((k.ident, 1.0), (k.identb, 1.0), (k.negbig, -BIG)):
                pool.affine_select(out=m[:], in_=m[:], compare_op=ALU.not_equal, fill=fill, base=0,
                                   pattern=[[-1, P]], channel_multiplier=1).then_inc(made, 1)


def emit_layernorm(dve, chain, src, dst, sq, st, width, eps, std_in, std_out):
    shape = list(src.shape)
    s = [st[:, i] for i in range(5)]

    def wide(a):
        return a.unsqueeze(len(shape) - 1).broadcast_to(shape)

    chain.link(dve.tensor_reduce(s[0], src, AX.X, ALU.add))
    chain.link(dve.tensor_scalar(s[0], s[0], 1.0 / width, None, ALU.mult))
    chain.link(dve.tensor_tensor(dst, src, wide(s[0]), ALU.subtract))
    chain.link(dve.tensor_tensor(sq, dst, dst, ALU.mult))
    chain.link(dve.tensor_reduce(s[1], sq, AX.X, ALU.add))
    dve.tensor_scalar(s[1], s[1], 1.0 / width, eps, ALU.mult, ALU.add).then_inc(std_in, 1)
    dve.wait_ge(std_out, 1)
    chain.link(dve.reciprocal(s[3], s[2]))
    chain.link(dve.tensor_tensor(s[4], s[3], s[3], ALU.mult))
    chain.link(dve.tensor_tensor(s[4], s[4], s[1], ALU.mult))
    chain.link(dve.tensor_scalar(s[4], s[4], -0.5, 1.5, ALU.mult, ALU.add))
    chain.link(dve.tensor_tensor(s[3], s[3], s[4], ALU.mult))
    chain.link(dve.tensor_tensor(dst, dst, wide(s[3]), ALU.mult))


def stage_layernorm(k, tag, Y, YT=None):
    nc = k.nc
    with ExitStack() as ctx:
        sq = k.sb(ctx, f"{tag}_sq", [P, NT, D], F32)
        st = k.sb(ctx, f"{tag}_st", [P, 5, NT], F32)
        pt = k.ps(ctx, f"{tag}_pt", [P, 2, CW])
        steps, std_in, std_out = k.sem(f"{tag}_steps"), k.sem(f"{tag}_var"), k.sem(f"{tag}_std")
        y_done, turned, moved = k.sem(f"{tag}_y_done"), k.sem(f"{tag}_turned"), k.sem(f"{tag}_moved")
        with nc.Block() as block:
            @block.vector
            def _(dve):
                emit_layernorm(dve, Chain(dve, steps), k.X[:], Y, sq[:], st, D, 1e-5, std_in, std_out)
                dve.sem_inc(y_done, 1)

            @block.scalar
            def _(act):
                act.wait_ge(std_in, 1)
                nc.scalar.activation(st[:, 2], st[:, 1], ACT.Sqrt).then_inc(std_out, 1)
                if YT is not None:
                    for c in range(NC):
                        act.wait_ge(turned, c + 1)
                        nc.scalar.activation(YT[:, c * CW:(c + 1) * CW], pt[:, c % 2], ACT.Copy).then_inc(moved, 1)

            if YT is not None:
                @block.tensor
                def _(pe):
                    pe.wait_ge(y_done, 1)
                    for c in range(NC):
                        if c >= 2:
                            pe.wait_ge(moved, c - 1)
                        for t in range(CT):
                            mm = nc.tensor.matmul(pt[:, c % 2, t * P:(t + 1) * P], Y[:, c * CT + t, :],
                                                  k.ident[:], start=(t == 0), stop=True, skip_group_check=True)
                        mm.then_inc(turned, 1)


def stage_gat_vectors(k, g, a):
    nc = k.nc
    with ExitStack() as ctx:
        in2 = k.sb(ctx, "in2", [P, NT, D], F32)
        sq = k.sb(ctx, "in2_sq", [P, NT, D], F32)
        W = k.sb(ctx, "gat_W", [P, D], F32)
        cols = k.sb(ctx, "gat_cols", [P, 5], F32)
        Ab = k.sb(ctx, "gat_Ab", [P, 2, D], F32)
        kap = k.sb(ctx, "gat_kap", [P, 2], F32)
        pA = k.ps(ctx, "gat_pA", [P, 2, D])
        pk = k.ps(ctx, "gat_pk", [P, 2])
        pF = k.ps(ctx, "gat_pF", [P, 2, CW])
        pS = k.ps(ctx, "gat_pS", [P, D + 1])
        loaded, steps, prod = k.sem("gatv_loaded"), k.sem("gatv_steps"), k.sem("gatv_A_done")
        f_done, rows, moved, summed = k.sem("gatv_f"), k.sem("gatv_rows"), k.sem("gatv_moved"), k.sem("gatv_sum")
        sv_done, filled = k.sem("gatv_sv"), k.sem("gatv_filled")
        with nc.Block() as block:
            @block.sync
            def _(sp):
                sp.dma_start(W[:], a["W"]).then_inc(loaded, 16)
                for i, v in enumerate((a["w1"], a["w2"], a["b"])):
                    sp.dma_start(cols[:, i:i + 1], v.rearrange("(p o) -> p o", o=1)).then_inc(loaded, 16)
                for i, v in enumerate((a["b1"], a["b2"])):
                    sp.dma_start(cols[:, 3 + i:4 + i], v.rearrange("(o p) -> o p", o=1).broadcast_to([P, 1])).then_inc(loaded, 16)
                sp.dma_start(in2[:], a["inlayer2"].rearrange("(t p) f -> p t f", p=P)).then_inc(loaded, 16)

            @block.gpsimd
            def _(pool):
                pool.memset(g.row0[:], 0.0).then_inc(filled, 1)
                pool.wait_ge(filled, 1)
                pool.memset(g.row0[0:1, :], 1.0).then_inc(filled, 1)
                pool.memset(g.V[:, :, D:D + 1], 1.0).then_inc(filled, 1)

            @block.tensor
            def _(pe):
                pe.wait_ge(loaded, 16 * 7)
                for i in range(2):
                    w = cols[:, i:i + 1].broadcast_to([P, P])
                    nc.tensor.matmul(pA[:, i], w, W[:], start=(i == 0), stop=True, skip_group_check=True)
                for i in range(2):
                    w = cols[:, i:i + 1].broadcast_to([P, P])
                    mm = nc.tensor.matmul(pk[:, i:i + 1], w, cols[:, 2:3], start=(i == 0), stop=True, skip_group_check=True)
                mm.then_inc(prod, 1)
                pe.wait_ge(filled, 3)
                for t in range(NT):
                    mm = nc.tensor.matmul(pS[:], k.ones[:], g.V[:, t, :], start=(t == 0), stop=(t == NT - 1))
                mm.then_inc(summed, 1)
                for i in range(2):
                    pe.wait_ge(f_done, i + 1)
                    for c in range(NC):
                        n = i * NC + c
                        if n >= 2:
                            pe.wait_ge(moved, n - 1)
                        for t in range(CT):
                            f = g.fcol[:, i, c * CT + t:c * CT + t + 1].broadcast_to([P, P])
                            mm = nc.tensor.matmul(pF[:, n % 2, t * P:(t + 1) * P], f, k.ident[:],
                                                  start=(t == 0), stop=True, skip_group_check=True)
                        mm.then_inc(rows, 1)

            @block.scalar
            def _(act):
                for i, dst in enumerate((g.f1row, g.f2row)):
                    for c in range(NC):
                        n = i * NC + c
                        act.wait_ge(rows, n + 1)
                        nc.scalar.activation(dst[:, c * CW:(c + 1) * CW], pF[:, n % 2], ACT.Copy).then_inc(moved, 1)

            @block.vector
            def _(dve):
                ch = Chain(dve, steps)
                dve.wait_ge(prod, 1)
                ch.link(dve.tensor_copy(Ab[:], pA[:]))
                ch.link(dve.tensor_tensor(kap[:], pk[:], cols[:, 3:5], ALU.add))
                dve.wait_ge(loaded, 16 * 7)
                for i in range(2):
                    w = Ab[:, i:i + 1, :].broadcast_to([P, NT, D])
                    ch.link(dve.tensor_tensor(sq[:], in2[:], w, ALU.mult))
                    ch.link(dve.tensor_reduce(g.fcol[:, i], sq[:], AX.X, ALU.add))
                    dve.tensor_scalar(g.fcol[:, i], g.fcol[:, i], kap[:, i:i + 1], None, ALU.add).then_inc(f_done, 1)
                dve.wait_ge(f_done, 2)
                ch.link(dve.tensor_scalar(g.f2s[:, 0], g.fcol[:, 1], SLOPE, None, ALU.mult))
                ch.link(dve.tensor_scalar(g.f2s[:, 1], g.fcol[:, 1], 1 - SLOPE, None, ALU.mult))
                dve.wait_ge(summed, 1)
                dve.tensor_copy(g.sumV[:], pS[:]).then_inc(sv_done, 1)


def stage_gat(k, g, adj):
    nc = k.nc
    QW = N // 4
    QN = 4 * CT
    AS = 4
    TS = 2
    LS = 4
    PSL = 4
    LAG = 2
    with ExitStack() as ctx:
        A = k.sb(ctx, "gat_adj", [P, AS, QW], I32)
        NM = k.sb(ctx, "gat_nm", [P, 2, CT, N], BF16)
        L = k.sb(ctx, "gat_logits", [P, LS, CW], F32)
        Pr = k.sb(ctx, "gat_probs", [P, PSL, CW], F32)
        f1c = k.sb(ctx, "gat_f1c", [P, CW], F32)
        mx = k.sb(ctx, "gat_mx", [P, CT, 4], F32)
        m4 = k.sb(ctx, "gat_m4", [P, 4, CT], F32)
        ecol = k.sb(ctx, "gat_ecol", [P, CT], F32)
        erow = k.sb(ctx, "gat_erow", [1, CW], F32)
        Mrow = k.sb(ctx, "gat_Mrow", [P, CW], BF16)
        rd = k.sb(ctx, "gat_rd", [P, CT], F32)
        pm = k.ps(ctx, "gat_pm", [P, 2, QW])
        pt = k.ps(ctx, "gat_pt", [P, TS, CW])
        po = k.ps(ctx, "gat_po", [P, CT, 2 * P])

        adj_in = [k.sem(f"gat_adj_in{s}") for s in range(AS)]
        converted = Count(k.sem("gat_converted"), QN, AS)
        biased = Count(k.sem("gat_biased"), QN + 2)
        reduced = Count(k.sem("gat_reduced"), QN + 2, 2)
        mcol = Count(k.sem("gat_mcol"), 1)
        steps = k.sem("gat_steps")
        f1_here = Count(k.sem("gat_f1_here"), 1)
        masked = Count(k.sem("gat_masked"), NT)
        logits = Count(k.sem("gat_logits_done"), NT)
        summed = Count(k.sem("gat_added"), NT, TS)
        probs = Count(k.sem("gat_probs_done"), NT, LS)
        used = Count(k.sem("gat_probs_used"), NT, PSL)
        out_done = Count(k.sem("gat_out"), 1)
        out_moved = Count(k.sem("gat_out_moved"), CT, CT)

        with nc.Block() as block:
            @block.sync
            def _(sp):
                with sp.Fori(0, NC) as c:
                    for q in range(QN):
                        t, w, s = q // 4, q % 4, q % AS
                        sp.wait_ge(converted.sem, converted.after(c, q + 1 - AS))
                        sp.dma_start(A[:, s], adj[bass.ds((c * CT + t) * P, P), w * QW:(w + 1) * QW]).then_inc(adj_in[s], 16)

            @block.vector
            def _(dve):
                dve.sem_inc(converted.sem, AS)
                dve.sem_inc(reduced.sem, 2)
                dve.sem_inc(summed.sem, TS)
                dve.sem_inc(out_moved.sem, CT)

                def convert(c, q):
                    t, w, s = q // 4, q % 4, q % AS
                    dve.wait_ge(adj_in[s], 16 * (c * (QN // AS) + q // AS + 1))
                    dve.tensor_scalar(NM[:, bass.ds(c % 2, 1), t, w * QW:(w + 1) * QW], A[:, s:s + 1], 0.0, None,
                                      ALU.is_le).then_inc(converted.sem, 1)

                def chunk(c, convert_next):
                    ch = Chain(dve, steps, c, 9)
                    for q in range(QN):
                        dve.wait_ge(biased.sem, biased.after(c, q + 1))
                        dve.tensor_reduce(mx[:, q // 4, q % 4:q % 4 + 1], pm[:, q % 2], AX.X, ALU.max).then_inc(reduced.sem, 1)
                    dve.wait_ge(reduced.sem, reduced.after(c, QN))
                    dve.tensor_copy(f1c[:].unsqueeze(1), g.f1row[:, bass.ds(c * CW, CW)].unsqueeze(1)).then_inc(f1_here.sem, 1)
                    F, z, M, Mn = (m4[:, i] for i in range(4))
                    ch.link(dve.tensor_reduce(F, mx[:], AX.X, ALU.max))
                    ch.link(dve.tensor_scalar(ecol[:], F, -BIG / 2, None, ALU.is_lt))
                    ch.link(dve.tensor_scalar(F, F, FLOOR, None, ALU.max))
                    ch.link(dve.tensor_tensor(z, F, g.fcol[:, 0, bass.ds(c * CT, CT)], ALU.add))
                    ch.link(dve.tensor_scalar(M, z, SLOPE, None, ALU.mult))
                    ch.link(dve.tensor_tensor(M, M, z, ALU.max))
                    dve.scalar_tensor_tensor(out=Mn, in0=g.fcol[:, 0, bass.ds(c * CT, CT)], scalar=SLOPE, in1=M,
                                             op0=ALU.mult, op1=ALU.subtract).then_inc(mcol.sem, 1)
                    dve.wait_ge(biased.sem, biased.after(c, QN + 1))
                    dve.tensor_copy(Mrow[:], pm[:, 0, 0:CW]).then_inc(reduced.sem, 1)
                    dve.wait_ge(biased.sem, biased.after(c, QN + 2))
                    ch.link(dve.tensor_copy(erow[:], pm[0:1, 1, 0:CW]))
                    ch.link(dve.tensor_copy(g.Erow[0:1, bass.ds(c * CW, CW)], erow[:]))
                    dve.sem_inc(reduced.sem, 1)
                    for j in range(NT):
                        s = j % TS
                        dve.wait_ge(masked.sem, masked.after(c, j + 1))
                        dve.wait_ge(logits.sem, logits.after(c, j + 1))
                        dve.tensor_tensor(L[:, j % LS], pt[:, s], L[:, j % LS], ALU.add).then_inc(summed.sem, 1)
                        if convert_next and j % 2 == 1:
                            convert(c + 1, j // 2)
                    dve.wait_ge(out_done.sem, out_done.after(c, 1))
                    dve.reciprocal(rd[:], po[:, :, D]).then_inc(steps, 1)
                    return ch

                def finish(c):
                    dve.wait_ge(steps, (c + 1) * 9)
                    for t in range(CT):
                        xt = k.X[:, bass.ds(c * CT + t, 1), :]
                        dve.scalar_tensor_tensor(out=xt, in0=po[:, t:t + 1, 0:D], scalar=rd[:, t:t + 1], in1=xt,
                                                 op0=ALU.mult, op1=ALU.add).then_inc(out_moved.sem, 1)

                for q in range(QN):
                    convert(0, q)
                with dve.Fori(0, NC - 1) as c:
                    chunk(c, True)
                    finish(c)
                chunk(NC - 1, False)
                finish(NC - 1)

            @block.scalar
            def _(act):
                act.sem_inc(probs.sem, LS)
                with act.Fori(0, NC) as c:
                    def logit(j):
                        act.wait_ge(probs.sem, probs.after(c, j + 1 - LS))
                        if j == 0:
                            act.wait_ge(f1_here.sem, f1_here.after(c, 1))
                        nc.scalar.activation(L[:, j % LS], f1c[:], ACT.Relu, bias=g.f2s[:, 1, j:j + 1],
                                             scale=1 - SLOPE).then_inc(logits.sem, 1)

                    logit(0)
                    for j in range(NT):
                        if j + 1 < NT:
                            logit(j + 1)
                        act.wait_ge(summed.sem, summed.after(c, j + 1))
                        act.wait_ge(used.sem, used.after(c, j + 1 - PSL))
                        nc.scalar.activation(Pr[:, j % PSL], L[:, j % LS], ACT.Exp,
                                             bias=g.f2s[:, 0, j:j + 1]).then_inc(probs.sem, 1)

            @block.tensor
            def _(pe):
                pe.sem_inc(used.sem, PSL)
                with pe.Fori(0, NC) as c:
                    par = c % 2
                    for q in range(QN):
                        t, w = q // 4, q % 4
                        pe.wait_ge(converted.sem, converted.after(c, q + 1))
                        pe.wait_ge(reduced.sem, reduced.after(c, q + 1 - 2))
                        for h in range(2):
                            o = w * QW + h * CW
                            dst = pm[:, q % 2, h * CW:(h + 1) * CW]
                            nc.tensor.matmul(dst, k.negbig[:], NM[:, bass.ds(par, 1), t, o:o + CW], start=True, stop=False)
                            mm = nc.tensor.matmul(dst, g.row0[:], g.f2row[:, o:o + CW], start=False, stop=True)
                        mm.then_inc(biased.sem, 1)
                    pe.wait_ge(mcol.sem, mcol.after(c, 1))
                    pe.wait_ge(reduced.sem, reduced.after(c, QN))
                    for t in range(CT):
                        mm = nc.tensor.matmul(pm[:, 0, t * P:(t + 1) * P], m4[:, 3, t:t + 1].broadcast_to([P, P]),
                                              k.ident[:], start=(t == 0), stop=True, skip_group_check=True)
                    mm.then_inc(biased.sem, 1)
                    for t in range(CT):
                        mm = nc.tensor.matmul(pm[0:1, 1, t * P:(t + 1) * P], ecol[:, t:t + 1],
                                              k.ident[:], start=(t == 0), stop=True, skip_group_check=True)
                    mm.then_inc(biased.sem, 1)
                    pe.wait_ge(reduced.sem, reduced.after(c, QN + 2))
                    for j in range(NT + LAG):
                        if j < NT:
                            pe.wait_ge(summed.sem, summed.after(c, j + 1 - TS))
                            nc.tensor.matmul(pt[:, j % TS], g.row0[:], Mrow[:], start=True, stop=False, skip_group_check=True)
                            for t in range(CT):
                                mm = nc.tensor.matmul(pt[:, j % TS, t * P:(t + 1) * P],
                                                      NM[:, bass.ds(par, 1), t, j * P:(j + 1) * P], k.negbig[:],
                                                      start=False, stop=(t == CT - 1), skip_group_check=True)
                            mm.then_inc(masked.sem, 1)
                        i = j - LAG
                        if i < 0:
                            continue
                        pe.wait_ge(probs.sem, probs.after(c, i + 1))
                        if i == 0:
                            pe.wait_ge(out_moved.sem, out_moved.after(c, 0))
                        for t in range(CT):
                            mm = nc.tensor.matmul(po[:, t, 0:D + 1], Pr[:, i % PSL, t * P:(t + 1) * P], g.V[:, i, :],
                                                  start=(i == 0 and t % 2 == 0), stop=False, skip_group_check=True)
                        mm.then_inc(used.sem, 1)
                    for t in range(CT):
                        mm = nc.tensor.matmul(po[:, t, 0:D + 1], erow[0:1, t * P:(t + 1) * P], g.sumV[0:1, :],
                                              start=False, stop=True, skip_group_check=True)
                    mm.then_inc(out_done.sem, 1)


class Gat:
    def __init__(self, k, ctx):
        self.V = k.sb(ctx, "gat_V", [P, NT, D + 1], F32)
        self.fcol = k.sb(ctx, "gat_fcol", [P, 2, NT], F32)
        self.f1row = k.sb(ctx, "gat_f1row", [P, N], F32)
        self.f2row = k.sb(ctx, "gat_f2row", [P, N], BF16)
        self.row0 = k.sb(ctx, "gat_row0", [P, P], BF16)
        self.sumV = k.sb(ctx, "gat_sumV", [P, D + 1], F32)
        self.f2s = k.sb(ctx, "gat_f2s", [P, 2, NT], F32)
        self.Erow = k.Erow


def build(nc, a, out):
    with ExitStack() as top:
        k = Core(nc, top)
        k.Erow = k.sb(top, "Erow", [1, N], BF16)
        stage_constants(k, a["x"])
        with ExitStack() as ctx:
            g = Gat(k, ctx)
            stage_layernorm(k, "ln0", g.V[:, :, 0:D])
            stage_gat_vectors(k, g, a)
            stage_gat(k, g, a["adj"])
        with ExitStack() as ctx:
            Y = k.sb(ctx, "moe_Y", [P, NT, D], F32)
            YT = k.sb(ctx, "moe_YT", [P, N], F32)
            stage_layernorm(k, "ln1", Y[:], YT)
            stage_moe(k, a, Y, YT)
        stage_graph_attention(k, a)
        with ExitStack() as ctx:
            SX = k.sb(ctx, "sa_SX", [P, NT, D], F32)
            MIX = k.sb(ctx, "sa_MIX", [P, NT, D], F32)
            stage_self_attention(k, a, (SX, MIX))
            stage_feed_forward(k, a, SX, MIX)
        stored = k.sem("stored")
        with nc.Block() as block:
            @block.sync
            def _(sp):
                sp.dma_start(out.rearrange("(t p) f -> p t f", p=P), k.X[:]).then_inc(stored, 16)
                sp.wait_ge(stored, 16)


def emit_softmax4(dve, chain, lg, tmp, exp_in, exp_out, turn=0):
    def wide(a):
        return a.unsqueeze(2).broadcast_to([P, NT, 4])

    chain.link(dve.tensor_reduce(tmp, lg, AX.X, ALU.max))
    dve.tensor_tensor(lg, lg, wide(tmp), ALU.subtract).then_inc(exp_in, 1)
    dve.wait_ge(exp_out, turn + 1)
    chain.link(dve.tensor_reduce(tmp, lg, AX.X, ALU.add))
    chain.link(dve.reciprocal(tmp, tmp))
    chain.link(dve.tensor_tensor(lg, lg, wide(tmp), ALU.mult))


def stage_moe(k, a, Y, YT):
    nc = k.nc
    U = 1 + N_EXP
    with ExitStack() as ctx:
        W1 = k.sb(ctx, "moe_W1", [P, U, P], F32)
        W2 = k.sb(ctx, "moe_W2", [P, U, P], F32)
        W3 = k.sb(ctx, "moe_W3", [P, U, P], F32)
        b1 = k.sb(ctx, "moe_b1", [P, U], F32)
        b2 = k.sb(ctx, "moe_b2", [P, U], F32)
        b3 = k.sb(ctx, "moe_b3", [P, D], F32)
        gW = k.sb(ctx, "moe_gW", [P, N_EXP], F32)
        gb = k.sb(ctx, "moe_gb", [P, N_EXP], F32)
        G = k.sb(ctx, "moe_G", [P, NT, N_EXP], F32)
        sel = k.sb(ctx, "moe_sel", [P, 2, NT, N_EXP], F32)
        coef = k.sb(ctx, "moe_coef", [P, NT, N_EXP], F32)
        sm = k.sb(ctx, "moe_small", [P, 6, NT], F32)
        H1 = k.sb(ctx, "moe_H1", [P, 2, CW], F32)
        H2s = k.sb(ctx, "moe_H2s", [P, CW], F32)
        H2 = k.sb(ctx, "moe_H2", [P, 2, CW], F32)
        cc = k.sb(ctx, "moe_cc", [P, CT, N_EXP], F32)
        p1 = k.ps(ctx, "moe_p1", [P, 2, CW])
        p2 = k.ps(ctx, "moe_p2", [P, 2, CW])
        p3 = k.ps(ctx, "moe_p3", [P, 2, CT, P])
        pg = k.ps(ctx, "moe_pg", [P, NT, N_EXP])
        loaded, steps, gated = k.sem("moe_loaded"), k.sem("moe_steps"), k.sem("moe_gated")
        exp_in, exp_out = k.sem("moe_exp_in"), k.sem("moe_exp_out")
        w_in, w_out, coef_ok = k.sem("moe_w_in"), k.sem("moe_w_out"), k.sem("moe_coef_done")
        ones_ok = k.sem("moe_ones")
        h1 = Count(k.sem("moe_h1"), U, 2)
        r1 = Count(k.sem("moe_r1"), U, 2)
        h2 = Count(k.sem("moe_h2"), U, 2)
        r2 = Count(k.sem("moe_r2"), U, 2)
        h3 = Count(k.sem("moe_h3"), U, 2)
        added = Count(k.sem("moe_added"), U, 2)
        steps2 = k.sem("moe_steps2")
        n_loads = 7 * 1 + 7

        def last_user(u):
            return {0: 0, 1: -1}.get(u, u - 1)

        def hidden2(u):
            return H2s[:] if u == 0 else H2[:, u % 2]

        def rows(u):
            return S_HIDDEN if u == 0 else E_HIDDEN + 1

        with nc.Block() as block:
            @block.sync
            def _(sp):
                sp.dma_start(W1[:, 0], a["sW1"]).then_inc(loaded, 16)
                sp.dma_start(W1[:, 1:U], a["eW1"].rearrange("e i o -> i e o")).then_inc(loaded, 16)
                sp.dma_start(W2[:, 0], a["sW2"]).then_inc(loaded, 16)
                sp.dma_start(W2[:, 1:U, 0:E_HIDDEN], a["eW2"].rearrange("e i o -> i e o")).then_inc(loaded, 16)
                sp.dma_start(W3[:, 0], a["sW3"]).then_inc(loaded, 16)
                sp.dma_start(W3[0:E_HIDDEN, 1:U], a["eW3"].rearrange("e i o -> i e o")).then_inc(loaded, 16)
                sp.dma_start(W3[E_HIDDEN:E_HIDDEN + 1, 1:U], a["eb3"].rearrange("(a e) o -> a e o", a=1)).then_inc(loaded, 16)
                sp.dma_start(b1[:, 0:1], a["sb1"].rearrange("(p o) -> p o", o=1)).then_inc(loaded, 16)
                sp.dma_start(b1[:, 1:U], a["eb1T"]).then_inc(loaded, 16)
                sp.dma_start(b2[:, 0:1], a["sb2"].rearrange("(p o) -> p o", o=1)).then_inc(loaded, 16)
                sp.dma_start(b2[0:E_HIDDEN, 1:U], a["eb2T"]).then_inc(loaded, 16)
                sp.dma_start(b3[:], a["sb3"].rearrange("(o n) -> o n", o=1).broadcast_to([P, D])).then_inc(loaded, 16)
                sp.dma_start(gW[:], a["gW"]).then_inc(loaded, 16)
                sp.dma_start(gb[:], a["gb"].rearrange("(o n) -> o n", o=1).broadcast_to([P, N_EXP])).then_inc(loaded, 16)

            @block.gpsimd
            def _(pool):
                pool.memset(H2[:], 1.0).then_inc(ones_ok, 1)

            @block.tensor
            def _(pe):
                pe.wait_ge(loaded, 16 * n_loads)
                for t in range(NT):
                    mm = nc.tensor.matmul(pg[:, t], YT[:, t * P:(t + 1) * P], gW[:], start=(t == 0), stop=True,
                                          skip_group_check=True)
                mm.then_inc(gated, 1)
                pe.sem_inc(h1.sem, 2)
                pe.sem_inc(h2.sem, 2)
                pe.sem_inc(h3.sem, 2)
                pe.wait_ge(ones_ok, 1)

                with pe.Fori(0, NC) as c:
                    def first(u):
                        pe.wait_ge(r1.sem, r1.after(c, last_user(u)))
                        nc.tensor.matmul(p1[:, u % 2].unsqueeze(1), W1[:, u], YT[:, bass.ds(c * CW, CW)].unsqueeze(1),
                                         start=True, stop=True).then_inc(h1.sem, 1)

                    def second(u):
                        m = S_HIDDEN if u == 0 else E_HIDDEN
                        pe.wait_ge(r1.sem, r1.after(c, u + 1))
                        pe.wait_ge(r2.sem, r2.after(c, last_user(u)))
                        nc.tensor.matmul(p2[0:m, u % 2], W2[:, u, 0:m], H1[:, u % 2], start=True, stop=True).then_inc(h2.sem, 1)

                    def third(u):
                        pe.wait_ge(r2.sem, r2.after(c, u + 1))
                        pe.wait_ge(added.sem, added.after(c, last_user(u)))
                        for t in range(CT):
                            mm = nc.tensor.matmul(p3[:, u % 2, t], hidden2(u)[0:rows(u), t * P:(t + 1) * P],
                                                  W3[0:rows(u), u], start=(t == 0), stop=True, skip_group_check=True)
                        mm.then_inc(h3.sem, 1)

                    first(0)
                    for u in range(U):
                        if u + 1 < U:
                            first(u + 1)
                        second(u)
                        if u >= 1:
                            third(u - 1)
                    third(U - 1)

            @block.scalar
            def _(act):
                act.wait_ge(exp_in, 1)
                nc.scalar.activation(G[:], G[:], ACT.Exp).then_inc(exp_out, 1)
                act.wait_ge(w_in, 1)
                nc.scalar.activation(sm[:, 3], sm[:, 3], ACT.Exp).then_inc(w_out, 1)
                act.sem_inc(r1.sem, 2)
                act.sem_inc(r2.sem, 2)
                act.wait_ge(ones_ok, 1)
                act.wait_ge(loaded, 16 * n_loads)
                with act.Fori(0, NC) as c:
                    def relu1(u):
                        act.wait_ge(h1.sem, h1.after(c, u + 1))
                        act.wait_ge(h2.sem, h2.after(c, last_user(u)))
                        nc.scalar.activation(H1[:, u % 2], p1[:, u % 2], ACT.Relu, bias=b1[:, u:u + 1]).then_inc(r1.sem, 1)

                    def relu2(u):
                        m = S_HIDDEN if u == 0 else E_HIDDEN
                        act.wait_ge(h2.sem, h2.after(c, u + 1))
                        act.wait_ge(h3.sem, h3.after(c, last_user(u)))
                        nc.scalar.activation(hidden2(u)[0:m], p2[0:m, u % 2], ACT.Relu, bias=b2[0:m, u:u + 1]).then_inc(r2.sem, 1)

                    relu1(0)
                    for u in range(U):
                        if u + 1 < U:
                            relu1(u + 1)
                        relu2(u)

            @block.vector
            def _(dve):
                ch = Chain(dve, steps)
                dve.wait_ge(gated, 1)
                ch.link(dve.tensor_tensor(G[:], pg[:], gb[:].unsqueeze(1).broadcast_to([P, NT, N_EXP]), ALU.add))
                emit_softmax4(dve, ch, G[:], sm[:, 0], exp_in, exp_out)
                free, m1, m2 = sm[:, 5], sm[:, 1], sm[:, 2]
                for r, m in enumerate((m1, m2)):
                    ch.link(dve.tensor_reduce(m, G[:], AX.X, ALU.max))
                    ch.link(dve.memset(free, 1.0))
                    for e in range(N_EXP):
                        s = sel[:, r, :, e]
                        ch.link(dve.tensor_tensor(s, G[:, :, e], m, ALU.is_equal))
                        ch.link(dve.tensor_tensor(s, s, free, ALU.mult))
                        ch.link(dve.tensor_tensor(free, free, s, ALU.subtract))
                    if r == 0:
                        ch.link(dve.scalar_tensor_tensor(out=G[:], in0=sel[:, 0], scalar=-2.0, in1=G[:],
                                                         op0=ALU.mult, op1=ALU.add))
                dve.tensor_tensor(sm[:, 3], m2, m1, ALU.subtract).then_inc(w_in, 1)
                dve.wait_ge(w_out, 1)
                ch.link(dve.tensor_scalar(sm[:, 4], sm[:, 3], 1.0, None, ALU.add))
                ch.link(dve.reciprocal(sm[:, 4], sm[:, 4]))
                ch.link(dve.tensor_tensor(sm[:, 3], sm[:, 3], sm[:, 4], ALU.mult))
                for r, w in ((0, sm[:, 4]), (1, sm[:, 3])):
                    ch.link(dve.tensor_tensor(sel[:, r], sel[:, r], w.unsqueeze(2).broadcast_to([P, NT, N_EXP]), ALU.mult))
                ch.link(dve.tensor_tensor(coef[:], sel[:, 0], sel[:, 1], ALU.add))
                ch.link(dve.tensor_tensor(k.X[:], k.X[:], b3[:].unsqueeze(1).broadcast_to([P, NT, D]), ALU.add))
                dve.sem_inc(added.sem, 2)
                with dve.Fori(0, NC) as c:
                    ch = Chain(dve, steps2, c, 1 + CT * U)
                    ch.link(dve.tensor_scalar(cc[:], coef[:, bass.ds(c * CT, CT), :], 1.0, None, ALU.mult))
                    for u in range(U):
                        dve.wait_ge(h3.sem, h3.after(c, u + 1))
                        for t in range(CT):
                            x = k.X[:, bass.ds(c * CT + t, 1), :]
                            o = p3[:, u % 2, t:t + 1]
                            if u == 0:
                                ins = dve.tensor_tensor(x, o, x, ALU.add)
                            else:
                                ins = dve.scalar_tensor_tensor(out=x, in0=o, scalar=cc[:, t, u - 1:u], in1=x,
                                                               op0=ALU.mult, op1=ALU.add)
                            ch.k += 1
                            ins.then_inc(steps2, 1)
                        dve.wait_ge(steps2, ch.base + ch.k)
                        dve.sem_inc(added.sem, 1)


def emit_convert(dve, c, q, A, NM, adj_in, converted, QW, QN, AS):
    t, w, s = q // 4, q % 4, q % AS
    dve.wait_ge(adj_in[s], 16 * (c * (QN // AS) + q // AS + 1))
    dve.tensor_scalar(NM[:, bass.ds(c % 2, 1), t, w * QW:(w + 1) * QW], A[:, s:s + 1], 0.0, None,
                      ALU.is_le).then_inc(converted.sem, 1)


def stage_graph_attention(k, a):
    nc = k.nc
    H, DH = G_HEADS, G_DH
    QW = N // 4
    QN = 4 * CT
    AS = 4
    PSL = 4
    LAG = 2
    U = H * NT
    with ExitStack() as outer:
        qA = k.sb(outer, "ga_qA", [P, H, N], F16)
        kA = k.sb(outer, "ga_kA", [P, H, N], F16)
        qB = k.sb(outer, "ga_qB", [96, H, N], F16)
        kB = k.sb(outer, "ga_kB", [96, H, N], F16)
        V = k.sb(outer, "ga_V", [P, NT, H, DH + 1], F32)
        sumV = k.sb(outer, "ga_sumV", [1, H * (DH + 1)], F32)
        We = k.sb(outer, "ga_We", [DH + 1, 2, H, D + 1], F32)
        bias = k.sb(outer, "ga_bias", [P, D], F32)
        with ExitStack() as ctx:
            YT = k.sb(ctx, "ga_YT", [P, N], F32)
            with ExitStack() as inner:
                Y = k.sb(inner, "ga_Y", [P, NT, D], F32)
                stage_layernorm(k, "ln2", Y[:], YT)
            Wq = k.sb(ctx, "ga_Wq", [P, H, P], F32)
            Wk = k.sb(ctx, "ga_Wk", [P, H, P], F32)
            Wv = k.sb(ctx, "ga_Wv", [P, D], F32)
            pp = k.ps(ctx, "ga_pp", [P, 2, CW])
            pv = k.ps(ctx, "ga_pv", [P, 2, CT, H, DH])
            ps = k.ps(ctx, "ga_ps", [1, H * (DH + 1)])
            loaded, late, filled = k.sem("ga_loaded"), k.sem("ga_late"), k.sem("ga_filled")
            projected, his, los = k.sem("ga_projected"), k.sem("ga_hi"), k.sem("ga_lo")
            vals, vmoved, vsum, vsum_ok = k.sem("ga_values"), k.sem("ga_vmoved"), k.sem("ga_vsum"), k.sem("ga_vsum_ok")
            units = [(h, s, c) for h in range(H) for s in range(2) for c in range(NC)]
            with nc.Block() as block:
                @block.sync
                def _(sp):
                    for h in range(H):
                        for r in range(2):
                            for W, name in ((Wq, "Wq"), (Wk, "Wk")):
                                sp.dma_start(W[:, h, r * DH:(r + 1) * DH], a[name][:, h * DH:(h + 1) * DH]).then_inc(loaded, 16)
                    sp.dma_start(Wv[:], a["Wv"]).then_inc(loaded, 16)
                    for s, name in enumerate(("weightr", "weightd")):
                        sp.dma_start(We[0:DH, s, :, 0:D], a[name].rearrange("(h i) o -> i h o", h=H)).then_inc(late, 16)
                    sp.dma_start(bias[:], a["bias"].rearrange("(o n) -> o n", o=1).broadcast_to([P, D])).then_inc(late, 16)
                    sp.wait_ge(late, 48)

                @block.gpsimd
                def _(pool):
                    for n, (tile, value) in enumerate((
                            (qB[DH:96], 0.0), (kB[DH:96], 0.0), (kB[DH:DH + 1], 1.0), (V[:, :, :, DH:DH + 1], 1.0),
                            (We[0:DH, :, :, D:D + 1], 0.0), (We[DH:DH + 1, :, :, 0:D], 0.0), (We[DH:DH + 1, :, :, D:D + 1], 1.0))):
                        pool.memset(tile, value).then_inc(filled, 1)
                        pool.wait_ge(filled, n + 1)

                @block.tensor
                def _(pe):
                    pe.wait_ge(loaded, 16 * 9)
                    for n, (h, s, c) in enumerate(units):
                        if n >= 2:
                            pe.wait_ge(los, n - 1)
                        nc.tensor.matmul(pp[:, n % 2], (Wk if s else Wq)[:, h], YT[:, c * CW:(c + 1) * CW],
                                         start=True, stop=True).then_inc(projected, 1)
                    for c in range(NC):
                        if c >= 2:
                            pe.wait_ge(vmoved, c - 1)
                        for t in range(CT):
                            mm = nc.tensor.matmul(pv[:, c % 2, t], YT[:, (c * CT + t) * P:(c * CT + t + 1) * P], Wv[:],
                                                  start=(t == 0), stop=True, skip_group_check=True)
                        mm.then_inc(vals, 1)
                    pe.wait_ge(vmoved, NC)
                    pe.wait_ge(filled, 4)
                    for t in range(NT):
                        mm = nc.tensor.matmul(ps[:], k.ones[:, 0:1], V[:, t], start=(t == 0), stop=(t == NT - 1))
                    mm.then_inc(vsum, 1)

                @block.scalar
                def _(act):
                    for n, (h, s, c) in enumerate(units):
                        cols = slice(c * CW, (c + 1) * CW)
                        act.wait_ge(projected, n + 1)
                        if s == 0:
                            nc.scalar.activation(qA[:, h, cols], pp[:, n % 2], ACT.Copy, scale=DH ** -0.5).then_inc(his, 2)
                        else:
                            nc.scalar.activation(kA[:, h, cols], pp[:, n % 2], ACT.Copy).then_inc(his, 1)
                            nc.scalar.activation(kB[0:DH, h, cols], pp[0:DH, n % 2], ACT.Copy).then_inc(his, 1)

                @block.vector
                def _(dve):
                    for n, (h, s, c) in enumerate(units):
                        cols = slice(c * CW, (c + 1) * CW)
                        dve.wait_ge(his, 2 * (n + 1))
                        if s == 0:
                            dve.scalar_tensor_tensor(out=qB[0:DH, h, cols], in0=pp[0:DH, n % 2], scalar=DH ** -0.5,
                                                     in1=qA[0:DH, h, cols], op0=ALU.mult, op1=ALU.subtract).then_inc(los, 1)
                        else:
                            dve.tensor_tensor(kA[DH:P, h, cols], pp[DH:P, n % 2], kA[DH:P, h, cols],
                                              ALU.subtract).then_inc(los, 1)
                    for c in range(NC):
                        dve.wait_ge(vals, c + 1)
                        dve.tensor_copy(V[:, c * CT:(c + 1) * CT, :, 0:DH], pv[:, c % 2]).then_inc(vmoved, 1)
                    dve.wait_ge(vsum, 1)
                    dve.tensor_copy(sumV[:], ps[:]).then_inc(vsum_ok, 1)

        with ExitStack() as ctx:
            A = k.sb(ctx, "ga_adj", [P, AS, QW], I32)
            NM = k.sb(ctx, "ga_nm", [P, 2, CT, N], BF16)
            Pr = k.sb(ctx, "ga_probs", [P, PSL, CW], F32)
            mx = k.sb(ctx, "ga_mx", [P, H, CT, 4], F32)
            mc = k.sb(ctx, "ga_mc", [P, H, CT], F32)
            pm = k.ps(ctx, "ga_pm", [P, 2, QW])
            pt = k.ps(ctx, "ga_pt", [P, 2, CW])
            po = k.ps(ctx, "ga_po", [DH + 1, H, CW])
            uT = k.sb(ctx, "ga_uT", [DH + 1, H, CW], F32)
            er = k.sb(ctx, "ga_er", [1, CW], F32)
            rd = k.sb(ctx, "ga_rd", [P, H, CT], F32)
            Z = k.sb(ctx, "ga_Z", [P, CT, D], F32)
            Z2 = k.sb(ctx, "ga_Z2", [P, CT, D], F32)
            steps = k.sem("ga_steps")
            adj_in = [k.sem(f"ga_adj_in{s}") for s in range(AS)]
            R = H * QN
            converted = Count(k.sem("ga_converted"), QN, AS)
            scored = Count(k.sem("ga_scored"), R + 2 * H)
            reduced = Count(k.sem("ga_reduced"), R + 2 * H, 2)
            mcol = Count(k.sem("ga_mcol"), 3)
            er_here = Count(k.sem("ga_er_here"), 1)
            trans = Count(k.sem("ga_trans"), U)
            probs = Count(k.sem("ga_probs_done"), U, 2)
            used = Count(k.sem("ga_probs_used"), U, PSL)
            out_done = Count(k.sem("ga_out"), H)
            out_moved = Count(k.sem("ga_out_moved"), H, H)
            with nc.Block() as block:
                @block.sync
                def _(sp):
                    with sp.Fori(0, NC) as c:
                        for q in range(QN):
                            t, w, s = q // 4, q % 4, q % AS
                            sp.wait_ge(converted.sem, converted.after(c, q + 1 - AS))
                            sp.dma_start(A[:, s], a["adj"][bass.ds((c * CT + t) * P, P), w * QW:(w + 1) * QW]).then_inc(adj_in[s], 16)

                @block.vector
                def _(dve):
                    dve.sem_inc(converted.sem, AS)
                    dve.sem_inc(reduced.sem, 2)
                    dve.sem_inc(out_moved.sem, H)

                    def chunk(c, convert_next):
                        for r in range(R):
                            h, q = r // QN, r % QN
                            dve.wait_ge(scored.sem, scored.after(c, r + 1))
                            dve.tensor_reduce(mx[:, h, q // 4, q % 4:q % 4 + 1], pm[:, r % 2], AX.X, ALU.max).then_inc(reduced.sem, 1)
                        dve.wait_ge(reduced.sem, reduced.after(c, R))
                        dve.tensor_scalar(er[:], k.Erow[:, bass.ds(c * CW, CW)], 1.0, None, ALU.mult).then_inc(er_here.sem, 1)
                        dve.tensor_reduce(mc[:], mx[:], AX.X, ALU.max).then_inc(mcol.sem, 1)
                        dve.wait_ge(mcol.sem, mcol.after(c, 1))
                        dve.tensor_scalar(mc[:], mc[:], -M16_MAX, M16_MAX, ALU.max, ALU.min).then_inc(mcol.sem, 1)
                        for h in range(H):
                            dve.wait_ge(scored.sem, scored.after(c, R + h + 1))
                            dve.tensor_scalar(qB[DH:DH + 1, h:h + 1, bass.ds(c * CW, CW)], pm[0:1, h:h + 1, 0:CW], -1.0, None,
                                              ALU.mult).then_inc(reduced.sem, 1)
                        if convert_next:
                            for q in range(QN):
                                emit_convert(dve, c + 1, q, A, NM, adj_in, converted, QW, QN, AS)
                        for h in range(H):
                            dve.wait_ge(out_done.sem, out_done.after(c, h + 1))
                            dve.tensor_copy(uT[:, h], po[:, h]).then_inc(out_moved.sem, 1)
                        ch = Chain(dve, steps, c, 5 + 2 * CT)
                        for h in range(H):
                            o = pm[:, h].rearrange("p (t n) -> p t n", t=CT)
                            dve.wait_ge(scored.sem, scored.after(c, R + H + h + 1))
                            ch.link(dve.reciprocal(rd[:, h], o[:, :, D]))
                            for t in range(CT):
                                if h == 0:
                                    ins = dve.tensor_scalar(Z[:, t], o[:, t, 0:D], rd[:, h, t:t + 1], None, ALU.mult)
                                else:
                                    ins = dve.scalar_tensor_tensor(out=Z[:, t], in0=o[:, t, 0:D], scalar=rd[:, h, t:t + 1],
                                                                   in1=Z[:, t], op0=ALU.mult, op1=ALU.add)
                                ch.k += 1
                                ins.then_inc(steps, 1)
                            dve.wait_ge(steps, ch.base + ch.k)
                            dve.sem_inc(reduced.sem, 1)
                        ch.link(dve.tensor_tensor(Z[:], Z[:], bias[:].unsqueeze(1).broadcast_to([P, CT, D]), ALU.add))
                        ch.link(dve.tensor_scalar(Z2[:], Z[:], SLOPE, None, ALU.mult))
                        ch.link(dve.tensor_tensor(Z[:], Z[:], Z2[:], ALU.max))
                        x = k.X[:, bass.ds(c * CT, CT), :]
                        dve.tensor_tensor(x, x, Z[:], ALU.add).then_inc(mcol.sem, 1)
                        dve.wait_ge(mcol.sem, mcol.after(c, 3))

                    for q in range(QN):
                        emit_convert(dve, 0, q, A, NM, adj_in, converted, QW, QN, AS)
                    with dve.Fori(0, NC - 1) as c:
                        chunk(c, True)
                    chunk(NC - 1, False)

                @block.scalar
                def _(act):
                    act.sem_inc(probs.sem, 2)
                    with act.Fori(0, NC) as c:
                        for u in range(U):
                            act.wait_ge(trans.sem, trans.after(c, u + 1))
                            act.wait_ge(used.sem, used.after(c, u + 1 - PSL))
                            nc.scalar.activation(Pr[:, u % PSL], pt[:, u % 2], ACT.Exp).then_inc(probs.sem, 1)

                @block.tensor
                def _(pe):
                    pe.sem_inc(used.sem, PSL)
                    with pe.Fori(0, NC) as c:
                        pe.get_value_cache().nocache = True
                        par = pe.snap(c % 2)
                        for r in range(R):
                            h, q = r // QN, r % QN
                            t, w = q // 4, q % 4
                            if h == 0:
                                pe.wait_ge(converted.sem, converted.after(c, q + 1))
                            pe.wait_ge(reduced.sem, reduced.after(c, r + 1 - 2))
                            for i in range(2):
                                o = w * QW + i * CW
                                dst = pm[:, r % 2, i * CW:(i + 1) * CW]
                                nc.tensor.matmul(dst, k.negbig[:], NM[:, bass.ds(par, 1), t, o:o + CW], start=True, stop=False)
                                mm = nc.tensor.matmul(dst, qA[:, h:h + 1, bass.ds(c * CW + t * P, P)], kA[:, h, o:o + CW],
                                                      start=False, stop=True)
                            mm.then_inc(scored.sem, 1)
                        pe.wait_ge(mcol.sem, mcol.after(c, 2))
                        pe.wait_ge(reduced.sem, reduced.after(c, R))
                        for h in range(H):
                            for t in range(CT):
                                mm = nc.tensor.matmul(pm[0:1, h, t * P:(t + 1) * P], mc[:, h, t:t + 1], k.ident[:],
                                                      start=(t == 0), stop=True, skip_group_check=True)
                            mm.then_inc(scored.sem, 1)
                        for u in range(U + LAG):
                            if u < U:
                                h, j = u // NT, u % NT
                                pe.wait_ge(probs.sem, probs.after(c, u + 1 - 2))
                                if j == 0:
                                    pe.wait_ge(reduced.sem, reduced.after(c, R + h + 1))
                                dst = pt[:, u % 2]
                                rhs = lambda q: q[:, h:h + 1, bass.ds(c * CW, CW)]
                                nc.tensor.matmul(dst.unsqueeze(1), kA[:, h, j * P:(j + 1) * P], rhs(qA), start=True, stop=False,
                                                 skip_group_check=True)
                                nc.tensor.matmul(dst.unsqueeze(1), kB[:, h, j * P:(j + 1) * P], rhs(qB), start=False, stop=False,
                                                 skip_group_check=True)
                                for t in range(CT):
                                    mm = nc.tensor.matmul(pt[:, u % 2, t * P:(t + 1) * P],
                                                          NM[:, bass.ds(par, 1), t, j * P:(j + 1) * P], k.negbig[:],
                                                          start=False, stop=(t == CT - 1), skip_group_check=True)
                                mm.then_inc(trans.sem, 1)
                            v = u - LAG
                            if v < 0:
                                continue
                            h, j = v // NT, v % NT
                            pe.wait_ge(probs.sem, probs.after(c, v + 1))
                            if j == 0:
                                pe.wait_ge(out_moved.sem, out_moved.after(c, h + 1 - H))
                            nc.tensor.matmul(po[:, h], V[:, j, h], Pr[:, v % PSL], start=(j == 0), stop=False,
                                             skip_group_check=True).then_inc(used.sem, 1)
                            if j == NT - 1:
                                pe.wait_ge(er_here.sem, er_here.after(c, 1))
                                nc.tensor.matmul(po[:, h], sumV[0:1, h * (DH + 1):(h + 1) * (DH + 1)], er[:], start=False,
                                                 stop=True, skip_group_check=True).then_inc(out_done.sem, 1)
                        for h in range(H):
                            pe.wait_ge(out_moved.sem, out_moved.after(c, h + 1))
                            pe.wait_ge(reduced.sem, reduced.after(c, R + H))
                            for t in range(CT):
                                mm = nc.tensor.matmul(pm[:, h:h + 1, t * 2 * P:t * 2 * P + D + 1], uT[:, h, t * P:(t + 1) * P],
                                                      We[:, bass.ds(c * CW // HALF, 1), h], start=(t % 2 == 0), stop=True,
                                                      skip_group_check=True)
                            mm.then_inc(scored.sem, 1)



def stage_self_attention(k, a, ctx_out):
    nc = k.nc
    H, E, DH = F_HEADS, F_EXP, F_DH
    MR = 3 * DH
    KR = MR + 1
    SCALE = float(DH) ** 0.5
    VW = DH + 1
    AW = DH + N_EXP
    G = H * E
    QW = 2 * CW
    NW = N // QW
    PSL = 4
    LAG = 2
    SX, MIX = ctx_out
    parts = nc.dram_tensor("sa_parts", (2, H * DH, N), F16).ap()
    seen = nc.dram_tensor("sa_seen", (H * DH, N), BF16).ap()
    with ExitStack() as outer:
        V = k.sb(outer, "sa_V", [P, NT, H, VW], F32)
        causA = k.sb(outer, "sa_causA", [P, P], BF16)
        causT = k.sb(outer, "sa_causT", [P, 2 * P], BF16)
        ident16 = k.sb(outer, "sa_ident16", [P, P], F16)
        two = k.sb(outer, "sa_two", [KR, G * (AW + 1) + P], F32)
        W16 = k.sb(outer, "sa_W16", [MR, H, 1 + E, MR], F16)
        gb = k.sb(outer, "sa_gb", [P, H, E], F32)
        with ExitStack() as ctx:
            HL = k.sb(ctx, "sa_HL", [P, P], F32)
            hb = k.sb(ctx, "sa_hb", [P, 1], F32)
            Wv = k.sb(ctx, "sa_Wv", [P, P], F32)
            W = k.sb(ctx, "sa_W", [MR, H, 1 + E, MR], F32)
            YT = k.sb(ctx, "sa_YT", [P, N], F32)
            with ExitStack() as inner:
                Y = k.sb(inner, "sa_Y", [P, NT, D], F32)
                stage_layernorm(k, "ln3", Y[:], YT)
            sxT = k.sb(ctx, "sa_sxT", [P, N], F32)
            hiT = k.sb(ctx, "sa_hiT", [P, N], F16)
            loT = k.sb(ctx, "sa_loT", [P, N], F16)
            npT = k.sb(ctx, "sa_npT", [P, N], BF16)
            pp = k.ps(ctx, "sa_pp", [P, 2, CW])
            px = k.ps(ctx, "sa_px", [P, 2, CT, P])
            pv = k.ps(ctx, "sa_pv", [P, 2, CT, P])
            loaded, filled, late = k.sem("sap_loaded"), k.sem("sap_filled"), k.sem("sap_late")
            proj, biased, split = k.sem("sap_proj"), k.sem("sap_biased"), k.sem("sap_split")
            his, wsplit, stored, seen_at = k.sem("sap_his"), k.sem("sap_wsplit"), k.sem("sap_stored"), k.sem("sap_seen")
            turned, xmoved, vals, vmoved = k.sem("sap_turned"), k.sem("sap_xmoved"), k.sem("sap_vals"), k.sem("sap_vmoved")
            with nc.Block() as block:
                @block.sync
                def _(sp):
                    sp.dma_start(HL[:], a["hlT"]).then_inc(loaded, 16)
                    sp.dma_start(hb[:], a["hlb"]).then_inc(loaded, 16)
                    sp.dma_start(Wv[:], a["wvB"]).then_inc(loaded, 16)
                    sp.dma_start(W[:], a["wqk"]).then_inc(late, 16)
                    sp.dma_start(two[:], a["two"]).then_inc(late, 16)
                    sp.dma_start(gb[:], a["gate_b"].rearrange("h e -> (h e)").rearrange("(o n) -> o n", o=1)
                                 .broadcast_to([P, H * E]).rearrange("p (h e) -> p h e", h=H)).then_inc(late, 16)
                    sp.wait_ge(late, 48)
                    sp.wait_ge(his, NC)
                    sp.dma_start(parts[0], hiT[:]).then_inc(stored, 16)
                    sp.wait_ge(split, NC)
                    sp.dma_start(parts[1], loT[:]).then_inc(stored, 16)
                    sp.wait_ge(seen_at, NC)
                    sp.dma_start(seen, npT[:]).then_inc(stored, 16)
                    sp.wait_ge(stored, 48)

                @block.gpsimd
                def _(pool):
                    for m in (causA, causT, ident16):
                        pool.memset(m[:], 0.0).then_inc(filled, 1)
                    pool.memset(V[:, :, :, DH:VW], 1.0).then_inc(filled, 1)
                    pool.wait_ge(filled, 4)
                    pool.affine_select(out=causA[:], in_=causA[:], compare_op=ALU.is_ge, fill=-BIG, base=0,
                                       pattern=[[-1, P]], channel_multiplier=1).then_inc(filled, 1)
                    pool.affine_select(out=causT[:], in_=causT[:], compare_op=ALU.is_ge, fill=-BIG, base=-P,
                                       pattern=[[1, 2 * P]], channel_multiplier=-1).then_inc(filled, 1)
                    pool.affine_select(out=ident16[:], in_=ident16[:], compare_op=ALU.not_equal, fill=1.0, base=0,
                                       pattern=[[-1, P]], channel_multiplier=1).then_inc(filled, 1)

                @block.tensor
                def _(pe):
                    pe.wait_ge(loaded, 48)
                    for c in range(NC):
                        if c >= 2:
                            pe.wait_ge(biased, c - 1)
                        nc.tensor.matmul(pp[:, c % 2], HL[:], YT[:, c * CW:(c + 1) * CW], start=True, stop=True).then_inc(proj, 1)
                    for c in range(NC):
                        pe.wait_ge(biased, c + 1)
                        for dst, w, done, freed in ((px, k.ident, turned, xmoved), (pv, Wv, vals, vmoved)):
                            if c >= 2:
                                pe.wait_ge(freed, c - 1)
                            for t in range(CT):
                                mm = nc.tensor.matmul(dst[:, c % 2, t], sxT[:, (c * CT + t) * P:(c * CT + t + 1) * P], w[:],
                                                      start=(t == 0), stop=True, skip_group_check=True)
                            mm.then_inc(done, 1)

                @block.scalar
                def _(act):
                    act.wait_ge(loaded, 48)
                    for c in range(NC):
                        act.wait_ge(proj, c + 1)
                        nc.scalar.activation(sxT[:, c * CW:(c + 1) * CW], pp[:, c % 2], ACT.Identity, bias=hb[:]).then_inc(biased, 1)
                    for c in range(NC):
                        act.wait_ge(biased, c + 1)
                        nc.scalar.activation(hiT[:, c * CW:(c + 1) * CW], sxT[:, c * CW:(c + 1) * CW], ACT.Copy).then_inc(his, 1)

                @block.vector
                def _(dve):
                    dve.wait_ge(late, 48)
                    dve.tensor_copy(W16[:], W[:]).then_inc(wsplit, 1)
                    dve.wait_ge(wsplit, 1)
                    lo = slice(DH, 2 * DH)
                    dve.tensor_tensor(W16[lo], W[lo], W16[lo], ALU.subtract).then_inc(wsplit, 1)
                    for c in range(NC):
                        dve.wait_ge(turned, c + 1)
                        dve.tensor_copy(SX[:, c * CT:(c + 1) * CT], px[:, c % 2]).then_inc(xmoved, 1)
                        dve.wait_ge(vals, c + 1)
                        dve.tensor_copy(V[:, c * CT:(c + 1) * CT, :, 0:DH],
                                        pv[:, c % 2].rearrange("p t (h d) -> p t h d", h=H)).then_inc(vmoved, 1)
                        cols = slice(c * CW, (c + 1) * CW)
                        dve.wait_ge(his, c + 1)
                        dve.tensor_tensor(loT[:, cols], sxT[:, cols], hiT[:, cols], ALU.subtract).then_inc(split, 1)
                        dve.tensor_scalar(npT[:, cols], sxT[:, cols], 0.0, None, ALU.not_equal).then_inc(seen_at, 1)

        with ExitStack() as ctx:
            XS = k.sb(ctx, "sa_XS", [MR, N], F16)
            QS = k.sb(ctx, "sa_QS", [KR, 2, N], F16)
            KS = k.sb(ctx, "sa_KS", [KR, 2, N], F16)
            NP = k.sb(ctx, "sa_NP", [KR, 2, N], BF16)
            Vc = k.sb(ctx, "sa_Vc", [P, NT, VW], F32)
            ATT = k.sb(ctx, "sa_ATT", [P, E, NT, AW], F32)
            tmp = k.sb(ctx, "sa_tmp", [P, 2, NT, DH], F32)
            Pr = k.sb(ctx, "sa_probs", [P, PSL, CW], F32)
            mx = k.sb(ctx, "sa_mx", [P, 2, CT, NW], F32)
            mc = k.sb(ctx, "sa_mc", [P, 2, CT], F32)
            mh = k.sb(ctx, "sa_mh", [P, 2, CT], F16)
            OT = k.sb(ctx, "sa_OT", [KR, CW], F32)
            rd = k.sb(ctx, "sa_rd", [P, CT], F32)
            lg = k.sb(ctx, "sa_lg", [P, NT, E], F32)
            sm = k.sb(ctx, "sa_sm", [P, NT], F32)
            pm = k.ps(ctx, "sa_pm", [P, 2, QW])
            pt = k.ps(ctx, "sa_pt", [P, 2, CW])
            po = k.ps(ctx, "sa_po", [P, CW])
            pz = k.ps(ctx, "sa_pz", [P, CT, P])

            TU = [CT * (c + 1) for c in range(NC)]
            T0 = [sum(TU[:c]) for c in range(NC + 1)]

            def pieces(c):
                return [("max", c, r) for r in range(CT * (c // 2 + 1))]

            def mixed_in(first, row_at, then):
                return then[:row_at] + [("row", first, 0)] + then[row_at:]

            def ring_plan():
                plan = mixed_in(2, 0, pieces(3))
                for c in range(4, NC):
                    plan += mixed_in(c - 1, 2, pieces(c))
                plan += [("row", NC - 1, 0)]
                head = len(plan)
                plan += [("project", s, w) for w in range(NW) for s in range(2)]
                plan += pieces(0)
                for c in (1, 2):
                    plan += mixed_in(c - 1, 2, pieces(c))
                return plan, head

            def rows_in(uses):
                return [i for i, use in enumerate(uses) if use[0] == "row"]

            ring, ahead_from = ring_plan()
            RING = len(ring)
            AHEAD = RING - ahead_from
            assert RING % 2 == 0 and len(rows_in(ring)) == NC
            rows = rows_in(ring)
            last_piece = {}
            for i, use in enumerate(ring):
                if use[0] == "max":
                    last_piece[use[1]] = i

            def row_count(i):
                return sum(1 for x in rows if x <= i)

            PROJ = 2 * NW
            x_in = Count(k.sem("sa_x_in"), 5 * 16)
            scored = Count(k.sem("sa_scored"), RING, AHEAD)
            reduced = Count(k.sem("sa_reduced"), RING, 2 + AHEAD)
            his = Count(k.sem("sa_hi"), PROJ, PROJ)
            mcol = Count(k.sem("sa_mcol"), 3 * NC, 3 * 3)
            zin = Count(k.sem("sa_zin"), NC, 1)
            zout = Count(k.sem("sa_zout"), NC, 1)
            trans = Count(k.sem("sa_trans"), T0[NC])
            probs = Count(k.sem("sa_probs_done"), T0[NC], 2)
            used = Count(k.sem("sa_used"), T0[NC], PSL)
            summed_out = Count(k.sem("sa_summed_out"), NC, 1)
            values_in = Count(k.sem("sa_values_in"), 1)
            mixed = Count(k.sem("sa_mixed"), 2 * E, 2 * E)
            gates = Count(k.sem("sa_gates"), 1)
            rds = k.sem("sa_rds")
            steps, psteps = k.sem("sa_steps"), k.sem("sa_psteps")
            e_in, e_out, ready = k.sem("sa_exp_in"), k.sem("sa_exp_out"), k.sem("sa_ready")

            def turn_plan():
                plan = []
                for c in range(NC):
                    for j in range(TU[c]):
                        u = T0[c] + j
                        plan += [(u, "scores", c, j), (u + LAG + 0.2, "values", c, j)]
                    end = T0[c + 1] - 1 + LAG
                    plan += [(end + 0.25, "sums_out", c), (end + 1.3, "by_token", c), (end + 2.2, "results", c)]
                    if c == NC - 1:
                        plan[-2:] = [(end + 0.9, "by_token", c), (end + 0.95, "results", c)]
                step = (T0[NC] + 1.0) / RING
                ends = [T0[c + 1] - 1 + LAG for c in range(NC)]
                for i, use in enumerate(ring):
                    at = (i + 0.4) * step
                    if i == rows[-3]:
                        at += 1.2
                    for end in ends[:-1]:
                        if end - 0.8 < at < end + 0.3:
                            at = end + 0.3
                    plan.append((at, "ring", i))
                return [p[1:] for p in sorted(plan, key=lambda p: p[0])]

            plan = turn_plan()
            ahead_plan = [("ring", i) for i in range(ahead_from, RING)]

            def piece(c, r):
                per = c // 2 + 1
                t, w = r // per, r % per
                end = (c * CT + t + 1) * P
                return t, w, w * QW, min(end, (w + 1) * QW)

            def parity_of(i, par):
                return 1 - par if i >= ahead_from else par

            def first_query(c, j):
                return 0 if (c == 0 and j == 1) else max(0, j - c * CT) * P

            with nc.Block() as block:
                @block.sync
                def _(sp):
                    def load(head, par):
                        rows_ = bass.ds(head * DH, DH)
                        for i, part in enumerate((0, 0, 1)):
                            sp.dma_start(XS[i * DH:(i + 1) * DH], parts[part][rows_, :]).then_inc(x_in.sem, 16)
                        for i in range(2):
                            sp.dma_start(NP[i * 64:i * 64 + DH, par], seen[rows_, :]).then_inc(x_in.sem, 16)

                    sp.wait_ge(ready, 3)
                    load(0, 0)
                    with sp.Fori(0, G // 2) as m:
                        for par in range(2):
                            g = 2 * m + par
                            sp.wait_ge(scored.sem, scored.after(g, PROJ - AHEAD))
                            sp.wait_ge(zout.sem, zout.after(g, 0))
                            load(((g + 1) % G) // E, 1 - par)
                    sp.wait_ge(x_in.sem, (G + 1) * 5 * 16)

                @block.gpsimd
                def _(pool):
                    pool.memset(OT[:], 0.0).then_inc(ready, 1)
                    pool.memset(NP[:], 1.0).then_inc(ready, 1)
                    pool.wait_ge(ready, 2)
                    pool.memset(KS[MR:KR], 1.0).then_inc(ready, 1)
                    with pool.Fori(0, H) as n:
                        ch = Chain(pool, psteps, n, E - 2)
                        pool.wait_ge(gates.sem, gates.after(n, 1))
                        for e in range(E):
                            w = lg[:, :, e:e + 1].broadcast_to([P, NT, DH])
                            pool.tensor_tensor(tmp[:, min(e, 1)], ATT[:, e, :, 0:DH], w, ALU.mult).then_inc(mixed.sem, 1)
                            pool.wait_ge(mixed.sem, mixed.after(n, e + 1))
                            if 0 < e < E - 1:
                                ch.link(pool.tensor_tensor(tmp[:, 0], tmp[:, 0], tmp[:, 1], ALU.add))
                        out = MIX[:, :, bass.ds(n * DH, DH)]
                        pool.tensor_tensor(out, tmp[:, 0], tmp[:, 1], ALU.add).then_inc(mixed.sem, E)
                        pool.wait_ge(mixed.sem, mixed.after(n, 2 * E))

                @block.tensor
                def _(pe):
                    pe.sem_inc(used.sem, PSL)
                    pe.sem_inc(zin.sem, 1)

                    def project(g, i, par):
                        s, w = ring[i][1:]
                        lhs = W16[:, bass.ds(g // E, 1), 0] if s == 0 else W16[:, bass.ds(g // E, 1), bass.ds(1 + g % E, 1)]
                        for h in range(2):
                            o = w * QW + h * CW
                            mm = nc.tensor.matmul(pm[0:MR, i % 2, h * CW:(h + 1) * CW], lhs, XS[:, o:o + CW],
                                                  start=True, stop=True, skip_group_check=True)
                        mm.then_inc(scored.sem, 1)

                    def maxima(i, par):
                        c, r = ring[i][1:]
                        t, w, a0, a1 = piece(c, r)
                        q = QS[0:MR, par, (c * CT + t) * P:(c * CT + t + 1) * P]
                        last = a1 == (c * CT + t + 1) * P
                        for o in range(a0, a1, CW):
                            o1 = min(a1, o + CW)
                            diag = last and o1 == a1
                            mm = nc.tensor.matmul(pm[:, i % 2, o - a0:o1 - a0], q, KS[0:MR, par, o:o1], start=True, stop=not diag,
                                                  skip_group_check=True)
                            if diag:
                                mm = nc.tensor.matmul(pm[:, i % 2, a1 - P - a0:a1 - a0], k.identb[:], causA[:], start=False,
                                                      stop=True, skip_group_check=True)
                        mm.then_inc(scored.sem, 1)

                    def row(g, i):
                        n = row_count(i)
                        pe.wait_ge(mcol.sem, mcol.after(g, 3 * (n - 1)))
                        for t in range(CT):
                            mm = nc.tensor.matmul(pm[0:1, i % 2, t * P:(t + 1) * P], mh[:, n % 2, t:t + 1], ident16[:],
                                                  start=(t == 0), stop=True, skip_group_check=True)
                        mm.then_inc(scored.sem, 1)

                    def use_ring(g, g_next, i, par):
                        pe.wait_ge(reduced.sem, reduced.after(g, i + 1 - 2))
                        if ring[i][0] == "project":
                            if i == ahead_from:
                                pe.wait_ge(x_in.sem, x_in.after(g, 2 * 5 * 16))
                            project(g_next, i, 1 - par)
                        elif ring[i][0] == "max":
                            maxima(i, parity_of(i, par))
                        else:
                            row(g, i)

                    def values(g, c, j):
                        u = T0[c] + j
                        o = first_query(c, j)
                        pe.wait_ge(probs.sem, probs.after(g, u + 1))
                        if j < 2:
                            pe.wait_ge(summed_out.sem, summed_out.after(g, c))
                        b = 64 * (j % 2)
                        mm = nc.tensor.matmul(po[b:b + VW, o:CW], Vc[:, j], Pr[:, u % PSL, o:CW], start=(j < 2),
                                              stop=(j >= TU[c] - 2), skip_group_check=True)
                        mm.then_inc(used.sem, 1)

                    def scores(g, c, j, par):
                        u = T0[c] + j
                        o = first_query(c, j)
                        pe.wait_ge(probs.sem, probs.after(g, u + 1 - 2))
                        if j == 0:
                            done = [i for i in rows if ring[i][1] == c][0]
                            pe.wait_ge(reduced.sem, reduced.after(g, done + 1 - (RING if done >= ahead_from else 0)))
                        q = QS[0:KR, par, c * CW + o:(c + 1) * CW]
                        diag = j >= c * CT
                        mm = nc.tensor.matmul(pt[:, u % 2, o:CW], KS[0:KR, par, j * P:(j + 1) * P], q, start=True,
                                              stop=not diag, skip_group_check=True)
                        if diag:
                            d = (j - c * CT) * P
                            mm = nc.tensor.matmul(pt[:, u % 2, o:d + P], k.identb[:], causT[:, P - (d - o):2 * P],
                                                  start=False, stop=True, skip_group_check=True)
                        mm.then_inc(trans.sem, 1)

                    def by_token(g, c):
                        pe.wait_ge(summed_out.sem, summed_out.after(g, c + 1))
                        pe.wait_ge(zout.sem, zout.after(g, c))
                        for t in range(CT):
                            mm = nc.tensor.matmul(pz[:, t], OT[:, t * P:(t + 1) * P], two[:, bass.ds(g * (AW + 1), P)],
                                                  start=(t == 0), stop=True, skip_group_check=True)
                        mm.then_inc(zin.sem, 1)

                    pe.wait_ge(ready, 3)
                    for _, i in ahead_plan:
                        use_ring(-1, 0, i, 1)
                    with pe.Fori(0, H) as n:
                        pe.get_value_cache().nocache = True
                        with pe.Fori(0, E // 2) as m:
                            pe.get_value_cache().nocache = True
                            for par in range(2):
                                g = pe.snap(n * E + m * 2 + par)
                                g_next = pe.snap((n * E + m * 2 + par + 1) % G)
                                if par == 0:
                                    pe.wait_ge(values_in.sem, values_in.after(n, 1))
                                for what, *args in plan:
                                    if what == "scores":
                                        scores(g, *args, par)
                                    elif what == "values":
                                        values(g, *args)
                                    elif what == "ring":
                                        use_ring(g, g_next, *args, par)
                                    elif what == "by_token":
                                        by_token(g, *args)

                @block.scalar
                def _(act):
                    act.sem_inc(probs.sem, 2)

                    def high(g, i, par):
                        s, w = ring[i][1:]
                        act.wait_ge(scored.sem, scored.after(g, i + 1))
                        dst = (QS if s else KS)[0:MR, 1 - par, w * QW:(w + 1) * QW]
                        nc.scalar.activation(dst, pm[0:MR, i % 2], ACT.Copy, scale=SCALE if s else 1.0).then_inc(his.sem, 1)

                    for _, i in ahead_plan:
                        if ring[i][0] == "project":
                            high(-1, i, 1)
                    with act.Fori(0, H) as n:
                        act.get_value_cache().nocache = True
                        with act.Fori(0, E // 2) as m:
                            act.get_value_cache().nocache = True
                            for par in range(2):
                                g = act.snap(n * E + m * 2 + par)
                                for what, *args in plan:
                                    if what == "ring" and ring[args[0]][0] == "project":
                                        high(g, args[0], par)
                                    elif what == "scores":
                                        c, j = args
                                        u = T0[c] + j
                                        o = first_query(c, j)
                                        act.wait_ge(trans.sem, trans.after(g, u + 1))
                                        act.wait_ge(used.sem, used.after(g, u + 1 - PSL))
                                        nc.scalar.activation(Pr[:, u % PSL, o:CW], pt[:, u % 2, o:CW], ACT.Exp).then_inc(probs.sem, 1)
                        act.wait_ge(e_in, n + 1)
                        nc.scalar.activation(lg[:], lg[:], ACT.Exp).then_inc(e_out, 1)

                @block.vector
                def _(dve):
                    dve.sem_inc(reduced.sem, 2)
                    dve.sem_inc(zout.sem, 1)
                    dve.sem_inc(mixed.sem, 2 * E)
                    dve.memset(po[:], 0.0).then_inc(summed_out.sem, 1)

                    def low(g, i, par):
                        s, w = ring[i][1:]
                        cols = slice(w * QW, (w + 1) * QW)
                        dve.wait_ge(his.sem, his.after(g, i + 1 - ahead_from))
                        if s == 0:
                            lo = slice(DH, 2 * DH)
                            dve.tensor_tensor(KS[lo, 1 - par, cols], pm[lo, i % 2], KS[lo, 1 - par, cols],
                                              ALU.subtract).then_inc(reduced.sem, 1)
                        else:
                            lo = slice(2 * DH, MR)
                            dve.scalar_tensor_tensor(out=QS[lo, 1 - par, cols], in0=pm[lo, i % 2], scalar=SCALE,
                                                     in1=QS[lo, 1 - par, cols], op0=ALU.mult, op1=ALU.subtract).then_inc(reduced.sem, 1)

                    def use_ring(g, i, par):
                        what, c, r = ring[i]
                        if what == "project":
                            low(g, i, par)
                            return
                        dve.wait_ge(scored.sem, scored.after(g, i + 1))
                        if what == "row":
                            dve.tensor_scalar(QS[MR:KR, parity_of(i, par), c * CW:(c + 1) * CW], pm[0:1, i % 2, 0:CW], -1.0, None,
                                              ALU.mult).then_inc(reduced.sem, 1)
                            return
                        t, w, a0, a1 = piece(c, r)
                        dve.tensor_reduce(mx[:, c % 2, t, w:w + 1], pm[:, i % 2, 0:a1 - a0], AX.X, ALU.max).then_inc(reduced.sem, 1)
                        if i == last_piece[c]:
                            at = [x for x in rows if ring[x][1] == c][0]
                            over = 0
                            if at < i:
                                over = 1
                            nth = row_count(at) + over * NC
                            m = mc[:, nth % 2]
                            dve.wait_ge(reduced.sem, reduced.after(g, i + 1))
                            dve.tensor_reduce(m, mx[:, c % 2, :, 0:c // 2 + 1], AX.X, ALU.max).then_inc(mcol.sem, 1)
                            dve.wait_ge(mcol.sem, mcol.after(g, 3 * (nth - 1) - 2))
                            dve.tensor_scalar(m, m, -M16_MAX, M16_MAX, ALU.max, ALU.min).then_inc(mcol.sem, 1)
                            dve.wait_ge(mcol.sem, mcol.after(g, 3 * (nth - 1) - 1))
                            dve.tensor_copy(mh[:, nth % 2], m).then_inc(mcol.sem, 1)

                    def sums_out(g, c, par):
                        dve.wait_ge(used.sem, used.after(g, T0[c + 1]))
                        dve.wait_ge(zin.sem, zin.after(g, c))
                        dve.tensor_tensor(OT[:], po[0:KR], NP[:, par, c * CW:(c + 1) * CW], ALU.mult).then_inc(summed_out.sem, 1)

                    def results(g, e, c):
                        dve.wait_ge(zin.sem, zin.after(g, c + 1))
                        dve.reciprocal(rd[:], pz[:, :, AW]).then_inc(rds, 1)
                        if c == 0:
                            dve.wait_ge(mixed.sem, e_free(e))
                        dve.wait_ge(rds, g * NC + (c + 1))
                        dve.tensor_tensor(ATT[:, bass.ds(e, 1), c * CT:(c + 1) * CT, :], pz[:, :, 0:AW].unsqueeze(1),
                                          rd[:].unsqueeze(2).broadcast_to([P, CT, AW]).unsqueeze(1), ALU.mult).then_inc(zout.sem, 1)

                    for _, i in ahead_plan:
                        use_ring(-1, i, 1)
                    with dve.Fori(0, H) as n:
                        dve.get_value_cache().nocache = True
                        def e_free(e):
                            return n * (2 * E) + e + 1
                        dve.wait_ge(used.sem, used.after(n * E, 0))
                        dve.tensor_scalar(Vc[:].unsqueeze(2), V[:, :, bass.ds(n, 1), :], 1.0, None, ALU.mult).then_inc(values_in.sem, 1)
                        with dve.Fori(0, E // 2) as m:
                            dve.get_value_cache().nocache = True
                            for par in range(2):
                                e = dve.snap(2 * m + par)
                                g = dve.snap(n * E + m * 2 + par)
                                dve.wait_ge(x_in.sem, x_in.after(g, 5 * 16))
                                for what, *args in plan:
                                    if what == "ring":
                                        use_ring(g, *args, par)
                                    elif what == "sums_out":
                                        sums_out(g, *args, par)
                                    elif what == "results":
                                        results(g, e, *args)

                        ch = Chain(dve, steps, n, 6)
                        dve.wait_ge(zout.sem, zout.after(n * E + (E - 1), NC))
                        ch.link(dve.tensor_reduce(lg[:], ATT[:, :, :, DH:AW].rearrange("p e t x -> p t x e"), AX.X, ALU.add))
                        ch.link(dve.tensor_tensor(lg[:], lg[:], gb[:, bass.ds(n, 1), :].broadcast_to([P, NT, E]), ALU.add))
                        emit_softmax4(dve, ch, lg[:], sm[:], e_in, e_out, n)
                        assert ch.k == 6, ch.k
                        dve.sem_inc(gates.sem, 1)


def emit_layernorm_heads(dve, chain, src, dst, sq, st, gb, eps, std_in, std_out, turn):
    s = [st[:, i] for i in range(5)]
    v = lambda x: x.rearrange("p t (h d) -> p (t h) d", h=F_HEADS)
    src, dst, sq = v(src), v(dst), v(sq)
    shape = [P, NT * F_HEADS, F_DH]

    def wide(a):
        return a.unsqueeze(2).broadcast_to(shape)

    chain.link(dve.tensor_reduce(s[0], src, AX.X, ALU.add))
    chain.link(dve.tensor_scalar(s[0], s[0], 1.0 / F_DH, None, ALU.mult))
    chain.link(dve.tensor_tensor(dst, src, wide(s[0]), ALU.subtract))
    chain.link(dve.tensor_tensor(sq, dst, dst, ALU.mult))
    chain.link(dve.tensor_reduce(s[1], sq, AX.X, ALU.add))
    dve.tensor_scalar(s[1], s[1], 1.0 / F_DH, eps, ALU.mult, ALU.add).then_inc(std_in, 1)
    dve.wait_ge(std_out, turn + 1)
    chain.link(dve.reciprocal(s[3], s[2]))
    chain.link(dve.tensor_tensor(s[4], s[3], s[3], ALU.mult))
    chain.link(dve.tensor_tensor(s[4], s[4], s[1], ALU.mult))
    chain.link(dve.tensor_scalar(s[4], s[4], -0.5, 1.5, ALU.mult, ALU.add))
    chain.link(dve.tensor_tensor(s[3], s[3], s[4], ALU.mult))
    chain.link(dve.tensor_tensor(dst, dst, wide(s[3]), ALU.mult))
    chain.link(dve.tensor_tensor(dst, dst, gb[:, 0:1, :].broadcast_to(shape), ALU.mult))
    chain.link(dve.tensor_tensor(dst, dst, gb[:, 1:2, :].broadcast_to(shape), ALU.add))


def stage_feed_forward(k, a, SX, MIX):
    nc = k.nc
    with ExitStack() as ctx:
        FN = k.sb(ctx, "ff_FN", [P, NT, D], F32)
        B = k.sb(ctx, "ff_B", [P, NT, D], F32)
        FT = k.sb(ctx, "ff_FT", [P, N], F32)
        H1 = k.sb(ctx, "ff_H1", [P, N], F32)
        st = k.sb(ctx, "ff_st", [P, 5, NT * F_HEADS], F32)
        ln = k.sb(ctx, "ff_ln", [P, 4, F_DH], F32)
        W1 = k.sb(ctx, "ff_W1", [P, P], F32)
        W2 = k.sb(ctx, "ff_W2", [P, P], F32)
        b1 = k.sb(ctx, "ff_b1", [P, 1], F32)
        b2 = k.sb(ctx, "ff_b2", [P, F_DH], F32)
        fg = k.sb(ctx, "ff_fg", [P, F_HEADS, D], F32)
        lg = k.sb(ctx, "ff_lg", [P, NT, F_HEADS], F32)
        sm = k.sb(ctx, "ff_sm", [P, NT], F32)
        pt = k.ps(ctx, "ff_pt", [P, 2, CW])
        ph = k.ps(ctx, "ff_ph", [P, 2, CW])
        pz = k.ps(ctx, "ff_pz", [P, 2, CT, P])
        loaded, steps, std_in, std_out = k.sem("ff_loaded"), k.sem("ff_steps"), k.sem("ff_std_in"), k.sem("ff_std_out")
        normed, turned, tmoved = k.sem("ff_normed"), k.sem("ff_turned"), k.sem("ff_tmoved")
        hid, relued, masked, outp, omoved = (k.sem("ff_hid"), k.sem("ff_relued"), k.sem("ff_masked"), k.sem("ff_out"),
                                             k.sem("ff_omoved"))
        e_in, e_out = k.sem("ff_exp_in"), k.sem("ff_exp_out")
        with nc.Block() as block:
            @block.sync
            def _(sp):
                for i, name in enumerate(("ln_g", "ln_b", "fnorm_g", "fnorm_b")):
                    sp.dma_start(ln[:, i], a[name].rearrange("(o n) -> o n", o=1).broadcast_to([P, F_DH])).then_inc(loaded, 16)
                sp.dma_start(b2[:], a["fc2_b"].rearrange("(o n) -> o n", o=1).broadcast_to([P, F_DH])).then_inc(loaded, 16)
                sp.dma_start(W1[:], a["fc1B"]).then_inc(loaded, 16)
                sp.dma_start(W2[:], a["fc2B"]).then_inc(loaded, 16)
                sp.dma_start(b1[:], a["fc1b"]).then_inc(loaded, 16)
                sp.dma_start(fg[:], a["fgate_w"].rearrange("h n -> (h n)").rearrange("(o n) -> o n", o=1)
                             .broadcast_to([P, F_HEADS * D]).rearrange("p (h n) -> p h n", h=F_HEADS)).then_inc(loaded, 16)

            @block.tensor
            def _(pe):
                pe.wait_ge(normed, 1)
                pe.wait_ge(loaded, 16 * 9)
                for c in range(NC + 2):
                    if c < NC:
                        if c >= 2:
                            pe.wait_ge(tmoved, c - 1)
                        for t in range(CT):
                            mm = nc.tensor.matmul(pt[:, c % 2, t * P:(t + 1) * P], FN[:, c * CT + t], k.ident[:], start=(t == 0),
                                                  stop=True, skip_group_check=True)
                        mm.then_inc(turned, 1)
                    if 1 <= c <= NC:
                        i = c - 1
                        pe.wait_ge(tmoved, i + 1)
                        if i >= 2:
                            pe.wait_ge(relued, i - 1)
                        nc.tensor.matmul(ph[:, i % 2], W1[:], FT[:, i * CW:(i + 1) * CW], start=True, stop=True).then_inc(hid, 1)
                    if c >= 2:
                        i = c - 2
                        pe.wait_ge(masked, i + 1)
                        if i >= 2:
                            pe.wait_ge(omoved, i - 1)
                        for t in range(CT):
                            j = i * CT + t
                            mm = nc.tensor.matmul(pz[:, i % 2, t], H1[:, j * P:(j + 1) * P], W2[:], start=(t == 0), stop=True,
                                                  skip_group_check=True)
                        mm.then_inc(outp, 1)

            @block.scalar
            def _(act):
                act.wait_ge(std_in, 1)
                nc.scalar.activation(st[:, 2], st[:, 1], ACT.Sqrt).then_inc(std_out, 1)
                act.wait_ge(loaded, 16 * 9)
                for c in range(NC + 1):
                    if c < NC:
                        act.wait_ge(turned, c + 1)
                        nc.scalar.activation(FT[:, c * CW:(c + 1) * CW], pt[:, c % 2], ACT.Copy).then_inc(tmoved, 1)
                    if c >= 1:
                        i = c - 1
                        act.wait_ge(hid, i + 1)
                        nc.scalar.activation(H1[:, i * CW:(i + 1) * CW], ph[:, i % 2], ACT.Relu, bias=b1[:]).then_inc(relued, 1)
                act.wait_ge(std_in, 2)
                nc.scalar.activation(st[:, 2], st[:, 1], ACT.Sqrt).then_inc(std_out, 1)
                act.wait_ge(e_in, 1)
                nc.scalar.activation(lg[:], lg[:], ACT.Exp).then_inc(e_out, 1)

            @block.vector
            def _(dve):
                ch = Chain(dve, steps)
                dve.wait_ge(loaded, 16 * 9)
                ch.link(dve.tensor_tensor(MIX[:], MIX[:], SX[:], ALU.add))
                emit_layernorm_heads(dve, ch, MIX[:], FN[:], B[:], st, ln[:, 0:2], 1e-8, std_in, std_out, 0)
                dve.sem_inc(normed, 1)
                for c in range(NC + 1):
                    if c < NC:
                        cols = slice(c * CW, (c + 1) * CW)
                        dve.wait_ge(relued, c + 1)
                        dve.scalar_tensor_tensor(out=H1[:, cols], in0=FT[:, cols], scalar=0.0, in1=H1[:, cols],
                                                 op0=ALU.not_equal, op1=ALU.mult).then_inc(masked, 1)
                    if c >= 1:
                        i = c - 1
                        dve.wait_ge(outp, i + 1)
                        v = lambda x: x.rearrange("p t (h d) -> p t h d", h=F_HEADS)
                        dve.tensor_tensor(v(B[:, i * CT:(i + 1) * CT]), v(pz[:, i % 2]),
                                          b2[:].unsqueeze(1).unsqueeze(1).broadcast_to([P, CT, F_HEADS, F_DH]),
                                          ALU.add).then_inc(omoved, 1)
                dve.wait_ge(omoved, NC)
                ch.link(dve.scalar_tensor_tensor(out=B[:], in0=FN[:], scalar=0.0, in1=B[:], op0=ALU.not_equal, op1=ALU.mult))
                ch.link(dve.tensor_tensor(B[:], B[:], FN[:], ALU.add))
                emit_layernorm_heads(dve, ch, B[:], FN[:], MIX[:], st, ln[:, 2:4], 1e-8, std_in, std_out, 1)
                for h in range(F_HEADS):
                    ch.link(dve.tensor_tensor(B[:], FN[:], fg[:, h:h + 1].broadcast_to([P, NT, D]), ALU.mult))
                    ch.link(dve.tensor_reduce(lg[:, :, h], B[:], AX.X, ALU.add))
                emit_softmax4(dve, ch, lg[:], sm[:], e_in, e_out)
                v = lambda x: x.rearrange("p t (h d) -> p (t h) d", h=F_HEADS)
                ch.link(dve.tensor_tensor(v(B[:]), v(FN[:]), lg[:].rearrange("p t h -> p (t h)").unsqueeze(2)
                                          .broadcast_to([P, NT * F_HEADS, F_DH]), ALU.mult))
                ch.link(dve.tensor_tensor(k.X[:], k.X[:], B[:], ALU.add))


def lay_out(inputs):
    import numpy as np
    get = {n: np.ascontiguousarray(np.asarray(v)) for n, v in inputs.items()}
    r = {"x": get["x"], "adj": get["adj"]}
    for n in ("inlayer2", "W", "b", "w1", "b1", "w2", "b2"):
        r[n] = get["L0_gnn_" + n]
    for n in ("sW1", "sb1", "sW2", "sb2", "sW3", "sb3", "eW1", "eW2", "eW3", "eb3", "gW", "gb"):
        r[n] = get["L0_ffn_" + n]
    for n in ("eb1", "eb2"):
        r[n + "T"] = np.ascontiguousarray(get["L0_ffn_" + n].T)
    for n in ("Wq", "Wk", "Wv", "weightr", "weightd", "bias"):
        r[n] = get["L1_gnn_" + n]
    f = {n[7:]: v for n, v in get.items() if n.startswith("L1_ffn_")}
    r["hlT"] = np.ascontiguousarray(f["hl_w"].reshape(D, D).T)
    r["hlb"] = f["hl_b"].reshape(D, 1)
    wqk = np.zeros((3 * F_DH, F_HEADS, 1 + F_EXP, 3 * F_DH), np.float32)
    for name in ("wvB", "fc1B", "fc2B"):
        r[name] = np.zeros((D, D), np.float32)
    for h in range(F_HEADS):
        rows = slice(h * F_DH, (h + 1) * F_DH)
        wqk[:, h, 0] = np.tile(f["wk"][h].T, (3, 3))
        for e in range(F_EXP):
            wqk[:, h, 1 + e] = np.tile(f["wq"][h, e].T, (3, 3))
        r["wvB"][rows, rows] = f["wv"][h].T
        r["fc1B"][rows, rows] = f["fc1_w"].T
        r["fc2B"][rows, rows] = f["fc2_w"].T
    r["wqk"] = wqk
    width = F_DH + N_EXP + 1
    two = np.zeros((3 * F_DH + 1, F_HEADS * F_EXP * width + P), np.float32)
    for turn in range(F_HEADS * F_EXP):
        h, e = divmod(turn, F_EXP)
        for i in (0, 64):
            block = two[i:i + F_DH + 1, turn * width:(turn + 1) * width]
            block[:F_DH, :F_DH] = np.eye(F_DH, dtype=np.float32)
            block[:F_DH, F_DH:F_DH + N_EXP] = f["gate_w"][h][:, e * F_DH:(e + 1) * F_DH].T
            block[F_DH, F_DH + N_EXP] = 1.0
    r["two"] = two
    r["fc1b"] = np.tile(f["fc1_b"], F_HEADS).reshape(D, 1)
    for n in ("gate_b", "ln_g", "ln_b", "fnorm_g", "fnorm_b", "fc2_b", "fgate_w"):
        r[n] = f[n]
    return r


def kernel(**inputs):
    import concourse.bacc as _bacc
    from concourse import mybir as _mybir
    from concourse.bass_utils import run_bass_kernel_spmd as _run

    nc = _bacc.Bacc("TRN2", target_bir_lowering=False, num_devices=1)
    arrays, args = {}, {}
    for name, arr in lay_out(inputs).items():
        arrays[f"in_{name}"] = arr
        args[name] = nc.dram_tensor(f"in_{name}", arr.shape, _mybir.dt.from_np(arr.dtype), kind="ExternalInput").ap()
    out = nc.dram_tensor("out_x", (N, D), F32, kind="ExternalOutput").ap()
    build(nc, args, out)
    res = _run(nc, [arrays], core_ids=[0])
    return res.results[0]["out_x"]
```

```python
from contextlib import ExitStack

import concourse.bass as bass
from concourse import mybir

ALU = mybir.AluOpType
ACT = mybir.ActivationFunctionType
AX = mybir.AxisListType
F32 = mybir.dt.float32
BF16 = mybir.dt.bfloat16
F16 = mybir.dt.float16
I32 = mybir.dt.int32

P = 128
N = 4096
D = 128
NT = N // P
CT = 4
CW = CT * P
NC = N // CW
HALF = N // 2
SLOPE = 0.01
BIG = 2.0 ** 60
FLOOR = -(2.0 ** 40)
M16_MAX = 60000.0
G_HEADS, G_DH = 2, 64
F_HEADS, F_EXP, F_DH = 4, 4, 32
S_HIDDEN, E_HIDDEN, N_EXP = 128, 64, 4


class Count:

    def __init__(self, sem, per=0, credit=0):
        self.sem, self.per, self.credit = sem, per, credit

    def after(self, turn, k):
        return turn * self.per + (self.credit + k)


class Chain:

    def __init__(self, eng, sem, turn=0, per=0):
        self.eng, self.sem, self.base, self.k, self.per = eng, sem, turn * per, 0, per

    def link(self, ins):
        self.k += 1
        ins.then_inc(self.sem, 1)
        self.eng.wait_ge(self.sem, self.base + self.k)


class Core:

    def __init__(self, nc, ctx):
        self.nc, self.ctx = nc, ctx
        self.X = self.sb(ctx, "X", [P, NT, D], F32)
        self.ident = self.sb(ctx, "ident", [P, P], F32)
        self.identb = self.sb(ctx, "identb", [P, P], BF16)
        self.negbig = self.sb(ctx, "negbig", [P, P], BF16)
        self.ones = self.sb(ctx, "ones", [P, P], F32)

    def sb(self, ctx, name, shape, dt):
        return ctx.enter_context(self.nc.sbuf_tensor(name, shape, dt))

    def ps(self, ctx, name, shape, dt=F32):
        return ctx.enter_context(self.nc.psum_tensor(name, shape, dt))

    def sem(self, name):
        return self.ctx.enter_context(self.nc.semaphore(name))


def stage_constants(k, x):
    nc = k.nc
    x_in, zeroed, made = k.sem("x_in"), k.sem("const_zeroed"), k.sem("const_made")
    with nc.Block() as block:
        @block.sync
        def _(sp):
            sp.dma_start(k.X[:], x.rearrange("(t p) f -> p t f", p=P)).then_inc(x_in, 16)
            sp.wait_ge(x_in, 16)

        @block.gpsimd
        def _(pool):
            pool.memset(k.ones[:], 1.0).then_inc(made, 1)
            for m in (k.ident, k.identb, k.negbig):
                pool.memset(m[:], 0.0).then_inc(zeroed, 1)
            pool.wait_ge(zeroed, 3)
            for m, fill in ((k.ident, 1.0), (k.identb, 1.0), (k.negbig, -BIG)):
                pool.affine_select(out=m[:], in_=m[:], compare_op=ALU.not_equal, fill=fill, base=0,
                                   pattern=[[-1, P]], channel_multiplier=1).then_inc(made, 1)


def stage_layernorm(k, tag, Y, YT=None, load=None):
    nc = k.nc
    EPS = 1e-5
    with ExitStack() as ctx:
        bn = k.sb(ctx, f"{tag}_bn", [P, NT, 6], F32)
        st = k.sb(ctx, f"{tag}_st", [P, 5, NT], F32)
        pt = k.ps(ctx, f"{tag}_pt", [P, 2, CW])
        stats, steps, var_in, std_out = (k.sem(f"{tag}_stats"), k.sem(f"{tag}_steps"), k.sem(f"{tag}_var"),
                                         k.sem(f"{tag}_std"))
        y_done, turned, moved = k.sem(f"{tag}_y_done"), k.sem(f"{tag}_turned"), k.sem(f"{tag}_moved")
        mean, var, std, rstd, tmp = (st[:, i] for i in range(5))
        with nc.Block() as block:
            if load is not None:
                @block.sync
                def _(sp):
                    load(sp)

            @block.vector
            def _(dve):
                ch = Chain(dve, steps)
                for t in range(NT):
                    dve.bn_stats(bn[:, t], k.X[:, t]).then_inc(stats, 1)
                dve.wait_ge(stats, NT)
                ch.link(dve.tensor_tensor(mean, bn[:, :, 1], bn[:, :, 4], ALU.add))
                ch.link(dve.tensor_scalar(mean, mean, 0.5, None, ALU.mult))
                ch.link(dve.tensor_tensor(tmp, bn[:, :, 1], mean, ALU.subtract))
                ch.link(dve.tensor_tensor(tmp, tmp, tmp, ALU.mult))
                ch.link(dve.tensor_scalar(tmp, tmp, EPS, None, ALU.add))
                ch.link(dve.tensor_tensor(var, bn[:, :, 2], bn[:, :, 5], ALU.add))
                dve.scalar_tensor_tensor(out=var, in0=var, scalar=1.0 / D, in1=tmp, op0=ALU.mult, op1=ALU.add).then_inc(var_in, 1)
                dve.wait_ge(std_out, 1)
                ch.link(dve.reciprocal(rstd, std))
                ch.link(dve.tensor_tensor(tmp, rstd, rstd, ALU.mult))
                ch.link(dve.tensor_tensor(tmp, tmp, var, ALU.mult))
                ch.link(dve.tensor_scalar(tmp, tmp, -0.5, 1.5, ALU.mult, ALU.add))
                ch.link(dve.tensor_tensor(rstd, rstd, tmp, ALU.mult))
                for t in range(NT):
                    dve.tensor_scalar(Y[:, t], k.X[:, t], mean[:, t:t + 1], rstd[:, t:t + 1], ALU.subtract,
                                      ALU.mult).then_inc(y_done, 1)

            @block.scalar
            def _(act):
                act.wait_ge(var_in, 1)
                nc.scalar.activation(std, var, ACT.Sqrt).then_inc(std_out, 1)
                if YT is not None:
                    for c in range(NC):
                        act.wait_ge(turned, c + 1)
                        nc.scalar.activation(YT[:, c * CW:(c + 1) * CW], pt[:, c % 2], ACT.Copy).then_inc(moved, 1)

            if YT is not None:
                @block.tensor
                def _(pe):
                    for c in range(NC):
                        pe.wait_ge(y_done, (c + 1) * CT)
                        if c >= 2:
                            pe.wait_ge(moved, c - 1)
                        for t in range(CT):
                            mm = nc.tensor.matmul(pt[:, c % 2, t * P:(t + 1) * P], Y[:, c * CT + t, :],
                                                  k.ident[:], start=(t == 0), stop=True, skip_group_check=True)
                        mm.then_inc(turned, 1)


def stage_gat_vectors(k, g, a):
    nc = k.nc
    with ExitStack() as ctx:
        in2 = k.sb(ctx, "in2", [P, NT, D], F32)
        sq = k.sb(ctx, "in2_sq", [P, NT, D], F32)
        W = k.sb(ctx, "gat_W", [P, D], F32)
        cols = k.sb(ctx, "gat_cols", [P, 5], F32)
        Ab = k.sb(ctx, "gat_Ab", [P, 2, D], F32)
        kap = k.sb(ctx, "gat_kap", [P, 2], F32)
        pA = k.ps(ctx, "gat_pA", [P, 2, D])
        pk = k.ps(ctx, "gat_pk", [P, 2])
        pF = k.ps(ctx, "gat_pF", [P, 2, CW])
        pS = k.ps(ctx, "gat_pS", [P, D + 1])
        loaded, steps, prod = k.sem("gatv_loaded"), k.sem("gatv_steps"), k.sem("gatv_A_done")
        f_done, rows, moved, summed = k.sem("gatv_f"), k.sem("gatv_rows"), k.sem("gatv_moved"), k.sem("gatv_sum")
        sv_done, filled = k.sem("gatv_sv"), k.sem("gatv_filled")

        def load(sp):
            sp.dma_start(W[:], a["W"]).then_inc(loaded, 16)
            for i, v in enumerate((a["w1"], a["w2"], a["b"])):
                sp.dma_start(cols[:, i:i + 1], v.rearrange("(p o) -> p o", o=1)).then_inc(loaded, 16)
            for i, v in enumerate((a["b1"], a["b2"])):
                sp.dma_start(cols[:, 3 + i:4 + i], v.rearrange("(o p) -> o p", o=1).broadcast_to([P, 1])).then_inc(loaded, 16)
            sp.dma_start(in2[:], a["inlayer2"].rearrange("(t p) f -> p t f", p=P)).then_inc(loaded, 16)

        stage_layernorm(k, "ln0", g.V[:, :, 0:D], load=load)
        with nc.Block() as block:
            @block.gpsimd
            def _(pool):
                pool.memset(g.row0[:], 0.0).then_inc(filled, 1)
                pool.wait_ge(filled, 1)
                pool.memset(g.row0[0:1, :], 1.0).then_inc(filled, 1)
                pool.memset(g.V[:, :, D:D + 1], 1.0).then_inc(filled, 1)

            @block.tensor
            def _(pe):
                pe.wait_ge(loaded, 16 * 7)
                for i in range(2):
                    w = cols[:, i:i + 1].broadcast_to([P, P])
                    nc.tensor.matmul(pA[:, i], w, W[:], start=(i == 0), stop=True, skip_group_check=True)
                for i in range(2):
                    w = cols[:, i:i + 1].broadcast_to([P, P])
                    mm = nc.tensor.matmul(pk[:, i:i + 1], w, cols[:, 2:3], start=(i == 0), stop=True, skip_group_check=True)
                mm.then_inc(prod, 1)
                pe.wait_ge(filled, 3)
                for t in range(NT):
                    mm = nc.tensor.matmul(pS[:], k.ones[:], g.V[:, t, :], start=(t == 0), stop=(t == NT - 1))
                mm.then_inc(summed, 1)
                for i in range(2):
                    pe.wait_ge(f_done, i + 1)
                    for c in range(NC):
                        n = i * NC + c
                        if n >= 2:
                            pe.wait_ge(moved, n - 1)
                        for t in range(CT):
                            f = g.fcol[:, i, c * CT + t:c * CT + t + 1].broadcast_to([P, P])
                            mm = nc.tensor.matmul(pF[:, n % 2, t * P:(t + 1) * P], f, k.ident[:],
                                                  start=(t == 0), stop=True, skip_group_check=True)
                        mm.then_inc(rows, 1)

            @block.scalar
            def _(act):
                for i, dst in enumerate((g.f1row, g.f2row)):
                    for c in range(NC):
                        n = i * NC + c
                        act.wait_ge(rows, n + 1)
                        nc.scalar.activation(dst[:, c * CW:(c + 1) * CW], pF[:, n % 2], ACT.Copy).then_inc(moved, 1)

            @block.vector
            def _(dve):
                ch = Chain(dve, steps)
                dve.wait_ge(prod, 1)
                ch.link(dve.tensor_copy(Ab[:], pA[:]))
                ch.link(dve.tensor_tensor(kap[:], pk[:], cols[:, 3:5], ALU.add))
                dve.wait_ge(loaded, 16 * 7)
                for i in range(2):
                    w = Ab[:, i:i + 1, :].broadcast_to([P, NT, D])
                    ch.link(dve.tensor_tensor(sq[:], in2[:], w, ALU.mult))
                    ch.link(dve.tensor_reduce(g.fcol[:, i], sq[:], AX.X, ALU.add))
                    dve.tensor_scalar(g.fcol[:, i], g.fcol[:, i], kap[:, i:i + 1], None, ALU.add).then_inc(f_done, 1)
                dve.wait_ge(f_done, 2)
                ch.link(dve.tensor_scalar(g.f2s[:, 0], g.fcol[:, 1], SLOPE, None, ALU.mult))
                ch.link(dve.tensor_scalar(g.f2s[:, 1], g.fcol[:, 1], 1 - SLOPE, None, ALU.mult))
                dve.wait_ge(summed, 1)
                dve.tensor_copy(g.sumV[:], pS[:]).then_inc(sv_done, 1)


def stage_gat(k, g, adj):
    nc = k.nc
    QW = N // 4
    QN = 4 * CT
    AS = 4
    TS = 2
    LS = 4
    PSL = 4
    LAG = 3
    RING = QN + 2
    with ExitStack() as ctx:
        A = k.sb(ctx, "gat_adj", [P, AS, QW], I32)
        NM = k.sb(ctx, "gat_nm", [P, 2, CT, N], BF16)
        L = k.sb(ctx, "gat_logits", [P, LS, CW], F32)
        Pr = k.sb(ctx, "gat_probs", [P, PSL, CW], F32)
        f1c = k.sb(ctx, "gat_f1c", [P, 2, CW], F32)
        mx = k.sb(ctx, "gat_mx", [P, CT, 4], F32)
        m4 = k.sb(ctx, "gat_m4", [P, 4, CT], F32)
        ecol = k.sb(ctx, "gat_ecol", [P, CT], F32)
        erow = k.sb(ctx, "gat_erow", [1, 2, CW], F32)
        Mrow = k.sb(ctx, "gat_Mrow", [P, 2, CW], BF16)
        rd = k.sb(ctx, "gat_rd", [P, CT], F32)
        pm = k.ps(ctx, "gat_pm", [P, 2, QW])
        pt = k.ps(ctx, "gat_pt", [P, TS, CW])
        po = k.ps(ctx, "gat_po", [P, CT, 2 * P])

        adj_in = [k.sem(f"gat_adj_in{s}") for s in range(AS)]
        converted = Count(k.sem("gat_converted"), QN, AS)
        biased = Count(k.sem("gat_biased"), RING)
        reduced = Count(k.sem("gat_reduced"), RING, 2)
        mcol = Count(k.sem("gat_mcol"), 1)
        steps = k.sem("gat_steps")
        rsteps = k.sem("gat_rsteps")
        f1_here = Count(k.sem("gat_f1_here"), 1)
        masked = Count(k.sem("gat_masked"), NT)
        logits = Count(k.sem("gat_logits_done"), NT)
        summed = Count(k.sem("gat_added"), NT, TS)
        probs = Count(k.sem("gat_probs_done"), NT, LS)
        used = Count(k.sem("gat_probs_used"), NT, PSL)
        out_done = Count(k.sem("gat_out"), 1)
        out_moved = Count(k.sem("gat_out_moved"), CT, CT)

        def chunk_plan(prepare):
            plan = []
            for j in range(NT):
                plan += [(j, "mask", j), (j + LAG + 0.2, "values", j)]
            plan += [(NT - 1 + LAG + 0.3, "finish", 0)]
            if prepare:
                step = (NT + 0.0) / RING
                for q in range(QN):
                    plan += [((q + 0.1) * step, "convert", q), ((q + 1.0) * step, "piece", q)]
                plan += [(NT - 1.5, "row", 0), (NT - 0.5, "row", 1)]
            return [p[1:] for p in sorted(plan, key=lambda p: p[0])]

        with nc.Block() as block:
            @block.sync
            def _(sp):
                with sp.Fori(0, NC) as c:
                    for q in range(QN):
                        t, w, s = q // 4, q % 4, q % AS
                        sp.wait_ge(converted.sem, converted.after(c, q + 1 - AS))
                        sp.dma_start(A[:, s], adj[bass.ds((c * CT + t) * P, P), w * QW:(w + 1) * QW]).then_inc(adj_in[s], 16)

            @block.vector
            def _(dve):
                dve.sem_inc(converted.sem, AS)
                dve.sem_inc(reduced.sem, 2)
                dve.sem_inc(summed.sem, TS)
                dve.sem_inc(out_moved.sem, CT)

                def convert(c, q, par):
                    t, w, s = q // 4, q % 4, q % AS
                    dve.wait_ge(adj_in[s], 16 * (c * (QN // AS) + (q // AS + 1)))
                    dve.tensor_scalar(NM[:, par, t, w * QW:(w + 1) * QW], A[:, s], 0.0, None, ALU.is_le).then_inc(converted.sem, 1)

                def piece(c, q):
                    dve.wait_ge(biased.sem, biased.after(c, q + 1))
                    dve.tensor_reduce(mx[:, q // 4, q % 4:q % 4 + 1], pm[:, q % 2], AX.X, ALU.max).then_inc(reduced.sem, 1)
                    if q < QN - 1:
                        return
                    ch = Chain(dve, steps, c, 6)
                    dve.wait_ge(reduced.sem, reduced.after(c, QN))
                    F, z, M, Mn = (m4[:, i] for i in range(4))
                    ch.link(dve.tensor_reduce(F, mx[:], AX.X, ALU.max))
                    ch.link(dve.tensor_scalar(ecol[:], F, -BIG / 2, None, ALU.is_lt))
                    ch.link(dve.tensor_scalar(F, F, FLOOR, None, ALU.max))
                    ch.link(dve.tensor_tensor(z, F, g.fcol[:, 0, bass.ds(c * CT, CT)], ALU.add))
                    ch.link(dve.tensor_scalar(M, z, SLOPE, None, ALU.mult))
                    ch.link(dve.tensor_tensor(M, M, z, ALU.max))
                    dve.scalar_tensor_tensor(out=Mn, in0=g.fcol[:, 0, bass.ds(c * CT, CT)], scalar=SLOPE, in1=M,
                                             op0=ALU.mult, op1=ALU.subtract).then_inc(mcol.sem, 1)

                def row(c, i, par):
                    s = (QN + i) % 2
                    dve.wait_ge(biased.sem, biased.after(c, QN + i + 1))
                    if i == 0:
                        dve.tensor_copy(Mrow[:, par], pm[:, s, 0:CW]).then_inc(reduced.sem, 1)
                        return
                    dve.tensor_copy(erow[:, par], pm[0:1, s, 0:CW]).then_inc(reduced.sem, 1)
                    dve.tensor_scalar(k.lone[:, bass.ds(c * CT, CT)], ecol[:], 1.0, None, ALU.mult).then_inc(rsteps, 1)
                    dve.tensor_scalar(f1c[:, par:par + 1], g.f1row[:, bass.ds(c * CW, CW)].unsqueeze(1), 1.0, None,
                                      ALU.mult).then_inc(f1_here.sem, 1)

                def chunk(c, par, prepare):
                    for what, i in chunk_plan(prepare):
                        if what == "mask":
                            s = i % TS
                            dve.wait_ge(masked.sem, masked.after(c, i + 1))
                            dve.wait_ge(logits.sem, logits.after(c, i + 1))
                            dve.tensor_tensor(L[:, i % LS], pt[:, s], L[:, i % LS], ALU.add).then_inc(summed.sem, 1)
                        elif what == "convert":
                            convert(c + 1, i, 1 - par)
                        elif what == "piece":
                            piece(c + 1, i)
                        elif what == "row":
                            row(c + 1, i, 1 - par)
                        elif what == "finish":
                            dve.wait_ge(out_done.sem, out_done.after(c, 1))
                            dve.reciprocal(rd[:], po[:, :, D]).then_inc(rsteps, 1)
                            dve.wait_ge(rsteps, 2 * c + (3 if prepare else 2))
                            for t in range(CT):
                                xt = k.X[:, bass.ds(c * CT + t, 1), :]
                                dve.scalar_tensor_tensor(out=xt, in0=po[:, t:t + 1, 0:D], scalar=rd[:, t:t + 1], in1=xt,
                                                         op0=ALU.mult, op1=ALU.add).then_inc(out_moved.sem, 1)

                for q in range(QN + 1):
                    if q < QN:
                        convert(0, q, 0)
                    if q >= 1:
                        piece(0, q - 1)
                for i in range(2):
                    row(0, i, 0)
                with dve.Fori(0, NC // 2 - 1) as m:
                    dve.get_value_cache().nocache = True
                    for par in range(2):
                        chunk(dve.snap(2 * m + par), par, True)
                chunk(NC - 2, 0, True)
                chunk(NC - 1, 1, False)

            @block.scalar
            def _(act):
                act.sem_inc(probs.sem, LS)

                def chunk(c, par):
                    def logit(j):
                        act.wait_ge(probs.sem, probs.after(c, j + 1 - LS))
                        if j == 0:
                            act.wait_ge(f1_here.sem, f1_here.after(c, 1))
                        nc.scalar.activation(L[:, j % LS], f1c[:, par], ACT.Relu, bias=g.f2s[:, 1, j:j + 1],
                                             scale=1 - SLOPE).then_inc(logits.sem, 1)

                    logit(0)
                    for j in range(NT):
                        if j + 1 < NT:
                            logit(j + 1)
                        act.wait_ge(summed.sem, summed.after(c, j + 1))
                        act.wait_ge(used.sem, used.after(c, j + 1 - PSL))
                        nc.scalar.activation(Pr[:, j % PSL], L[:, j % LS], ACT.Exp,
                                             bias=g.f2s[:, 0, j:j + 1]).then_inc(probs.sem, 1)

                with act.Fori(0, NC // 2) as m:
                    act.get_value_cache().nocache = True
                    for par in range(2):
                        chunk(act.snap(2 * m + par), par)

            @block.tensor
            def _(pe):
                pe.sem_inc(used.sem, PSL)

                def piece(c, q, par):
                    t, w = q // 4, q % 4
                    pe.wait_ge(converted.sem, converted.after(c, q + 1))
                    pe.wait_ge(reduced.sem, reduced.after(c, q + 1 - 2))
                    for h in range(2):
                        o = w * QW + h * CW
                        dst = pm[:, q % 2, h * CW:(h + 1) * CW]
                        nc.tensor.matmul(dst, k.negbig[:], NM[:, par, t, o:o + CW], start=True, stop=False)
                        mm = nc.tensor.matmul(dst, g.row0[:], g.f2row[:, o:o + CW], start=False, stop=True)
                    mm.then_inc(biased.sem, 1)

                def row(c, i):
                    s = (QN + i) % 2
                    pe.wait_ge(mcol.sem, mcol.after(c, 1))
                    pe.wait_ge(reduced.sem, reduced.after(c, QN + i + 1 - 2))
                    for t in range(CT):
                        cols = slice(t * P, (t + 1) * P)
                        if i == 0:
                            mm = nc.tensor.matmul(pm[:, s, cols], m4[:, 3, t:t + 1].broadcast_to([P, P]), k.ident[:],
                                                  start=(t == 0), stop=True, skip_group_check=True)
                        else:
                            mm = nc.tensor.matmul(pm[0:1, s, cols], ecol[:, t:t + 1], k.ident[:], start=(t == 0), stop=True,
                                                  skip_group_check=True)
                    mm.then_inc(biased.sem, 1)

                def mask(c, j, par):
                    pe.wait_ge(summed.sem, summed.after(c, j + 1 - TS))
                    if j == 0:
                        pe.wait_ge(reduced.sem, reduced.after(c, RING))
                    nc.tensor.matmul(pt[:, j % TS], g.row0[:], Mrow[:, par], start=True, stop=False, skip_group_check=True)
                    for t in range(CT):
                        mm = nc.tensor.matmul(pt[:, j % TS, t * P:(t + 1) * P], NM[:, par, t, j * P:(j + 1) * P], k.negbig[:],
                                              start=False, stop=(t == CT - 1), skip_group_check=True)
                    mm.then_inc(masked.sem, 1)

                def values(c, i):
                    pe.wait_ge(probs.sem, probs.after(c, i + 1))
                    if i == 0:
                        pe.wait_ge(out_moved.sem, out_moved.after(c, 0))
                    for t in range(CT):
                        mm = nc.tensor.matmul(po[:, t, 0:D + 1], Pr[:, i % PSL, t * P:(t + 1) * P], g.V[:, i, :],
                                              start=(i == 0 and t % 2 == 0), stop=False, skip_group_check=True)
                    mm.then_inc(used.sem, 1)

                def chunk(c, par, prepare):
                    for what, i in chunk_plan(prepare):
                        if what == "mask":
                            mask(c, i, par)
                        elif what == "values":
                            values(c, i)
                        elif what == "piece":
                            piece(c + 1, i, 1 - par)
                        elif what == "row":
                            row(c + 1, i)
                        elif what == "finish":
                            for t in range(CT):
                                mm = nc.tensor.matmul(po[:, t, 0:D + 1], erow[0:1, par, t * P:(t + 1) * P], g.sumV[0:1, :],
                                                      start=False, stop=True, skip_group_check=True)
                            mm.then_inc(out_done.sem, 1)

                for q in range(QN):
                    piece(0, q, 0)
                for i in range(2):
                    row(0, i)
                with pe.Fori(0, NC // 2 - 1) as m:
                    pe.get_value_cache().nocache = True
                    for par in range(2):
                        chunk(pe.snap(2 * m + par), par, True)
                chunk(NC - 2, 0, True)
                chunk(NC - 1, 1, False)


class Gat:

    def __init__(self, k, ctx):
        self.V = k.sb(ctx, "gat_V", [P, NT, D + 1], F32)
        self.fcol = k.sb(ctx, "gat_fcol", [P, 2, NT], F32)
        self.f1row = k.sb(ctx, "gat_f1row", [P, N], F32)
        self.f2row = k.sb(ctx, "gat_f2row", [P, N], BF16)
        self.row0 = k.sb(ctx, "gat_row0", [P, P], BF16)
        self.sumV = k.sb(ctx, "gat_sumV", [P, D + 1], F32)
        self.f2s = k.sb(ctx, "gat_f2s", [P, 2, NT], F32)


def build(nc, a, out):
    with ExitStack() as top:
        k = Core(nc, top)
        k.lone = k.sb(top, "lone", [P, NT], BF16)
        stage_constants(k, a["x"])
        with ExitStack() as ctx:
            g = Gat(k, ctx)
            stage_gat_vectors(k, g, a)
            stage_gat(k, g, a["adj"])
        with ExitStack() as ctx:
            Y = k.sb(ctx, "moe_Y", [P, NT, D], F32)
            YT = k.sb(ctx, "moe_YT", [P, N], F32)
            stage_moe(k, a, Y, YT)
        stage_graph_attention(k, a)
        with ExitStack() as ctx:
            SX = k.sb(ctx, "sa_SX", [P, NT, D], F32)
            MIX = k.sb(ctx, "sa_MIX", [P, NT, D], F32)
            stage_self_attention(k, a, (SX, MIX))
            stage_feed_forward(k, a, SX, MIX)
        stored = k.sem("stored")
        with nc.Block() as block:
            @block.sync
            def _(sp):
                sp.dma_start(out.rearrange("(t p) f -> p t f", p=P), k.X[:]).then_inc(stored, 16)
                sp.wait_ge(stored, 16)


def emit_softmax4(dve, chain, lg, tmp, exp_in, exp_out, turn=0):
    def wide(a):
        return a.unsqueeze(2).broadcast_to([P, NT, 4])

    chain.link(dve.tensor_reduce(tmp, lg, AX.X, ALU.max))
    dve.tensor_tensor(lg, lg, wide(tmp), ALU.subtract).then_inc(exp_in, 1)
    dve.wait_ge(exp_out, turn + 1)
    chain.link(dve.tensor_reduce(tmp, lg, AX.X, ALU.add))
    chain.link(dve.reciprocal(tmp, tmp))
    chain.link(dve.tensor_tensor(lg, lg, wide(tmp), ALU.mult))


def stage_moe(k, a, Y, YT):
    nc = k.nc
    U = 1 + N_EXP
    with ExitStack() as ctx:
        W1 = k.sb(ctx, "moe_W1", [P, U, P], F32)
        W2 = k.sb(ctx, "moe_W2", [P, U, P], F32)
        W3 = k.sb(ctx, "moe_W3", [P, U, P], F32)
        b1 = k.sb(ctx, "moe_b1", [P, U], F32)
        b2 = k.sb(ctx, "moe_b2", [P, U], F32)
        b3 = k.sb(ctx, "moe_b3", [P, D], F32)
        gW = k.sb(ctx, "moe_gW", [P, N_EXP], F32)
        gb = k.sb(ctx, "moe_gb", [P, N_EXP], F32)
        G = k.sb(ctx, "moe_G", [P, NT, N_EXP], F32)
        sel = k.sb(ctx, "moe_sel", [P, 2, NT, N_EXP], F32)
        coef = k.sb(ctx, "moe_coef", [P, NT, N_EXP], F32)
        sm = k.sb(ctx, "moe_small", [P, 6, NT], F32)
        H1 = k.sb(ctx, "moe_H1", [P, 2, CW], F32)
        H2s = k.sb(ctx, "moe_H2s", [P, CW], F32)
        H2 = k.sb(ctx, "moe_H2", [P, 2, CW], F32)
        cc = k.sb(ctx, "moe_cc", [P, CT, N_EXP], F32)
        loaded, steps, gated = k.sem("moe_loaded"), k.sem("moe_steps"), k.sem("moe_gated")
        exp_in, exp_out = k.sem("moe_exp_in"), k.sem("moe_exp_out")
        w_in, w_out = k.sem("moe_w_in"), k.sem("moe_w_out")
        ones_ok = k.sem("moe_ones")
        h1 = Count(k.sem("moe_h1"), U, 2)
        r1 = Count(k.sem("moe_r1"), U, 2)
        h2 = Count(k.sem("moe_h2"), U, 2)
        r2 = Count(k.sem("moe_r2"), U, 2)
        h3 = Count(k.sem("moe_h3"), U, 2)
        added = Count(k.sem("moe_added"), U, 2)
        steps2 = k.sem("moe_steps2")
        n_loads = 14

        def last_user(u):
            return {0: 0, 1: -1}.get(u, u - 1)

        def hidden2(u):
            return H2s[:] if u == 0 else H2[:, u % 2]

        def rows(u):
            return S_HIDDEN if u == 0 else E_HIDDEN + 1

        def load(sp):
            sp.dma_start(W1[:, 0], a["sW1"]).then_inc(loaded, 16)
            sp.dma_start(W1[:, 1:U], a["eW1"].rearrange("e i o -> i e o")).then_inc(loaded, 16)
            sp.dma_start(W2[:, 0], a["sW2"]).then_inc(loaded, 16)
            sp.dma_start(W2[:, 1:U, 0:E_HIDDEN], a["eW2"].rearrange("e i o -> i e o")).then_inc(loaded, 16)
            sp.dma_start(W3[:, 0], a["sW3"]).then_inc(loaded, 16)
            sp.dma_start(W3[0:E_HIDDEN, 1:U], a["eW3"].rearrange("e i o -> i e o")).then_inc(loaded, 16)
            sp.dma_start(W3[E_HIDDEN:E_HIDDEN + 1, 1:U], a["eb3"].rearrange("(a e) o -> a e o", a=1)).then_inc(loaded, 16)
            sp.dma_start(b1[:, 0:1], a["sb1"].rearrange("(p o) -> p o", o=1)).then_inc(loaded, 16)
            sp.dma_start(b1[:, 1:U], a["eb1T"]).then_inc(loaded, 16)
            sp.dma_start(b2[:, 0:1], a["sb2"].rearrange("(p o) -> p o", o=1)).then_inc(loaded, 16)
            sp.dma_start(b2[0:E_HIDDEN, 1:U], a["eb2T"]).then_inc(loaded, 16)
            sp.dma_start(b3[:], a["sb3"].rearrange("(o n) -> o n", o=1).broadcast_to([P, D])).then_inc(loaded, 16)
            sp.dma_start(gW[:], a["gW"]).then_inc(loaded, 16)
            sp.dma_start(gb[:], a["gb"].rearrange("(o n) -> o n", o=1).broadcast_to([P, N_EXP])).then_inc(loaded, 16)

        stage_layernorm(k, "ln1", Y[:], YT, load)
        p1 = k.ps(ctx, "moe_p1", [P, 2, CW])
        p2 = k.ps(ctx, "moe_p2", [P, 2, CW])
        p3 = k.ps(ctx, "moe_p3", [P, 2, CT, P])
        pg = k.ps(ctx, "moe_pg", [P, NT, N_EXP])
        with nc.Block() as block:
            @block.gpsimd
            def _(pool):
                pool.memset(H2[:], 1.0).then_inc(ones_ok, 1)

            @block.tensor
            def _(pe):
                pe.wait_ge(loaded, 16 * n_loads)
                for t in range(NT):
                    mm = nc.tensor.matmul(pg[:, t], YT[:, t * P:(t + 1) * P], gW[:], start=(t == 0), stop=True,
                                          skip_group_check=True)
                mm.then_inc(gated, 1)
                pe.sem_inc(h1.sem, 2)
                pe.sem_inc(h2.sem, 2)
                pe.sem_inc(h3.sem, 2)
                pe.wait_ge(ones_ok, 1)

                with pe.Fori(0, NC) as c:
                    def first(u):
                        pe.wait_ge(r1.sem, r1.after(c, last_user(u)))
                        nc.tensor.matmul(p1[:, u % 2].unsqueeze(1), W1[:, u], YT[:, bass.ds(c * CW, CW)].unsqueeze(1),
                                         start=True, stop=True).then_inc(h1.sem, 1)

                    def second(u):
                        m = S_HIDDEN if u == 0 else E_HIDDEN
                        pe.wait_ge(r1.sem, r1.after(c, u + 1))
                        pe.wait_ge(r2.sem, r2.after(c, last_user(u)))
                        nc.tensor.matmul(p2[0:m, u % 2], W2[:, u, 0:m], H1[:, u % 2], start=True, stop=True).then_inc(h2.sem, 1)

                    def third(u):
                        pe.wait_ge(r2.sem, r2.after(c, u + 1))
                        pe.wait_ge(added.sem, added.after(c, last_user(u)))
                        for t in range(CT):
                            mm = nc.tensor.matmul(p3[:, u % 2, t], hidden2(u)[0:rows(u), t * P:(t + 1) * P],
                                                  W3[0:rows(u), u], start=(t == 0), stop=True, skip_group_check=True)
                        mm.then_inc(h3.sem, 1)

                    first(0)
                    for u in range(U):
                        if u + 1 < U:
                            first(u + 1)
                        second(u)
                        if u >= 1:
                            third(u - 1)
                    third(U - 1)

            @block.scalar
            def _(act):
                act.wait_ge(exp_in, 1)
                nc.scalar.activation(G[:], G[:], ACT.Exp).then_inc(exp_out, 1)
                act.wait_ge(w_in, 1)
                nc.scalar.activation(sm[:, 3], sm[:, 3], ACT.Exp).then_inc(w_out, 1)
                act.sem_inc(r1.sem, 2)
                act.sem_inc(r2.sem, 2)
                act.wait_ge(ones_ok, 1)
                act.wait_ge(loaded, 16 * n_loads)
                with act.Fori(0, NC) as c:
                    def relu1(u):
                        act.wait_ge(h1.sem, h1.after(c, u + 1))
                        act.wait_ge(h2.sem, h2.after(c, last_user(u)))
                        nc.scalar.activation(H1[:, u % 2], p1[:, u % 2], ACT.Relu, bias=b1[:, u:u + 1]).then_inc(r1.sem, 1)

                    def relu2(u):
                        m = S_HIDDEN if u == 0 else E_HIDDEN
                        act.wait_ge(h2.sem, h2.after(c, u + 1))
                        act.wait_ge(h3.sem, h3.after(c, last_user(u)))
                        nc.scalar.activation(hidden2(u)[0:m], p2[0:m, u % 2], ACT.Relu, bias=b2[0:m, u:u + 1]).then_inc(r2.sem, 1)

                    relu1(0)
                    for u in range(U):
                        if u + 1 < U:
                            relu1(u + 1)
                        relu2(u)

            @block.vector
            def _(dve):
                ch = Chain(dve, steps)
                dve.wait_ge(gated, 1)
                ch.link(dve.tensor_tensor(G[:], pg[:], gb[:].unsqueeze(1).broadcast_to([P, NT, N_EXP]), ALU.add))
                emit_softmax4(dve, ch, G[:], sm[:, 0], exp_in, exp_out)
                free, m1, m2 = sm[:, 5], sm[:, 1], sm[:, 2]
                for r, m in enumerate((m1, m2)):
                    ch.link(dve.tensor_reduce(m, G[:], AX.X, ALU.max))
                    ch.link(dve.memset(free, 1.0))
                    for e in range(N_EXP):
                        s = sel[:, r, :, e]
                        ch.link(dve.tensor_tensor(s, G[:, :, e], m, ALU.is_equal))
                        ch.link(dve.tensor_tensor(s, s, free, ALU.mult))
                        ch.link(dve.tensor_tensor(free, free, s, ALU.subtract))
                    if r == 0:
                        ch.link(dve.scalar_tensor_tensor(out=G[:], in0=sel[:, 0], scalar=-2.0, in1=G[:],
                                                         op0=ALU.mult, op1=ALU.add))
                dve.tensor_tensor(sm[:, 3], m2, m1, ALU.subtract).then_inc(w_in, 1)
                dve.wait_ge(w_out, 1)
                ch.link(dve.tensor_scalar(sm[:, 4], sm[:, 3], 1.0, None, ALU.add))
                ch.link(dve.reciprocal(sm[:, 4], sm[:, 4]))
                ch.link(dve.tensor_tensor(sm[:, 3], sm[:, 3], sm[:, 4], ALU.mult))
                for r, w in ((0, sm[:, 4]), (1, sm[:, 3])):
                    ch.link(dve.tensor_tensor(sel[:, r], sel[:, r], w.unsqueeze(2).broadcast_to([P, NT, N_EXP]), ALU.mult))
                ch.link(dve.tensor_tensor(coef[:], sel[:, 0], sel[:, 1], ALU.add))
                ch.link(dve.tensor_tensor(k.X[:], k.X[:], b3[:].unsqueeze(1).broadcast_to([P, NT, D]), ALU.add))
                dve.sem_inc(added.sem, 2)
                with dve.Fori(0, NC) as c:
                    ch = Chain(dve, steps2, c, 1 + CT * U)
                    ch.link(dve.tensor_scalar(cc[:], coef[:, bass.ds(c * CT, CT), :], 1.0, None, ALU.mult))
                    for u in range(U):
                        dve.wait_ge(h3.sem, h3.after(c, u + 1))
                        for t in range(CT):
                            x = k.X[:, bass.ds(c * CT + t, 1), :]
                            o = p3[:, u % 2, t:t + 1]
                            if u == 0:
                                ins = dve.tensor_tensor(x, o, x, ALU.add)
                            else:
                                ins = dve.scalar_tensor_tensor(out=x, in0=o, scalar=cc[:, t, u - 1:u], in1=x,
                                                               op0=ALU.mult, op1=ALU.add)
                            ch.k += 1
                            ins.then_inc(steps2, 1)
                        dve.wait_ge(steps2, ch.base + ch.k)
                        dve.sem_inc(added.sem, 1)


def stage_graph_attention(k, a):
    nc = k.nc
    H, DH = G_HEADS, G_DH
    QW = N // 4
    QN = 4 * CT
    AS = 2
    PSL = 4
    LAG = 3
    U = H * NT
    KB = DH + 32
    with ExitStack() as outer:
        qA = k.sb(outer, "ga_qA", [P, H, N], F16)
        kA = k.sb(outer, "ga_kA", [P, H, N], F16)
        qB = k.sb(outer, "ga_qB", [KB, H, N], F16)
        kB = k.sb(outer, "ga_kB", [KB, H, N], F16)
        V = k.sb(outer, "ga_V", [P, NT, H, 2 * DH + 1], F16)
        sumV = k.sb(outer, "ga_sumV", [1, H, DH + 1], F32)
        We = k.sb(outer, "ga_We", [DH + 1, 2, H, D + 1], F32)
        We2 = k.sb(outer, "ga_We2", [P, 2, H, D + 1], F32)
        bias = k.sb(outer, "ga_bias", [P, D], F32)
        with ExitStack() as ctx:
            YT = k.sb(ctx, "ga_YT", [P, N], F32)
            Wq = k.sb(ctx, "ga_Wq", [P, H, P], F32)
            Wk = k.sb(ctx, "ga_Wk", [P, H, P], F32)
            Wv = k.sb(ctx, "ga_Wv", [P, D], F32)
            one16 = k.sb(ctx, "ga_one16", [P, 1], F16)
            sums = k.sb(ctx, "ga_sums", [1, H, 2 * DH + 1], F32)
            pp = k.ps(ctx, "ga_pp", [P, 2, CW])
            pv = k.ps(ctx, "ga_pv", [P, 2, CT, H, DH])
            ps = k.ps(ctx, "ga_ps", [1, H, 2 * DH + 1])
            loaded, late, filled = k.sem("ga_loaded"), k.sem("ga_late"), k.sem("ga_filled")
            projected, his, los = k.sem("ga_projected"), k.sem("ga_hi"), k.sem("ga_lo")
            vals, vhigh, vmoved = k.sem("ga_values"), k.sem("ga_vhigh"), k.sem("ga_vmoved")
            vsum, vsum_ok = k.sem("ga_vsum"), k.sem("ga_vsum_ok")
            units = [(h, s, c) for h in range(H) for s in range(2) for c in range(NC)]
            def load(sp):
                for h in range(H):
                    for r in range(2):
                        for W, name in ((Wq, "Wq"), (Wk, "Wk")):
                            sp.dma_start(W[:, h, r * DH:(r + 1) * DH], a[name][:, h * DH:(h + 1) * DH]).then_inc(loaded, 16)
                sp.dma_start(Wv[:], a["Wv"]).then_inc(loaded, 16)
                for s, name in enumerate(("weightr", "weightd")):
                    w = a[name].rearrange("(h i) o -> i h o", h=H)
                    for dst in (We[0:DH], We2[0:DH], We2[DH:P]):
                        sp.dma_start(dst[:, s, :, 0:D], w).then_inc(late, 16)
                sp.dma_start(bias[:], a["bias"].rearrange("(o n) -> o n", o=1).broadcast_to([P, D])).then_inc(late, 16)

            with ExitStack() as inner:
                Y = k.sb(inner, "ga_Y", [P, NT, D], F32)
                stage_layernorm(k, "ln2", Y[:], YT, load)
            with nc.Block() as block:
                @block.sync
                def _(sp):
                    sp.wait_ge(late, 16 * 7)

                @block.gpsimd
                def _(pool):
                    for n, (tile, value) in enumerate((
                            (one16[:], 1.0), (V[:, :, :, 2 * DH:2 * DH + 1], 1.0), (qB[DH:KB], 0.0), (kB[DH:KB], 0.0),
                            (kB[DH:DH + 2], 1.0), (We2[:, :, :, D:D + 1], 0.0), (We[0:DH, :, :, D:D + 1], 0.0),
                            (We[DH:DH + 1, :, :, 0:D], 0.0), (We[DH:DH + 1, :, :, D:D + 1], 1.0))):
                        pool.memset(tile, value).then_inc(filled, 1)
                        pool.wait_ge(filled, n + 1)

                @block.tensor
                def _(pe):
                    pe.wait_ge(loaded, 16 * 9)
                    for n, (h, s, c) in enumerate(units):
                        if n >= 2:
                            pe.wait_ge(los, n - 1)
                        nc.tensor.matmul(pp[:, n % 2], (Wk if s else Wq)[:, h], YT[:, c * CW:(c + 1) * CW],
                                         start=True, stop=True).then_inc(projected, 1)
                    for c in range(NC):
                        if c >= 2:
                            pe.wait_ge(vmoved, c - 1)
                        for t in range(CT):
                            mm = nc.tensor.matmul(pv[:, c % 2, t], YT[:, (c * CT + t) * P:(c * CT + t + 1) * P], Wv[:],
                                                  start=(t == 0), stop=True, skip_group_check=True)
                        mm.then_inc(vals, 1)
                    pe.wait_ge(vmoved, NC)
                    pe.wait_ge(filled, 2)
                    for t in range(NT):
                        mm = nc.tensor.matmul(ps[:], one16[:], V[:, t], start=(t == 0), stop=(t == NT - 1))
                    mm.then_inc(vsum, 1)

                @block.scalar
                def _(act):
                    for n, (h, s, c) in enumerate(units):
                        cols = slice(c * CW, (c + 1) * CW)
                        act.wait_ge(projected, n + 1)
                        if s == 0:
                            nc.scalar.activation(qA[:, h, cols], pp[:, n % 2], ACT.Copy, scale=DH ** -0.5).then_inc(his, 2)
                        else:
                            nc.scalar.activation(kA[:, h, cols], pp[:, n % 2], ACT.Copy).then_inc(his, 1)
                            nc.scalar.activation(kB[0:DH, h, cols], pp[0:DH, n % 2], ACT.Copy).then_inc(his, 1)
                    for c in range(NC):
                        act.wait_ge(vals, c + 1)
                        nc.scalar.activation(V[:, c * CT:(c + 1) * CT, :, DH:2 * DH], pv[:, c % 2], ACT.Copy).then_inc(vhigh, 1)

                @block.vector
                def _(dve):
                    for n, (h, s, c) in enumerate(units):
                        cols = slice(c * CW, (c + 1) * CW)
                        dve.wait_ge(his, 2 * (n + 1))
                        if s == 0:
                            dve.scalar_tensor_tensor(out=qB[0:DH, h, cols], in0=pp[0:DH, n % 2], scalar=DH ** -0.5,
                                                     in1=qA[0:DH, h, cols], op0=ALU.mult, op1=ALU.subtract).then_inc(los, 1)
                        else:
                            dve.tensor_tensor(kA[DH:P, h, cols], pp[DH:P, n % 2], kA[DH:P, h, cols],
                                              ALU.subtract).then_inc(los, 1)
                    for c in range(NC):
                        tiles = slice(c * CT, (c + 1) * CT)
                        dve.wait_ge(vhigh, c + 1)
                        dve.tensor_tensor(V[:, tiles, :, 0:DH], pv[:, c % 2], V[:, tiles, :, DH:2 * DH], ALU.subtract).then_inc(vmoved, 1)
                    dve.wait_ge(vsum, 1)
                    dve.tensor_copy(sums[:], ps[:]).then_inc(vsum_ok, 1)
                    dve.wait_ge(vsum_ok, 1)
                    dve.tensor_copy(sumV[:], sums[:, :, DH:2 * DH + 1]).then_inc(vsum_ok, 1)
                    dve.wait_ge(vsum_ok, 2)
                    dve.tensor_tensor(sumV[:, :, 0:DH], sumV[:, :, 0:DH], sums[:, :, 0:DH], ALU.add).then_inc(vsum_ok, 1)

        with ExitStack() as ctx:
            A = k.sb(ctx, "ga_adj", [P, AS, QW], I32)
            NM = k.sb(ctx, "ga_nm", [P, 2, CT, N], BF16)
            Pr = k.sb(ctx, "ga_probs", [P, PSL, CW], F32)
            Ph = k.sb(ctx, "ga_probs_hi", [P, PSL, CW], F16)
            Pl = k.sb(ctx, "ga_probs_lo", [P, PSL, CW], F16)
            mx = k.sb(ctx, "ga_mx", [P, H, CT, 4], F32)
            mc = k.sb(ctx, "ga_mc", [P, H, CT], F32)
            ms = k.sb(ctx, "ga_ms", [P, H, CT, 2], F16)
            ident16 = k.sb(ctx, "ga_ident16", [P, P], F16)
            uA = k.sb(ctx, "ga_uA", [P, CW], F32)
            uB = k.sb(ctx, "ga_uB", [DH + 1, CW], F32)
            lone = k.sb(ctx, "ga_lone", [1, CW], F32)
            rd = k.sb(ctx, "ga_rd", [P, CT], F32)
            Z = k.sb(ctx, "ga_Z", [P, 2, CT, D], F32)
            pm = k.ps(ctx, "ga_pm", [P, 2, QW])
            pt = k.ps(ctx, "ga_pt", [P, 2, CW])
            poA = k.ps(ctx, "ga_poA", [P, CW])
            poB = k.ps(ctx, "ga_poB", [DH + 1, CW])

            def pieces(h):
                return [("max", h, q) for q in range(QN)]

            def ring_with_next():
                uses = [("row", 1, 0)] + pieces(0) + pieces(1)[:2] + [("row", 0, 0)] + pieces(1)[2:]
                uses.insert(len(uses) // 2 + 4, ("output", 0, 0))
                return uses + [("output", 1, 0)]

            RING = len(ring_with_next())
            AHEAD = RING - 3
            assert RING % 2 == 0
            ahead = pieces(0) + pieces(1)[:2] + [("row", 0, 0)] + pieces(1)[2:]
            last_ring = [("row", 1, 0), ("output", 0, 0), ("output", 1, 0)]

            def chunk_plan(ring):
                plan = []
                for u in range(U):
                    plan += [(u, "scores", u), (u + LAG + 0.2, "values", u)]
                for h in range(H):
                    end = (h + 1) * NT - 1 + LAG
                    plan += [(end + 0.25, "lone", h), (end + 0.3, "sums_out", h)]
                step = (U + 1.0) / RING
                full = len(ring) == RING
                at = 0.0
                for i, (what, h, q) in enumerate(ring):
                    at = max(at, (i + 0.3) * step if full else 0.3)
                    if full and i >= RING - 3:
                        at = max(at, U - 1 + LAG + 0.4)
                    if what == "output":
                        at = max(at, (h + 1) * NT - 1 + LAG + 1.3)
                    plan.append((at, "ring", i))
                    at += 0.01
                for q in range(QN if full else 0):
                    plan.append(((q + 0.1) * step, "convert", q))
                return [p[1:] for p in sorted(plan, key=lambda p: p[0])]

            def slot(i):
                return (AHEAD + i) % 2

            adj_in = [k.sem(f"ga_adj_in{s}") for s in range(AS)]
            converted = Count(k.sem("ga_converted"), QN, AS)
            scored = Count(k.sem("ga_scored"), RING, AHEAD)
            reduced = Count(k.sem("ga_reduced"), RING, 2 + AHEAD)
            mcol = Count(k.sem("ga_mcol"), 4 * H, 4 * H)
            trans = Count(k.sem("ga_trans"), U)
            probs = Count(k.sem("ga_probs_done"), U, 2)
            highs = Count(k.sem("ga_highs"), U, 2)
            lows = Count(k.sem("ga_lows"), U)
            used = Count(k.sem("ga_probs_used"), U, PSL)
            out_done = Count(k.sem("ga_out"), H, 1)
            moved_a = Count(k.sem("ga_moved_a"), H, 1)
            moved_b = Count(k.sem("ga_moved_b"), H, 1)
            steps = k.sem("ga_steps")
            made = k.sem("ga_made")

            with nc.Block() as block:
                @block.sync
                def _(sp):
                    with sp.Fori(0, NC) as c:
                        for q in range(QN):
                            t, w, s = q // 4, q % 4, q % AS
                            sp.wait_ge(converted.sem, converted.after(c, q + 1 - AS))
                            sp.dma_start(A[:, s], a["adj"][bass.ds((c * CT + t) * P, P), w * QW:(w + 1) * QW]).then_inc(adj_in[s], 16)

                @block.gpsimd
                def _(pool):
                    pool.memset(ident16[:], 0.0).then_inc(made, 1)
                    pool.wait_ge(made, 1)
                    pool.affine_select(out=ident16[:], in_=ident16[:], compare_op=ALU.not_equal, fill=1.0, base=0,
                                       pattern=[[-1, P]], channel_multiplier=1).then_inc(made, 1)

                @block.vector
                def _(dve):
                    dve.sem_inc(converted.sem, AS)
                    dve.sem_inc(reduced.sem, 2)
                    dve.sem_inc(moved_b.sem, 1)

                    def convert(c, q, par):
                        t, w, s = q // 4, q % 4, q % AS
                        dve.wait_ge(adj_in[s], 16 * (c * (QN // AS) + (q // AS + 1)))
                        dve.tensor_scalar(NM[:, par, t, w * QW:(w + 1) * QW], A[:, s], 0.0, None,
                                          ALU.is_le).then_inc(converted.sem, 1)

                    def use_ring(c, ring, i, first=0):
                        what, h, q = ring[i]
                        k_ = i + first
                        to = c + 1 if first == 0 else c
                        dve.wait_ge(scored.sem, scored.after(c, k_ + 1))
                        if what == "max":
                            dve.tensor_reduce(mx[:, h, q // 4, q % 4:q % 4 + 1], pm[:, slot(k_)], AX.X, ALU.max).then_inc(reduced.sem, 1)
                            if q == QN - 1:
                                done = 4 * h - (4 * H if first else 0)
                                dve.wait_ge(reduced.sem, reduced.after(c, k_ + 1))
                                dve.tensor_reduce(mc[:, h], mx[:, h], AX.X, ALU.max).then_inc(mcol.sem, 1)
                                dve.wait_ge(mcol.sem, mcol.after(c, done + 1))
                                dve.tensor_scalar(mc[:, h], mc[:, h], -M16_MAX, M16_MAX, ALU.max, ALU.min).then_inc(mcol.sem, 1)
                                dve.wait_ge(mcol.sem, mcol.after(c, done + 2))
                                dve.tensor_copy(ms[:, h, :, 0], mc[:, h]).then_inc(mcol.sem, 1)
                                dve.wait_ge(mcol.sem, mcol.after(c, done + 3))
                                dve.tensor_tensor(ms[:, h, :, 1], mc[:, h], ms[:, h, :, 0], ALU.subtract).then_inc(mcol.sem, 1)
                        elif what == "row":
                            cols = bass.ds((to if h == 0 else c) * CW, CW)
                            if h == 1:
                                dve.tensor_scalar(lone[:], pm[0:1, slot(k_), CW:QW], 1.0, None, ALU.mult).then_inc(steps, 1)
                            dve.tensor_scalar(qB[DH:DH + 2, h:h + 1, cols], pm[0:2, slot(k_):slot(k_) + 1, 0:CW], -1.0, None,
                                              ALU.mult).then_inc(reduced.sem, 1)
                        else:
                            o = pm[:, slot(k_)].rearrange("p (t n) -> p t n", t=CT)
                            z = Z[:, h]
                            ch = Chain(dve, steps, c, 9)
                            ch.k = 1 + 2 * h
                            ch.link(dve.reciprocal(rd[:], o[:, :, D]))
                            ch.link(dve.tensor_tensor(z, o[:, :, 0:D], rd[:].unsqueeze(2).broadcast_to([P, CT, D]), ALU.mult))
                            dve.sem_inc(reduced.sem, 1)
                            if h == 1:
                                ch.link(dve.tensor_tensor(z, z, Z[:, 0], ALU.add))
                                ch.link(dve.tensor_tensor(z, z, bias[:].unsqueeze(1).broadcast_to([P, CT, D]), ALU.add))
                                ch.link(dve.scalar_tensor_tensor(out=z, in0=z, scalar=SLOPE, in1=z, op0=ALU.mult, op1=ALU.max))
                                x = k.X[:, bass.ds(c * CT, CT), :]
                                ch.link(dve.tensor_tensor(x, x, z, ALU.add))

                    def chunk(c, ring, par):
                        for what, i in chunk_plan(ring):
                            if what == "convert":
                                convert(c + 1, i, 1 - par)
                            elif what == "ring":
                                use_ring(c, ring, i)
                            elif what == "values":
                                pass
                            elif what == "sums_out":
                                dve.wait_ge(out_done.sem, out_done.after(c, i + 1))
                                dve.tensor_copy(uB[:], poB[:]).then_inc(moved_b.sem, 1)
                            elif what == "scores" and i >= 1:
                                low(c, i - 1)
                            if what == "scores" and i == U - 1:
                                low(c, U - 1)

                    def low(c, u):
                        dve.wait_ge(highs.sem, highs.after(c, u + 1))
                        dve.wait_ge(probs.sem, probs.after(c, u + 1))
                        dve.tensor_tensor(Pl[:, u % PSL], Pr[:, u % PSL], Ph[:, u % PSL], ALU.subtract).then_inc(lows.sem, 1)

                    for q in range(QN):
                        convert(0, q, 0)
                        if q >= 1:
                            use_ring(0, ahead, q - 1, -AHEAD)
                    for i in range(QN - 1, len(ahead)):
                        use_ring(0, ahead, i, -AHEAD)
                    with dve.Fori(0, NC // 2 - 1) as m:
                        dve.get_value_cache().nocache = True
                        for par in range(2):
                            chunk(dve.snap(2 * m + par), ring_with_next(), par)
                    chunk(NC - 2, ring_with_next(), 0)
                    chunk(NC - 1, last_ring, 1)

                @block.scalar
                def _(act):
                    act.sem_inc(probs.sem, 2)
                    act.sem_inc(highs.sem, 2)
                    act.sem_inc(moved_a.sem, 1)
                    with act.Fori(0, NC) as c:
                        act.get_value_cache().nocache = True
                        for what, i in chunk_plan(last_ring):
                            if what == "scores":
                                act.wait_ge(trans.sem, trans.after(c, i + 1))
                                act.wait_ge(used.sem, used.after(c, i + 1 - PSL))
                                nc.scalar.activation(Pr[:, i % PSL], pt[:, i % 2], ACT.Exp).then_inc(probs.sem, 1)
                                nc.scalar.activation(Ph[:, i % PSL], pt[:, i % 2], ACT.Exp).then_inc(highs.sem, 1)
                            elif what == "sums_out":
                                act.wait_ge(out_done.sem, out_done.after(c, i + 1))
                                nc.scalar.activation(uA[:], poA[:], ACT.Copy).then_inc(moved_a.sem, 1)

                @block.tensor
                def _(pe):
                    pe.sem_inc(used.sem, PSL)
                    pe.sem_inc(out_done.sem, 1)
                    pe.wait_ge(made, 2)

                    def use_ring(c, ring, i, par, first=0):
                        what, h, q = ring[i]
                        k_ = i + first
                        to = c + 1 if first == 0 else c
                        pe.wait_ge(reduced.sem, reduced.after(c, k_ + 1 - 2))
                        if what == "max":
                            t, w = q // 4, q % 4
                            if h == 0:
                                pe.wait_ge(converted.sem, converted.after(to, q + 1))
                            for o in range(w * QW, (w + 1) * QW, CW):
                                dst = pm[:, slot(k_), o - w * QW:o - w * QW + CW]
                                nc.tensor.matmul(dst, k.negbig[:], NM[:, 1 - par if first == 0 else par, t, o:o + CW],
                                                 start=True, stop=False)
                                mm = nc.tensor.matmul(dst, qA[:, h:h + 1, bass.ds(to * CW + t * P, P)], kA[:, h, o:o + CW],
                                                      start=False, stop=True)
                        elif what == "row":
                            done = 4 * (h + 1) - (4 * H if (first or h == 1) else 0)
                            pe.wait_ge(mcol.sem, mcol.after(c, done))
                            for t in range(CT):
                                mm = nc.tensor.matmul(pm[0:2, slot(k_), t * P:(t + 1) * P], ms[:, h, t], ident16[:],
                                                      start=(t == 0), stop=True, skip_group_check=True)
                            for t in range(CT if h == 1 else 0):
                                mm = nc.tensor.matmul(pm[0:1, slot(k_), CW + t * P:CW + (t + 1) * P], k.lone[:, bass.ds(c * CT + t, 1)],
                                                      k.identb[:], start=(t == 0), stop=True, skip_group_check=True)
                        else:
                            side = c * CW // HALF
                            pe.wait_ge(moved_a.sem, moved_a.after(c, h + 1))
                            pe.wait_ge(moved_b.sem, moved_b.after(c, h + 1))
                            for t in range(CT):
                                dst = pm[:, slot(k_):slot(k_) + 1, t * 2 * P:t * 2 * P + D + 1]
                                nc.tensor.matmul(dst, uA[:, t * P:(t + 1) * P], We2[:, bass.ds(side, 1), h],
                                                 start=(t % 2 == 0), stop=False, skip_group_check=True)
                                mm = nc.tensor.matmul(dst, uB[:, t * P:(t + 1) * P], We[:, bass.ds(side, 1), h],
                                                      start=False, stop=True, skip_group_check=True)
                        mm.then_inc(scored.sem, 1)

                    def scores(c, u, par):
                        h, j = u // NT, u % NT
                        pe.wait_ge(probs.sem, probs.after(c, u + 1 - 2))
                        pe.wait_ge(highs.sem, highs.after(c, u + 1 - 2))
                        if u == 0:
                            pe.wait_ge(reduced.sem, reduced.after(c, 0))
                        if j == 0 and h == 1:
                            pe.wait_ge(reduced.sem, reduced.after(c, 1))
                        dst = pt[:, u % 2].unsqueeze(1)
                        nc.tensor.matmul(dst, kA[:, h, j * P:(j + 1) * P], qA[:, h:h + 1, bass.ds(c * CW, CW)],
                                         start=True, stop=False, skip_group_check=True)
                        nc.tensor.matmul(dst, kB[:, h, j * P:(j + 1) * P], qB[:, h:h + 1, bass.ds(c * CW, CW)],
                                         start=False, stop=False, skip_group_check=True)
                        for t in range(CT):
                            mm = nc.tensor.matmul(pt[:, u % 2, t * P:(t + 1) * P], NM[:, par, t, j * P:(j + 1) * P],
                                                  k.negbig[:], start=False, stop=(t == CT - 1), skip_group_check=True)
                        mm.then_inc(trans.sem, 1)

                    def values(c, u):
                        h, j = u // NT, u % NT
                        pe.wait_ge(lows.sem, lows.after(c, u + 1))
                        if j == 0:
                            pe.wait_ge(moved_a.sem, moved_a.after(c, h))
                            pe.wait_ge(moved_b.sem, moved_b.after(c, h))
                        nc.tensor.matmul(poA[:], V[:, j, h, 0:2 * DH], Ph[:, u % PSL], start=(j == 0), stop=(j == NT - 1),
                                         skip_group_check=True)
                        nc.tensor.matmul(poB[:], V[:, j, h, DH:2 * DH + 1], Pl[:, u % PSL], start=(j == 0), stop=False,
                                         skip_group_check=True)
                        nc.tensor.matmul(poB[DH:DH + 1], V[:, j, h, 2 * DH:2 * DH + 1], Ph[:, u % PSL], start=False,
                                         stop=False, skip_group_check=True).then_inc(used.sem, 1)

                    def chunk(c, ring, par):
                        for what, i in chunk_plan(ring):
                            if what == "scores":
                                scores(c, i, par)
                            elif what == "values":
                                values(c, i)
                            elif what == "ring":
                                use_ring(c, ring, i, par)
                            elif what == "lone":
                                if i == 0:
                                    pe.wait_ge(reduced.sem, reduced.after(c, 1))
                                nc.tensor.matmul(poB[:], sumV[:, i], lone[:], start=False, stop=True,
                                                 skip_group_check=True).then_inc(out_done.sem, 1)

                    for i in range(len(ahead)):
                        use_ring(0, ahead, i, 0, -AHEAD)
                    with pe.Fori(0, NC // 2 - 1) as m:
                        pe.get_value_cache().nocache = True
                        for par in range(2):
                            chunk(pe.snap(2 * m + par), ring_with_next(), par)
                    chunk(NC - 2, ring_with_next(), 0)
                    chunk(NC - 1, last_ring, 1)


def stage_self_attention(k, a, ctx_out):
    nc = k.nc
    H, E, DH = F_HEADS, F_EXP, F_DH
    MR = 3 * DH
    KR = MR + 1
    SCALE = float(DH) ** 0.5
    VW = DH + 1
    AW = DH + N_EXP
    G = H * E
    QW = 2 * CW
    NW = N // QW
    PSL = 4
    LAG = 2
    SX, MIX = ctx_out
    parts = nc.dram_tensor("sa_parts", (2, H * DH, N), F16).ap()
    seen = nc.dram_tensor("sa_seen", (H * DH, N), BF16).ap()
    with ExitStack() as outer:
        V = k.sb(outer, "sa_V", [P, NT, H, VW], F32)
        causA = k.sb(outer, "sa_causA", [P, P], BF16)
        causT = k.sb(outer, "sa_causT", [P, 2 * P], BF16)
        ident16 = k.sb(outer, "sa_ident16", [P, P], F16)
        two = k.sb(outer, "sa_two", [KR, G * (AW + 1) + P], F32)
        KS = k.sb(outer, "sa_KS", [KR, 2, N], F16)
        NP = k.sb(outer, "sa_NP", [KR, 2, N], BF16)
        OT = k.sb(outer, "sa_OT", [KR, CW], F32)
        W16 = k.sb(outer, "sa_W16", [MR, H, 1 + E, MR], F16)
        gb = k.sb(outer, "sa_gb", [P, H, E], F32)
        with ExitStack() as ctx:
            HL = k.sb(ctx, "sa_HL", [P, P], F32)
            hb = k.sb(ctx, "sa_hb", [P, 1], F32)
            Wv = k.sb(ctx, "sa_Wv", [P, P], F32)
            W = k.sb(ctx, "sa_W", [MR, H, 1 + E, MR], F32)
            YT = k.sb(ctx, "sa_YT", [P, N], F32)
            pp = k.ps(ctx, "sa_pp", [P, 2, CW])
            px = k.ps(ctx, "sa_px", [P, 2, CT, P])
            pv = k.ps(ctx, "sa_pv", [P, 2, CT, P])
            loaded, filled, late = k.sem("sap_loaded"), k.sem("sap_filled"), k.sem("sap_late")
            proj, biased, split = k.sem("sap_proj"), k.sem("sap_biased"), k.sem("sap_split")
            his, wsplit, stored, seen_at = k.sem("sap_his"), k.sem("sap_wsplit"), k.sem("sap_stored"), k.sem("sap_seen")
            turned, xmoved, vals, vmoved = k.sem("sap_turned"), k.sem("sap_xmoved"), k.sem("sap_vals"), k.sem("sap_vmoved")

            def load(sp):
                sp.dma_start(HL[:], a["hlT"]).then_inc(loaded, 16)
                sp.dma_start(hb[:], a["hlb"]).then_inc(loaded, 16)
                sp.dma_start(Wv[:], a["wvB"]).then_inc(loaded, 16)
                sp.dma_start(W[:], a["wqk"]).then_inc(late, 16)
                sp.dma_start(two[:], a["two"]).then_inc(late, 16)
                sp.dma_start(gb[:], a["gate_b"].rearrange("h e -> (h e)").rearrange("(o n) -> o n", o=1)
                             .broadcast_to([P, H * E]).rearrange("p (h e) -> p h e", h=H)).then_inc(late, 16)

            with ExitStack() as inner:
                Y = k.sb(inner, "sa_Y", [P, NT, D], F32)
                stage_layernorm(k, "ln3", Y[:], YT, load)
            sxT = k.sb(ctx, "sa_sxT", [P, N], F32)
            hiT = k.sb(ctx, "sa_hiT", [P, N], F16)
            loT = k.sb(ctx, "sa_loT", [P, N], F16)
            npT = k.sb(ctx, "sa_npT", [P, N], BF16)
            with nc.Block() as block:
                @block.sync
                def _(sp):
                    sp.wait_ge(late, 48)
                    sp.wait_ge(his, NC)
                    sp.dma_start(parts[0], hiT[:]).then_inc(stored, 16)
                    sp.wait_ge(split, NC)
                    sp.dma_start(parts[1], loT[:]).then_inc(stored, 16)
                    sp.wait_ge(seen_at, NC)
                    sp.dma_start(seen, npT[:]).then_inc(stored, 16)
                    sp.wait_ge(stored, 48)

                @block.gpsimd
                def _(pool):
                    for m in (causA, causT, ident16):
                        pool.memset(m[:], 0.0).then_inc(filled, 1)
                    pool.memset(V[:, :, :, DH:VW], 1.0).then_inc(filled, 1)
                    pool.wait_ge(filled, 4)
                    pool.affine_select(out=causA[:], in_=causA[:], compare_op=ALU.is_ge, fill=-BIG, base=0,
                                       pattern=[[-1, P]], channel_multiplier=1).then_inc(filled, 1)
                    pool.affine_select(out=causT[:], in_=causT[:], compare_op=ALU.is_ge, fill=-BIG, base=-P,
                                       pattern=[[1, 2 * P]], channel_multiplier=-1).then_inc(filled, 1)
                    pool.affine_select(out=ident16[:], in_=ident16[:], compare_op=ALU.not_equal, fill=1.0, base=0,
                                       pattern=[[-1, P]], channel_multiplier=1).then_inc(filled, 1)
                    for n, (tile, value) in enumerate(((KS[MR:KR], 1.0), (NP[:], 1.0), (OT[:], 0.0))):
                        pool.wait_ge(filled, 7 + n)
                        pool.memset(tile, value).then_inc(filled, 1)

                @block.tensor
                def _(pe):
                    pe.wait_ge(loaded, 48)
                    for c in range(NC):
                        if c >= 2:
                            pe.wait_ge(biased, c - 1)
                        nc.tensor.matmul(pp[:, c % 2], HL[:], YT[:, c * CW:(c + 1) * CW], start=True, stop=True).then_inc(proj, 1)
                    for c in range(NC):
                        pe.wait_ge(biased, c + 1)
                        for dst, w, done, freed in ((px, k.ident, turned, xmoved), (pv, Wv, vals, vmoved)):
                            if c >= 2:
                                pe.wait_ge(freed, c - 1)
                            for t in range(CT):
                                mm = nc.tensor.matmul(dst[:, c % 2, t], sxT[:, (c * CT + t) * P:(c * CT + t + 1) * P], w[:],
                                                      start=(t == 0), stop=True, skip_group_check=True)
                            mm.then_inc(done, 1)

                @block.scalar
                def _(act):
                    act.wait_ge(loaded, 48)
                    for c in range(NC):
                        act.wait_ge(proj, c + 1)
                        nc.scalar.activation(sxT[:, c * CW:(c + 1) * CW], pp[:, c % 2], ACT.Identity, bias=hb[:]).then_inc(biased, 1)
                    for c in range(NC):
                        act.wait_ge(biased, c + 1)
                        nc.scalar.activation(hiT[:, c * CW:(c + 1) * CW], sxT[:, c * CW:(c + 1) * CW], ACT.Copy).then_inc(his, 1)

                @block.vector
                def _(dve):
                    dve.wait_ge(late, 48)
                    dve.tensor_copy(W16[:], W[:]).then_inc(wsplit, 1)
                    dve.wait_ge(wsplit, 1)
                    lo = slice(DH, 2 * DH)
                    dve.tensor_tensor(W16[lo], W[lo], W16[lo], ALU.subtract).then_inc(wsplit, 1)
                    for c in range(NC):
                        dve.wait_ge(turned, c + 1)
                        dve.tensor_copy(SX[:, c * CT:(c + 1) * CT], px[:, c % 2]).then_inc(xmoved, 1)
                        dve.wait_ge(vals, c + 1)
                        dve.tensor_copy(V[:, c * CT:(c + 1) * CT, :, 0:DH],
                                        pv[:, c % 2].rearrange("p t (h d) -> p t h d", h=H)).then_inc(vmoved, 1)
                        cols = slice(c * CW, (c + 1) * CW)
                        dve.wait_ge(his, c + 1)
                        dve.tensor_tensor(loT[:, cols], sxT[:, cols], hiT[:, cols], ALU.subtract).then_inc(split, 1)
                        dve.tensor_scalar(npT[:, cols], sxT[:, cols], 0.0, None, ALU.not_equal).then_inc(seen_at, 1)

        with ExitStack() as ctx:
            XS = k.sb(ctx, "sa_XS", [MR, N], F16)
            QS = k.sb(ctx, "sa_QS", [KR, 2, N], F16)
            Vc = k.sb(ctx, "sa_Vc", [P, NT, VW], F32)
            ATT = k.sb(ctx, "sa_ATT", [P, E, NT, AW], F32)
            tmp = k.sb(ctx, "sa_tmp", [P, 2, NT, DH], F32)
            Pr = k.sb(ctx, "sa_probs", [P, PSL, CW], F32)
            mx = k.sb(ctx, "sa_mx", [P, 2, CT, NW], F32)
            mc = k.sb(ctx, "sa_mc", [P, 2, CT], F32)
            mh = k.sb(ctx, "sa_mh", [P, 2, CT], F16)
            rd = k.sb(ctx, "sa_rd", [P, CT], F32)
            lg = k.sb(ctx, "sa_lg", [P, NT, E], F32)
            sm = k.sb(ctx, "sa_sm", [P, NT], F32)
            pm = k.ps(ctx, "sa_pm", [P, 2, QW])
            pt = k.ps(ctx, "sa_pt", [P, 2, CW])
            po = k.ps(ctx, "sa_po", [P, CW])
            pz = k.ps(ctx, "sa_pz", [P, CT, P])

            TU = [CT * (c + 1) for c in range(NC)]
            T0 = [sum(TU[:c]) for c in range(NC + 1)]
            VALUES_AT = 0.3

            def pieces(c):
                return [("max", c, r) for r in range(CT * (c // 2 + 1))]

            def mixed_in(first, row_at, then):
                return then[:row_at] + [("row", first, 0)] + then[row_at:]

            def ring_plan():
                plan = mixed_in(2, 0, pieces(3))
                for c in range(4, NC):
                    plan += mixed_in(c - 1, 2, pieces(c))
                plan += [("row", NC - 1, 0)]
                head = len(plan)
                plan += [("project", s, w) for w in range(NW) for s in range(2)]
                plan += pieces(0)
                for c in (1, 2):
                    plan += mixed_in(c - 1, 2, pieces(c))
                return plan, head

            def rows_in(uses):
                return [i for i, use in enumerate(uses) if use[0] == "row"]

            ring, ahead_from = ring_plan()
            RING = len(ring)
            AHEAD = RING - ahead_from
            assert RING % 2 == 0 and len(rows_in(ring)) == NC
            rows = rows_in(ring)
            last_piece = {}
            for i, use in enumerate(ring):
                if use[0] == "max":
                    last_piece[use[1]] = i

            def row_count(i):
                return sum(1 for x in rows if x <= i)

            PROJ = 2 * NW
            x_in = Count(k.sem("sa_x_in"), 5 * 16)
            scored = Count(k.sem("sa_scored"), RING, AHEAD)
            reduced = Count(k.sem("sa_reduced"), RING, 2 + AHEAD)
            his = Count(k.sem("sa_hi"), PROJ, PROJ)
            mcol = Count(k.sem("sa_mcol"), 3 * NC, 3 * 3)
            zin = Count(k.sem("sa_zin"), NC, 1)
            zout = Count(k.sem("sa_zout"), NC, 1)
            trans = Count(k.sem("sa_trans"), T0[NC])
            probs = Count(k.sem("sa_probs_done"), T0[NC], 2)
            used = Count(k.sem("sa_used"), T0[NC], PSL)
            summed_out = Count(k.sem("sa_summed_out"), NC, 1)
            values_in = Count(k.sem("sa_values_in"), 1)
            mixed = Count(k.sem("sa_mixed"), 2 * E, 2 * E)
            gates = Count(k.sem("sa_gates"), 1)
            rds = k.sem("sa_rds")
            steps, psteps = k.sem("sa_steps"), k.sem("sa_psteps")
            e_in, e_out = k.sem("sa_exp_in"), k.sem("sa_exp_out")

            def turn_plan():
                plan = []
                for c in range(NC):
                    for j in range(TU[c]):
                        u = T0[c] + j
                        pair = u - u % 2
                        plan += [(pair + 0.01 * (u % 2), "scores", c, j), (pair + LAG + VALUES_AT + 0.01 * (u % 2), "values", c, j)]
                    end = T0[c + 1] - 2 + LAG + VALUES_AT
                    plan += [(end + 0.1, "sums_out", c), (end + 2.1, "by_token", c), (end + 2.9, "results", c)]
                    if c == NC - 1:
                        plan[-2:] = [(end + 0.2, "by_token", c), (end + 0.25, "results", c)]
                step = (T0[NC] + 1.0) / RING
                for i in range(RING):
                    at = i * step
                    if i >= RING - 2:
                        at = max(at, T0[NC] - 2 + LAG + VALUES_AT + 0.15)
                    if i == rows[-3]:
                        at += 1.2
                    if at % 2 < VALUES_AT + 0.15:
                        at += VALUES_AT + 0.15 - at % 2
                    plan.append((at, "ring", i))
                return [p[1:] for p in sorted(plan, key=lambda p: p[0])]

            plan = turn_plan()
            ahead_plan = [("ring", i) for i in range(ahead_from, RING)]

            def piece(c, r):
                per = c // 2 + 1
                t, w = r // per, r % per
                end = (c * CT + t + 1) * P
                return t, w, w * QW, min(end, (w + 1) * QW)

            def parity_of(i, par):
                return 1 - par if i >= ahead_from else par

            def first_query(c, j):
                return 0 if (c == 0 and j == 1) else max(0, j - c * CT) * P

            with nc.Block() as block:
                @block.sync
                def _(sp):
                    def load(head, par):
                        rows_ = bass.ds(head * DH, DH)
                        for i, part in enumerate((0, 0, 1)):
                            sp.dma_start(XS[i * DH:(i + 1) * DH], parts[part][rows_, :]).then_inc(x_in.sem, 16)
                        for i in range(2):
                            sp.dma_start(NP[i * 64:i * 64 + DH, par], seen[rows_, :]).then_inc(x_in.sem, 16)

                    load(0, 0)
                    with sp.Fori(0, G // 2) as m:
                        for par in range(2):
                            g = 2 * m + par
                            sp.wait_ge(scored.sem, scored.after(g, PROJ - AHEAD))
                            sp.wait_ge(zout.sem, zout.after(g, 0))
                            load(((g + 1) % G) // E, 1 - par)
                    sp.wait_ge(x_in.sem, (G + 1) * 5 * 16)

                @block.gpsimd
                def _(pool):
                    with pool.Fori(0, H) as n:
                        ch = Chain(pool, psteps, n, E - 2)
                        pool.wait_ge(gates.sem, gates.after(n, 1))
                        for e in range(E):
                            w = lg[:, :, e:e + 1].broadcast_to([P, NT, DH])
                            pool.tensor_tensor(tmp[:, min(e, 1)], ATT[:, e, :, 0:DH], w, ALU.mult).then_inc(mixed.sem, 1)
                            pool.wait_ge(mixed.sem, mixed.after(n, e + 1))
                            if 0 < e < E - 1:
                                ch.link(pool.tensor_tensor(tmp[:, 0], tmp[:, 0], tmp[:, 1], ALU.add))
                        out = MIX[:, :, bass.ds(n * DH, DH)]
                        pool.tensor_tensor(out, tmp[:, 0], tmp[:, 1], ALU.add).then_inc(mixed.sem, E)
                        pool.wait_ge(mixed.sem, mixed.after(n, 2 * E))

                @block.tensor
                def _(pe):
                    pe.sem_inc(used.sem, PSL)
                    pe.sem_inc(zin.sem, 1)

                    def project(g, i, par):
                        s, w = ring[i][1:]
                        lhs = W16[:, bass.ds(g // E, 1), 0] if s == 0 else W16[:, bass.ds(g // E, 1), bass.ds(1 + g % E, 1)]
                        for h in range(2):
                            o = w * QW + h * CW
                            mm = nc.tensor.matmul(pm[0:MR, i % 2, h * CW:(h + 1) * CW], lhs, XS[:, o:o + CW],
                                                  start=True, stop=True, skip_group_check=True)
                        mm.then_inc(scored.sem, 1)

                    def maxima(i, par):
                        c, r = ring[i][1:]
                        t, w, a0, a1 = piece(c, r)
                        q = QS[0:MR, par, (c * CT + t) * P:(c * CT + t + 1) * P]
                        last = a1 == (c * CT + t + 1) * P
                        for o in range(a0, a1, CW):
                            o1 = min(a1, o + CW)
                            diag = last and o1 == a1
                            mm = nc.tensor.matmul(pm[:, i % 2, o - a0:o1 - a0], q, KS[0:MR, par, o:o1], start=True, stop=not diag,
                                                  skip_group_check=True)
                            if diag:
                                mm = nc.tensor.matmul(pm[:, i % 2, a1 - P - a0:a1 - a0], k.identb[:], causA[:], start=False,
                                                      stop=True, skip_group_check=True)
                        mm.then_inc(scored.sem, 1)

                    def row(g, i):
                        n = row_count(i)
                        pe.wait_ge(mcol.sem, mcol.after(g, 3 * (n - 1)))
                        for t in range(CT):
                            mm = nc.tensor.matmul(pm[0:1, i % 2, t * P:(t + 1) * P], mh[:, n % 2, t:t + 1], ident16[:],
                                                  start=(t == 0), stop=True, skip_group_check=True)
                        mm.then_inc(scored.sem, 1)

                    def use_ring(g, g_next, i, par):
                        pe.wait_ge(reduced.sem, reduced.after(g, i + 1 - 2))
                        if ring[i][0] == "project":
                            if i == ahead_from:
                                pe.wait_ge(x_in.sem, x_in.after(g, 2 * 5 * 16))
                            project(g_next, i, 1 - par)
                        elif ring[i][0] == "max":
                            maxima(i, parity_of(i, par))
                        else:
                            row(g, i)

                    def values(g, c, j):
                        u = T0[c] + j
                        o = first_query(c, j)
                        pe.wait_ge(probs.sem, probs.after(g, u + 1))
                        if j < 2:
                            pe.wait_ge(summed_out.sem, summed_out.after(g, c))
                        b = 64 * (j % 2)
                        mm = nc.tensor.matmul(po[b:b + VW, o:CW], Vc[:, j], Pr[:, u % PSL, o:CW], start=(j < 2),
                                              stop=(j >= TU[c] - 2), skip_group_check=True)
                        mm.then_inc(used.sem, 1)

                    def scores(g, c, j, par):
                        u = T0[c] + j
                        o = first_query(c, j)
                        pe.wait_ge(probs.sem, probs.after(g, u + 1 - 2))
                        if j == 0:
                            done = [i for i in rows if ring[i][1] == c][0]
                            pe.wait_ge(reduced.sem, reduced.after(g, done + 1 - (RING if done >= ahead_from else 0)))
                        q = QS[0:KR, par, c * CW + o:(c + 1) * CW]
                        diag = j >= c * CT
                        mm = nc.tensor.matmul(pt[:, u % 2, o:CW], KS[0:KR, par, j * P:(j + 1) * P], q, start=True,
                                              stop=not diag, skip_group_check=True)
                        if diag:
                            d = (j - c * CT) * P
                            mm = nc.tensor.matmul(pt[:, u % 2, o:d + P], k.identb[:], causT[:, P - (d - o):2 * P],
                                                  start=False, stop=True, skip_group_check=True)
                        mm.then_inc(trans.sem, 1)

                    def by_token(g, c):
                        pe.wait_ge(summed_out.sem, summed_out.after(g, c + 1))
                        pe.wait_ge(zout.sem, zout.after(g, c))
                        for t in range(CT):
                            mm = nc.tensor.matmul(pz[:, t], OT[:, t * P:(t + 1) * P], two[:, bass.ds(g * (AW + 1), P)],
                                                  start=(t == 0), stop=True, skip_group_check=True)
                        mm.then_inc(zin.sem, 1)

                    for _, i in ahead_plan:
                        use_ring(-1, 0, i, 1)
                    with pe.Fori(0, H) as n:
                        pe.get_value_cache().nocache = True
                        with pe.Fori(0, E // 2) as m:
                            pe.get_value_cache().nocache = True
                            for par in range(2):
                                g = pe.snap(n * E + m * 2 + par)
                                g_next = pe.snap((n * E + m * 2 + par + 1) % G)
                                if par == 0:
                                    pe.wait_ge(values_in.sem, values_in.after(n, 1))
                                for what, *args in plan:
                                    if what == "scores":
                                        scores(g, *args, par)
                                    elif what == "values":
                                        values(g, *args)
                                    elif what == "ring":
                                        use_ring(g, g_next, *args, par)
                                    elif what == "by_token":
                                        by_token(g, *args)

                @block.scalar
                def _(act):
                    act.sem_inc(probs.sem, 2)

                    def high(g, i, par):
                        s, w = ring[i][1:]
                        act.wait_ge(scored.sem, scored.after(g, i + 1))
                        dst = (QS if s else KS)[0:MR, 1 - par, w * QW:(w + 1) * QW]
                        nc.scalar.activation(dst, pm[0:MR, i % 2], ACT.Copy, scale=SCALE if s else 1.0).then_inc(his.sem, 1)

                    for _, i in ahead_plan:
                        if ring[i][0] == "project":
                            high(-1, i, 1)
                    with act.Fori(0, H) as n:
                        act.get_value_cache().nocache = True
                        with act.Fori(0, E // 2) as m:
                            act.get_value_cache().nocache = True
                            for par in range(2):
                                g = act.snap(n * E + m * 2 + par)
                                for what, *args in plan:
                                    if what == "ring" and ring[args[0]][0] == "project":
                                        high(g, args[0], par)
                                    elif what == "scores":
                                        c, j = args
                                        u = T0[c] + j
                                        o = first_query(c, j)
                                        act.wait_ge(trans.sem, trans.after(g, u + 1))
                                        act.wait_ge(used.sem, used.after(g, u + 1 - PSL))
                                        nc.scalar.activation(Pr[:, u % PSL, o:CW], pt[:, u % 2, o:CW], ACT.Exp).then_inc(probs.sem, 1)
                        act.wait_ge(e_in, n + 1)
                        nc.scalar.activation(lg[:], lg[:], ACT.Exp).then_inc(e_out, 1)

                @block.vector
                def _(dve):
                    dve.sem_inc(reduced.sem, 2)
                    dve.sem_inc(zout.sem, 1)
                    dve.sem_inc(mixed.sem, 2 * E)
                    dve.memset(po[:], 0.0).then_inc(summed_out.sem, 1)

                    def low(g, i, par):
                        s, w = ring[i][1:]
                        cols = slice(w * QW, (w + 1) * QW)
                        dve.wait_ge(his.sem, his.after(g, i + 1 - ahead_from))
                        if s == 0:
                            lo = slice(DH, 2 * DH)
                            dve.tensor_tensor(KS[lo, 1 - par, cols], pm[lo, i % 2], KS[lo, 1 - par, cols],
                                              ALU.subtract).then_inc(reduced.sem, 1)
                        else:
                            lo = slice(2 * DH, MR)
                            dve.scalar_tensor_tensor(out=QS[lo, 1 - par, cols], in0=pm[lo, i % 2], scalar=SCALE,
                                                     in1=QS[lo, 1 - par, cols], op0=ALU.mult, op1=ALU.subtract).then_inc(reduced.sem, 1)

                    def use_ring(g, i, par):
                        what, c, r = ring[i]
                        if what == "project":
                            low(g, i, par)
                            return
                        dve.wait_ge(scored.sem, scored.after(g, i + 1))
                        if what == "row":
                            dve.tensor_scalar(QS[MR:KR, parity_of(i, par), c * CW:(c + 1) * CW], pm[0:1, i % 2, 0:CW], -1.0, None,
                                              ALU.mult).then_inc(reduced.sem, 1)
                            return
                        t, w, a0, a1 = piece(c, r)
                        dve.tensor_reduce(mx[:, c % 2, t, w:w + 1], pm[:, i % 2, 0:a1 - a0], AX.X, ALU.max).then_inc(reduced.sem, 1)
                        if i == last_piece[c]:
                            at = [x for x in rows if ring[x][1] == c][0]
                            over = 0
                            if at < i:
                                over = 1
                            nth = row_count(at) + over * NC
                            m = mc[:, nth % 2]
                            dve.wait_ge(reduced.sem, reduced.after(g, i + 1))
                            dve.tensor_reduce(m, mx[:, c % 2, :, 0:c // 2 + 1], AX.X, ALU.max).then_inc(mcol.sem, 1)
                            dve.wait_ge(mcol.sem, mcol.after(g, 3 * (nth - 1) - 2))
                            dve.tensor_scalar(m, m, -M16_MAX, M16_MAX, ALU.max, ALU.min).then_inc(mcol.sem, 1)
                            dve.wait_ge(mcol.sem, mcol.after(g, 3 * (nth - 1) - 1))
                            dve.tensor_copy(mh[:, nth % 2], m).then_inc(mcol.sem, 1)

                    def sums_out(g, c, par):
                        dve.wait_ge(used.sem, used.after(g, T0[c + 1]))
                        dve.wait_ge(zin.sem, zin.after(g, c))
                        dve.tensor_tensor(OT[:], po[0:KR], NP[:, par, c * CW:(c + 1) * CW], ALU.mult).then_inc(summed_out.sem, 1)

                    def results(g, e, c):
                        dve.wait_ge(zin.sem, zin.after(g, c + 1))
                        dve.reciprocal(rd[:], pz[:, :, AW]).then_inc(rds, 1)
                        if c == 0:
                            dve.wait_ge(mixed.sem, e_free(e))
                        dve.wait_ge(rds, g * NC + (c + 1))
                        dve.tensor_tensor(ATT[:, bass.ds(e, 1), c * CT:(c + 1) * CT, :], pz[:, :, 0:AW].unsqueeze(1),
                                          rd[:].unsqueeze(2).broadcast_to([P, CT, AW]).unsqueeze(1), ALU.mult).then_inc(zout.sem, 1)

                    dve.tensor_copy(Vc[:], V[:, :, 0]).then_inc(values_in.sem, 1)
                    for _, i in ahead_plan:
                        use_ring(-1, i, 1)
                    with dve.Fori(0, H) as n:
                        dve.get_value_cache().nocache = True
                        def e_free(e):
                            return n * (2 * E) + e + 1
                        with dve.Fori(0, E // 2) as m:
                            dve.get_value_cache().nocache = True
                            for par in range(2):
                                e = dve.snap(2 * m + par)
                                g = dve.snap(n * E + m * 2 + par)
                                dve.wait_ge(x_in.sem, x_in.after(g, 5 * 16))
                                for what, *args in plan:
                                    if what == "ring":
                                        use_ring(g, *args, par)
                                    elif what == "sums_out":
                                        sums_out(g, *args, par)
                                    elif what == "results":
                                        results(g, e, *args)

                        dve.wait_ge(used.sem, used.after(n * E + E, 0))
                        dve.tensor_scalar(Vc[:].unsqueeze(2), V[:, :, bass.ds((n + 1) % H, 1), :], 1.0, None,
                                          ALU.mult).then_inc(values_in.sem, 1)
                        ch = Chain(dve, steps, n, 6)
                        dve.wait_ge(zout.sem, zout.after(n * E + (E - 1), NC))
                        ch.link(dve.tensor_reduce(lg[:], ATT[:, :, :, DH:AW].rearrange("p e t x -> p t x e"), AX.X, ALU.add))
                        ch.link(dve.tensor_tensor(lg[:], lg[:], gb[:, bass.ds(n, 1), :].broadcast_to([P, NT, E]), ALU.add))
                        emit_softmax4(dve, ch, lg[:], sm[:], e_in, e_out, n)
                        assert ch.k == 6, ch.k
                        dve.sem_inc(gates.sem, 1)


def stage_feed_forward(k, a, SX, MIX):
    nc = k.nc
    GR = NT * F_HEADS
    QP = 4
    QT, QG = NT // QP, GR // QP
    EPS = 1e-8
    with ExitStack() as ctx:
        FN = k.sb(ctx, "ff_FN", [P, NT, D], F32)
        B = k.sb(ctx, "ff_B", [P, NT, D], F32)
        FT = k.sb(ctx, "ff_FT", [P, N], F32)
        H1 = k.sb(ctx, "ff_H1", [P, N], F32)
        st = k.sb(ctx, "ff_st", [P, 5, GR], F32)
        ln = k.sb(ctx, "ff_ln", [P, 4, F_DH], F32)
        W1 = k.sb(ctx, "ff_W1", [P, P], F32)
        W2 = k.sb(ctx, "ff_W2", [P, P], F32)
        b1 = k.sb(ctx, "ff_b1", [P, 1], F32)
        b2 = k.sb(ctx, "ff_b2", [P, F_DH], F32)
        fg = k.sb(ctx, "ff_fg", [P, F_HEADS], F32)
        lg = k.sb(ctx, "ff_lg", [P, NT, F_HEADS], F32)
        sm = k.sb(ctx, "ff_sm", [P, NT], F32)
        pt = k.ps(ctx, "ff_pt", [P, 2, CW])
        ph = k.ps(ctx, "ff_ph", [P, 2, CW])
        pz = k.ps(ctx, "ff_pz", [P, 2, CT, P])
        pg = k.ps(ctx, "ff_pg", [P, NT, F_HEADS])
        loaded, steps, std_in, std_out = k.sem("ff_loaded"), k.sem("ff_steps"), k.sem("ff_std_in"), k.sem("ff_std_out")
        centred, squared, scaled, gained = k.sem("ff_centred"), k.sem("ff_squared"), k.sem("ff_scaled"), k.sem("ff_gained")
        normed, turned, tmoved = k.sem("ff_normed"), k.sem("ff_turned"), k.sem("ff_tmoved")
        hid, relued, masked, outp, omoved = (k.sem("ff_hid"), k.sem("ff_relued"), k.sem("ff_masked"), k.sem("ff_out"),
                                             k.sem("ff_omoved"))
        logits, e_in, e_out, added = k.sem("ff_logits"), k.sem("ff_exp_in"), k.sem("ff_exp_out"), k.sem("ff_added")

        def part(x, q):
            return x[:, q * QT:(q + 1) * QT].rearrange("p t (h d) -> p (t h) d", h=F_HEADS)

        def wide(x, q):
            return x[:, q * QG:(q + 1) * QG].unsqueeze(2).broadcast_to([P, QG, F_DH])

        mean, var, std, rstd, tmp = (st[:, i] for i in range(5))

        with nc.Block() as block:
            @block.sync
            def _(sp):
                for i, name in enumerate(("ln_g", "ln_b", "fnorm_g", "fnorm_b")):
                    sp.dma_start(ln[:, i], a[name].rearrange("(o n) -> o n", o=1).broadcast_to([P, F_DH])).then_inc(loaded, 16)
                sp.dma_start(b2[:], a["fc2_b"].rearrange("(o n) -> o n", o=1).broadcast_to([P, F_DH])).then_inc(loaded, 16)
                sp.dma_start(W1[:], a["fc1B"]).then_inc(loaded, 16)
                sp.dma_start(W2[:], a["fc2B"]).then_inc(loaded, 16)
                sp.dma_start(b1[:], a["fc1b"]).then_inc(loaded, 16)
                sp.dma_start(fg[:], a["fgate_wT"]).then_inc(loaded, 16)

            @block.gpsimd
            def _(pool):
                pool.wait_ge(loaded, 16 * 9)
                for n, X_ in enumerate((FN, FN)):
                    for q in range(QP):
                        pool.wait_ge(scaled, n * QP + q + 1)
                        pool.tensor_tensor(part(X_, q), part(X_, q), ln[:, 2 * n:2 * n + 1].broadcast_to([P, QG, F_DH]),
                                           ALU.mult).then_inc(gained, 1)

            @block.tensor
            def _(pe):
                pe.wait_ge(loaded, 16 * 9)

                def turn(n, c):
                    u = n * NC + c
                    pe.wait_ge(normed, n * QP + c * CT // QT + 1)
                    if u >= 2:
                        pe.wait_ge(tmoved, u - 1)
                    for t in range(CT):
                        mm = nc.tensor.matmul(pt[:, u % 2, t * P:(t + 1) * P], FN[:, c * CT + t], k.ident[:], start=(t == 0),
                                              stop=True, skip_group_check=True)
                    mm.then_inc(turned, 1)

                for c in range(NC + 2):
                    if c < NC:
                        turn(0, c)
                    if 1 <= c <= NC:
                        i = c - 1
                        pe.wait_ge(tmoved, i + 1)
                        if i >= 2:
                            pe.wait_ge(relued, i - 1)
                        nc.tensor.matmul(ph[:, i % 2], W1[:], FT[:, i * CW:(i + 1) * CW], start=True, stop=True).then_inc(hid, 1)
                    if c >= 2:
                        i = c - 2
                        pe.wait_ge(masked, i + 1)
                        if i >= 2:
                            pe.wait_ge(omoved, i - 1)
                        for t in range(CT):
                            j = i * CT + t
                            mm = nc.tensor.matmul(pz[:, i % 2, t], H1[:, j * P:(j + 1) * P], W2[:], start=(t == 0), stop=True,
                                                  skip_group_check=True)
                        mm.then_inc(outp, 1)
                for c in range(NC + 1):
                    if c < NC:
                        turn(1, c)
                    if c >= 1:
                        pe.wait_ge(tmoved, NC + c)
                        for t in range((c - 1) * CT, c * CT):
                            mm = nc.tensor.matmul(pg[:, t], FT[:, t * P:(t + 1) * P], fg[:], start=(t == 0), stop=True,
                                                  skip_group_check=True)
                mm.then_inc(logits, 1)

            @block.scalar
            def _(act):
                def norm(n):
                    for q in range(QP):
                        act.wait_ge(centred, n * QP + q + 1)
                        nc.scalar.activation(part((B, MIX)[n], q), part(FN, q), ACT.Square).then_inc(squared, 1)
                    act.wait_ge(std_in, n + 1)
                    nc.scalar.activation(std, var, ACT.Sqrt).then_inc(std_out, 1)

                norm(0)
                act.wait_ge(loaded, 16 * 9)
                for c in range(NC + 1):
                    if c < NC:
                        act.wait_ge(turned, c + 1)
                        nc.scalar.activation(FT[:, c * CW:(c + 1) * CW], pt[:, c % 2], ACT.Copy).then_inc(tmoved, 1)
                    if c >= 1:
                        i = c - 1
                        act.wait_ge(hid, i + 1)
                        nc.scalar.activation(H1[:, i * CW:(i + 1) * CW], ph[:, i % 2], ACT.Relu, bias=b1[:]).then_inc(relued, 1)
                norm(1)
                for c in range(NC):
                    act.wait_ge(turned, NC + c + 1)
                    nc.scalar.activation(FT[:, c * CW:(c + 1) * CW], pt[:, c % 2], ACT.Copy).then_inc(tmoved, 1)
                act.wait_ge(e_in, 1)
                nc.scalar.activation(lg[:], lg[:], ACT.Exp).then_inc(e_out, 1)

            @block.vector
            def _(dve):
                ch = Chain(dve, steps)

                def norm(n, src):
                    for q in range(QP):
                        sums = mean[:, q * QG:(q + 1) * QG]
                        ch.link(dve.tensor_reduce(sums, part(src, q), AX.X, ALU.add))
                        ch.link(dve.tensor_scalar(sums, sums, 1.0 / F_DH, None, ALU.mult))
                        dve.tensor_tensor(part(FN, q), part(src, q), wide(mean, q), ALU.subtract).then_inc(centred, 1)
                    for q in range(QP):
                        dve.wait_ge(squared, n * QP + q + 1)
                        ch.link(dve.tensor_reduce(var[:, q * QG:(q + 1) * QG], part((B, MIX)[n], q), AX.X, ALU.add))
                    dve.tensor_scalar(var, var, 1.0 / F_DH, EPS, ALU.mult, ALU.add).then_inc(std_in, 1)
                    dve.wait_ge(std_out, n + 1)
                    ch.link(dve.reciprocal(rstd, std))
                    ch.link(dve.tensor_tensor(tmp, rstd, rstd, ALU.mult))
                    ch.link(dve.tensor_tensor(tmp, tmp, var, ALU.mult))
                    ch.link(dve.tensor_scalar(tmp, tmp, -0.5, 1.5, ALU.mult, ALU.add))
                    ch.link(dve.tensor_tensor(rstd, rstd, tmp, ALU.mult))
                    for q in range(QP + 1):
                        if q < QP:
                            dve.tensor_tensor(part(FN, q), part(FN, q), wide(rstd, q), ALU.mult).then_inc(scaled, 1)
                        if q >= 1:
                            dve.wait_ge(gained, n * QP + q)
                            dve.tensor_tensor(part(FN, q - 1), part(FN, q - 1), ln[:, 2 * n + 1:2 * n + 2].broadcast_to([P, QG, F_DH]),
                                              ALU.add).then_inc(normed, 1)

                dve.wait_ge(loaded, 16 * 9)
                ch.link(dve.tensor_tensor(MIX[:], MIX[:], SX[:], ALU.add))
                norm(0, MIX)
                for c in range(NC + 1):
                    if c < NC:
                        cols = slice(c * CW, (c + 1) * CW)
                        dve.wait_ge(relued, c + 1)
                        dve.scalar_tensor_tensor(out=H1[:, cols], in0=FT[:, cols], scalar=0.0, in1=H1[:, cols],
                                                 op0=ALU.not_equal, op1=ALU.mult).then_inc(masked, 1)
                    if c >= 1:
                        i = c - 1
                        dve.wait_ge(outp, i + 1)
                        v = lambda x: x.rearrange("p t (h d) -> p t h d", h=F_HEADS)
                        dve.tensor_tensor(v(B[:, i * CT:(i + 1) * CT]), v(pz[:, i % 2]),
                                          b2[:].unsqueeze(1).unsqueeze(1).broadcast_to([P, CT, F_HEADS, F_DH]),
                                          ALU.add).then_inc(omoved, 1)
                dve.wait_ge(omoved, NC)
                ch.link(dve.scalar_tensor_tensor(out=B[:], in0=FN[:], scalar=0.0, in1=B[:], op0=ALU.not_equal, op1=ALU.mult))
                ch.link(dve.tensor_tensor(B[:], B[:], FN[:], ALU.add))
                norm(1, B)
                dve.wait_ge(logits, 1)
                ch.link(dve.tensor_copy(lg[:], pg[:]))
                emit_softmax4(dve, ch, lg[:], sm[:], e_in, e_out)
                gate = lg[:].rearrange("p t h -> p (t h)")
                for q in range(QP):
                    ch.link(dve.tensor_tensor(part(FN, q), part(FN, q), wide(gate, q), ALU.mult))
                    x = k.X[:, q * QT:(q + 1) * QT]
                    dve.tensor_tensor(x, x, FN[:, q * QT:(q + 1) * QT], ALU.add).then_inc(added, 1)


def lay_out(inputs):
    import numpy as np
    get = {n: np.ascontiguousarray(np.asarray(v)) for n, v in inputs.items()}
    r = {"x": get["x"], "adj": get["adj"]}
    for n in ("inlayer2", "W", "b", "w1", "b1", "w2", "b2"):
        r[n] = get["L0_gnn_" + n]
    for n in ("sW1", "sb1", "sW2", "sb2", "sW3", "sb3", "eW1", "eW2", "eW3", "eb3", "gW", "gb"):
        r[n] = get["L0_ffn_" + n]
    for n in ("eb1", "eb2"):
        r[n + "T"] = np.ascontiguousarray(get["L0_ffn_" + n].T)
    for n in ("Wq", "Wk", "Wv", "weightr", "weightd", "bias"):
        r[n] = get["L1_gnn_" + n]
    f = {n[7:]: v for n, v in get.items() if n.startswith("L1_ffn_")}
    r["hlT"] = np.ascontiguousarray(f["hl_w"].reshape(D, D).T)
    r["hlb"] = f["hl_b"].reshape(D, 1)
    wqk = np.zeros((3 * F_DH, F_HEADS, 1 + F_EXP, 3 * F_DH), np.float32)
    for name in ("wvB", "fc1B", "fc2B"):
        r[name] = np.zeros((D, D), np.float32)
    for h in range(F_HEADS):
        rows = slice(h * F_DH, (h + 1) * F_DH)
        wqk[:, h, 0] = np.tile(f["wk"][h].T, (3, 3))
        for e in range(F_EXP):
            wqk[:, h, 1 + e] = np.tile(f["wq"][h, e].T, (3, 3))
        r["wvB"][rows, rows] = f["wv"][h].T
        r["fc1B"][rows, rows] = f["fc1_w"].T
        r["fc2B"][rows, rows] = f["fc2_w"].T
    r["wqk"] = wqk
    width = F_DH + N_EXP + 1
    two = np.zeros((3 * F_DH + 1, F_HEADS * F_EXP * width + P), np.float32)
    for turn in range(F_HEADS * F_EXP):
        h, e = divmod(turn, F_EXP)
        for i in (0, 64):
            block = two[i:i + F_DH + 1, turn * width:(turn + 1) * width]
            block[:F_DH, :F_DH] = np.eye(F_DH, dtype=np.float32)
            block[:F_DH, F_DH:F_DH + N_EXP] = f["gate_w"][h][:, e * F_DH:(e + 1) * F_DH].T
            block[F_DH, F_DH + N_EXP] = 1.0
    r["two"] = two
    r["fc1b"] = np.tile(f["fc1_b"], F_HEADS).reshape(D, 1)
    for n in ("gate_b", "ln_g", "ln_b", "fnorm_g", "fnorm_b", "fc2_b"):
        r[n] = f[n]
    r["fgate_wT"] = np.ascontiguousarray(f["fgate_w"].T)
    return r


def kernel(**inputs):
    import concourse.bacc as _bacc
    from concourse import mybir as _mybir
    from concourse.bass_utils import run_bass_kernel_spmd as _run

    nc = _bacc.Bacc("TRN2", target_bir_lowering=False, num_devices=1)
    arrays, args = {}, {}
    for name, arr in lay_out(inputs).items():
        arrays[f"in_{name}"] = arr
        args[name] = nc.dram_tensor(f"in_{name}", arr.shape, _mybir.dt.from_np(arr.dtype), kind="ExternalInput").ap()
    out = nc.dram_tensor("out_x", (N, D), F32, kind="ExternalOutput").ap()
    build(nc, args, out)
    res = _run(nc, [arrays], core_ids=[0])
    return res.results[0]["out_x"]
```
